# Optimizing a Trainium2 kernel written in Bass

```python
import numpy as np
import jax
import jax.numpy as jnp

def _softmax(x, axis=-1):
    return jax.nn.softmax(x, axis=axis)

def _gelu(x):
    return jax.nn.gelu(x, approximate=True)

def _silu(x):
    return jax.nn.silu(x)

def _sigmoid(x):
    return jax.nn.sigmoid(x)

def _layernorm(x, axis=-1, eps=1e-05):
    m = jnp.mean(x, axis=axis, keepdims=True)
    v = jnp.var(x, axis=axis, keepdims=True)
    return (x - m) / jnp.sqrt(v + eps)

def _scatter_add(tgt, idx, src, axis=0):
    return tgt.at[idx].add(src)

def _segment_sum(src, seg, n):
    return jax.ops.segment_sum(src, seg, n)
kernel_name = 'mk_decoder_postln_d1_seqx_r8_699337'

def setup_inputs(seed: int=0):
    np.random.seed(seed)
    _w = jnp.asarray

    def _rec_inputs():
        import jax
        import jax.numpy as jnp
        _rk = jax.random.key(seed)
        x = -0.000125 + 0.9999 * jax.random.normal(jax.random.fold_in(_rk, 1), (16, 128, 128), jnp.float32)
        _lenS = 128 - jax.random.randint(jax.random.fold_in(_rk, 7), (16,), 0, max(1, 128 // 4) + 1, jnp.int32)
        _lenS2 = 77 - jax.random.randint(jax.random.fold_in(_rk, 8), (16,), 0, max(1, 77 // 4) + 1, jnp.int32)
        _ctx_2048P = jax.random.normal(jax.random.fold_in(_rk, 11), (16, 16, 256), jnp.float32)
        _ctx_2048c = jax.random.dirichlet(jax.random.fold_in(_rk, 511), 0.3 * jnp.ones((16,), jnp.float32), (16, 77))
        _ctx_2048t = jnp.einsum('bsk,bkd->bsd', _ctx_2048c, _ctx_2048P)
        _ctx_2048t = _ctx_2048t * jax.lax.rsqrt(jnp.mean(jnp.square(_ctx_2048t)) + 1e-12) * 0.953939
        ctx_2048 = -1.39393e-06 + 0.999914 * (_ctx_2048t + 0.3 * jax.random.normal(jax.random.fold_in(_rk, 611), (16, 77, 256), jnp.float32))
        return (x, ctx_2048)
    x, ctx_2048 = _rec_inputs()

    def _L0_attn_setup():
        import jax, jax.numpy as jnp
        import numpy as np
        LN_EPS = 1e-05
        DENOM_EPS = 1e-06
        NUM_HEADS = 16

        def _layer_norm(x, gamma, beta):
            mu = jnp.mean(x, axis=-1, keepdims=True)
            var = jnp.mean(jnp.square(x - mu), axis=-1, keepdims=True)
            return (x - mu) * jax.lax.rsqrt(var + LN_EPS) * gamma + beta
        key = jax.random.key(seed)
        k1, k2, k3 = jax.random.split(key, 3)
        B, L, D = (4, 512, 128)
        x = jax.random.normal(k1, (B, L, D), dtype=jnp.float32)
        gamma = jnp.ones((D,), dtype=jnp.float32)
        beta = jnp.zeros((D,), dtype=jnp.float32)
        Wqkv = jax.random.normal(k2, (D, 3 * D), dtype=jnp.float32) / np.sqrt(D)
        Wout = jax.random.normal(k3, (D, D), dtype=jnp.float32) / np.sqrt(D)
        return {'x': x, 'gamma': gamma, 'beta': beta, 'Wqkv': Wqkv, 'Wout': Wout}
    _L0_attn_all = _L0_attn_setup()
    _L0_attn_in = {k: v for k, v in _L0_attn_all.items() if k in ('gamma', 'beta', 'Wqkv', 'Wout')}
    del _L0_attn_all

    def _L0_xattn_setup():
        import jax, jax.numpy as jnp
        import numpy as np
        B, N, DIM = (8, 512, 128)
        M, CTX = (32, 256)
        HEADS, DH = (16, 64)
        INNER = HEADS * DH
        EPS = 1e-06

        def _split_heads(t):
            b, n, _ = t.shape
            return t.reshape(b, n, HEADS, DH).transpose(0, 2, 1, 3)
        key = jax.random.key(seed)
        ks = jax.random.split(key, 6)
        x = jax.random.normal(ks[0], (B, N, DIM), dtype=jnp.float32)
        context = jax.random.normal(ks[1], (B, M, CTX), dtype=jnp.float32)
        Wq = jax.random.normal(ks[2], (DIM, INNER), dtype=jnp.float32) / np.sqrt(DIM)
        Wkv = jax.random.normal(ks[3], (CTX, 2 * INNER), dtype=jnp.float32) / np.sqrt(CTX)
        null_kv = jax.random.normal(ks[4], (2, DH), dtype=jnp.float32) / np.sqrt(2.0)
        Wout = jax.random.normal(ks[5], (INNER, DIM), dtype=jnp.float32) / np.sqrt(INNER)
        ln_scale = jnp.ones((DIM,), dtype=jnp.float32)
        ln_bias = jnp.zeros((DIM,), dtype=jnp.float32)
        return {'x': x, 'context': context, 'Wq': Wq, 'Wkv': Wkv, 'null_kv': null_kv, 'Wout': Wout, 'ln_scale': ln_scale, 'ln_bias': ln_bias}
    _L0_xattn_all = _L0_xattn_setup()
    _L0_xattn_in = {k: v for k, v in _L0_xattn_all.items() if k in ('Wq', 'Wkv', 'null_kv', 'Wout', 'ln_scale', 'ln_bias')}
    del _L0_xattn_all

    def _L0_ffn_setup():
        import jax, jax.numpy as jnp
        import numpy as np
        DIM = 128
        DEPTH = 6
        HEADS = 16
        DIM_HEAD = 64
        WINDOW = 32
        INNER = HEADS * DIM_HEAD
        DIM_INNER = int(DIM * 4 * 2 / 3)
        QK_SCALE = 8.0

        def shift_tokens(t):
            a, s = jnp.split(t, 2, -1)
            s = jnp.pad(s, ((0, 0), (1, 0), (0, 0)))[:, :-1]
            return jnp.concatenate([a, s], -1)

        def l2norm(t):
            return t / jnp.maximum(jnp.linalg.norm(t, axis=-1, keepdims=True), 1e-12)

        def rotate_half(x):
            x1, x2 = jnp.split(x, 2, -1)
            return jnp.concatenate([-x2, x1], -1)

        def rotary_tables(n):
            half = jnp.arange(0, DIM_HEAD, 2, dtype=jnp.float32)
            inv_freq = 1.0 / 10000.0 ** (half / DIM_HEAD)
            t = jnp.arange(n, dtype=jnp.float32)
            freqs = t[:, None] * inv_freq[None, :]
            freqs = jnp.concatenate([freqs, freqs], -1)
            base_scale = (half + 0.4 * DIM_HEAD) / (1.4 * DIM_HEAD)
            power = (t - n // 2) / (WINDOW // 2)
            scale = base_scale[None, :] ** power[:, None]
            scale = jnp.concatenate([scale, scale], -1)
            return (freqs, scale)

        def local_attention(q, k, v):
            b, h, n, d = q.shape
            w = WINDOW
            nw = n // w
            bq = q.reshape(b, h, nw, w, d)
            bk = k.reshape(b, h, nw, w, d)
            bv = v.reshape(b, h, nw, w, d)

            def look(t):
                p = jnp.pad(t, ((0, 0), (0, 0), (1, 0), (0, 0), (0, 0)))
                return jnp.concatenate([p[:, :, :nw], p[:, :, 1:]], axis=3)
            bk2, bv2 = (look(bk), look(bv))
            seq = jnp.arange(n).reshape(nw, w)
            seq_p = jnp.pad(seq, ((1, 0), (0, 0)), constant_values=-1)
            jt = jnp.concatenate([seq_p[:nw], seq_p[1:]], axis=1)
            it = seq[:, :, None]
            jb = jt[:, None, :]
            mask = (it < jb) | (it > jb + w) | (jb == -1)
            sim = jnp.einsum('bhwie,bhwje->bhwij', bq, bk2) * QK_SCALE
            sim = jnp.where(mask, -jnp.finfo(sim.dtype).max, sim)
            attn = jax.nn.softmax(sim, -1)
            out = jnp.einsum('bhwij,bhwje->bhwie', attn, bv2)
            return out.reshape(b, h, n, d)

        def attn_layer(x, Wqkv, qs, ksc, Wo):
            b, n, _ = x.shape
            qkv = x @ Wqkv
            q, k, v = jnp.split(qkv, 3, -1)
            sh = lambda t: t.reshape(b, n, HEADS, DIM_HEAD).transpose(0, 2, 1, 3)
            q, k, v = (sh(q), sh(k), sh(v))
            q = l2norm(q) * qs
            k = l2norm(k) * ksc
            freqs, scale = rotary_tables(n)
            cos, sin = (jnp.cos(freqs), jnp.sin(freqs))
            q = q * cos * scale + rotate_half(q) * sin * scale
            inv = 1.0 / scale
            k = k * cos * inv + rotate_half(k) * sin * inv
            out = local_attention(q, k, v)
            out = out.transpose(0, 2, 1, 3).reshape(b, n, INNER)
            return out @ Wo

        def ffn_layer(x, g, bln, W1, b1, W2, b2):
            mu = x.mean(-1, keepdims=True)
            var = ((x - mu) ** 2).mean(-1, keepdims=True)
            xn = (x - mu) / jnp.sqrt(var + 1e-05) * g + bln
            hg = xn @ W1 + b1
            a, gate = jnp.split(hg, 2, -1)
            return a * jax.nn.gelu(gate, approximate=False) @ W2 + b2
        key = jax.random.key(seed)
        ks = jax.random.split(key, 8)
        B, N = (2, 256)
        init = lambda k, shape: jax.random.normal(k, shape, jnp.float32) * 0.02
        return {'x': jax.random.normal(ks[0], (B, N, DIM), jnp.float32), 'Wqkv': init(ks[1], (DEPTH, DIM, 3 * INNER)), 'q_scale': jnp.ones((DEPTH, DIM_HEAD), jnp.float32), 'k_scale': jnp.ones((DEPTH, DIM_HEAD), jnp.float32), 'Wo': init(ks[2], (DEPTH, INNER, DIM)), 'ln_g': jnp.ones((DEPTH, DIM), jnp.float32), 'ln_b': jnp.zeros((DEPTH, DIM), jnp.float32), 'W1': init(ks[3], (DEPTH, DIM, 2 * DIM_INNER)), 'b1': jnp.zeros((DEPTH, 2 * DIM_INNER), jnp.float32), 'W2': init(ks[4], (DEPTH, DIM_INNER, DIM)), 'b2': jnp.zeros((DEPTH, DIM), jnp.float32)}
    _L0_ffn_all = _L0_ffn_setup()
    _L0_ffn_in = {k: v for k, v in _L0_ffn_all.items() if k in ('Wqkv', 'q_scale', 'k_scale', 'Wo', 'ln_g', 'ln_b', 'W1', 'b1', 'W2', 'b2')}
    del _L0_ffn_all
    return {'x': x, 'ctx_2048': ctx_2048, 'L0_attn_gamma': _L0_attn_in['gamma'], 'L0_attn_beta': _L0_attn_in['beta'], 'L0_attn_Wqkv': _L0_attn_in['Wqkv'], 'L0_attn_Wout': _L0_attn_in['Wout'], 'L0_xattn_Wq': _L0_xattn_in['Wq'], 'L0_xattn_Wkv': _L0_xattn_in['Wkv'], 'L0_xattn_null_kv': _L0_xattn_in['null_kv'], 'L0_xattn_Wout': _L0_xattn_in['Wout'], 'L0_xattn_ln_scale': _L0_xattn_in['ln_scale'], 'L0_xattn_ln_bias': _L0_xattn_in['ln_bias'], 'L0_ffn_Wqkv': _L0_ffn_in['Wqkv'], 'L0_ffn_q_scale': _L0_ffn_in['q_scale'], 'L0_ffn_k_scale': _L0_ffn_in['k_scale'], 'L0_ffn_Wo': _L0_ffn_in['Wo'], 'L0_ffn_ln_g': _L0_ffn_in['ln_g'], 'L0_ffn_ln_b': _L0_ffn_in['ln_b'], 'L0_ffn_W1': _L0_ffn_in['W1'], 'L0_ffn_b1': _L0_ffn_in['b1'], 'L0_ffn_W2': _L0_ffn_in['W2'], 'L0_ffn_b2': _L0_ffn_in['b2']}

def reference(x, ctx_2048, L0_attn_gamma, L0_attn_beta, L0_attn_Wqkv, L0_attn_Wout, L0_xattn_Wq, L0_xattn_Wkv, L0_xattn_null_kv, L0_xattn_Wout, L0_xattn_ln_scale, L0_xattn_ln_bias, L0_ffn_Wqkv, L0_ffn_q_scale, L0_ffn_k_scale, L0_ffn_Wo, L0_ffn_ln_g, L0_ffn_ln_b, L0_ffn_W1, L0_ffn_b1, L0_ffn_W2, L0_ffn_b2):
    import jax
    import jax.numpy as jnp

    def _L0_attn_ref(x, gamma, beta, Wqkv, Wout):
        import jax, jax.numpy as jnp
        import numpy as np
        LN_EPS = 1e-05
        DENOM_EPS = 1e-06
        NUM_HEADS = 16

        def _layer_norm(x, gamma, beta):
            mu = jnp.mean(x, axis=-1, keepdims=True)
            var = jnp.mean(jnp.square(x - mu), axis=-1, keepdims=True)
            return (x - mu) * jax.lax.rsqrt(var + LN_EPS) * gamma + beta
        B, L, D = x.shape
        H = NUM_HEADS
        HD = D // H
        residual = x
        xn = _layer_norm(x, gamma, beta)
        qkv = (xn @ Wqkv).reshape(B, L, 3, H, HD)
        qkv = jnp.transpose(qkv, (2, 0, 3, 1, 4))
        q, k, v = (qkv[0], qkv[1], qkv[2])
        q = jax.nn.elu(q) + 1.0
        k = jax.nn.elu(k) + 1.0
        kv = jnp.einsum('bhld,bhle->bhde', k, v)
        qkv_out = jnp.einsum('bhld,bhde->bhle', q, kv)
        denom = jnp.einsum('bhld,bhd->bhl', q, k.sum(axis=2)) + DENOM_EPS
        out = qkv_out / denom[..., None]
        out = jnp.transpose(out, (0, 2, 1, 3)).reshape(B, L, D)
        return residual + out @ Wout

    def _L0_xattn_ref(x, context, Wq, Wkv, null_kv, Wout, ln_scale, ln_bias):
        import jax, jax.numpy as jnp
        import numpy as np
        B, N, DIM = (8, 512, 128)
        M, CTX = (32, 256)
        HEADS, DH = (16, 64)
        INNER = HEADS * DH
        EPS = 1e-06

        def _split_heads(t):
            b, n, _ = t.shape
            return t.reshape(b, n, HEADS, DH).transpose(0, 2, 1, 3)
        scale = DH ** (-0.5)
        b = x.shape[0]
        q = _split_heads(jnp.einsum('bnd,df->bnf', x, Wq))
        kv = jnp.einsum('bmc,cf->bmf', context, Wkv)
        k, v = jnp.split(kv, 2, axis=-1)
        k, v = (_split_heads(k), _split_heads(v))
        nk = jnp.broadcast_to(null_kv[0], (b, HEADS, 1, DH))
        nv = jnp.broadcast_to(null_kv[1], (b, HEADS, 1, DH))
        k = jnp.concatenate((nk, k), axis=-2)
        v = jnp.concatenate((nv, v), axis=-2)
        q = q * scale
        sim = jnp.einsum('bhid,bhjd->bhij', q, k)
        attn = jax.nn.softmax(sim, axis=-1)
        out = jnp.einsum('bhij,bhjd->bhid', attn, v)
        out = out.transpose(0, 2, 1, 3).reshape(b, -1, INNER)
        out = jnp.einsum('bnf,fd->bnd', out, Wout)
        mu = jnp.mean(out, axis=-1, keepdims=True)
        var = jnp.var(out, axis=-1, keepdims=True)
        out = (out - mu) * jax.lax.rsqrt(var + EPS) * ln_scale + ln_bias
        return out

    def _L0_ffn_ref(x, Wqkv, q_scale, k_scale, Wo, ln_g, ln_b, W1, b1, W2, b2):
        import jax, jax.numpy as jnp
        import numpy as np
        DIM = 128
        DEPTH = 6
        HEADS = 16
        DIM_HEAD = 64
        WINDOW = 32
        INNER = HEADS * DIM_HEAD
        DIM_INNER = int(DIM * 4 * 2 / 3)
        QK_SCALE = 8.0

        def shift_tokens(t):
            a, s = jnp.split(t, 2, -1)
            s = jnp.pad(s, ((0, 0), (1, 0), (0, 0)))[:, :-1]
            return jnp.concatenate([a, s], -1)

        def l2norm(t):
            return t / jnp.maximum(jnp.linalg.norm(t, axis=-1, keepdims=True), 1e-12)

        def rotate_half(x):
            x1, x2 = jnp.split(x, 2, -1)
            return jnp.concatenate([-x2, x1], -1)

        def rotary_tables(n):
            half = jnp.arange(0, DIM_HEAD, 2, dtype=jnp.float32)
            inv_freq = 1.0 / 10000.0 ** (half / DIM_HEAD)
            t = jnp.arange(n, dtype=jnp.float32)
            freqs = t[:, None] * inv_freq[None, :]
            freqs = jnp.concatenate([freqs, freqs], -1)
            base_scale = (half + 0.4 * DIM_HEAD) / (1.4 * DIM_HEAD)
            power = (t - n // 2) / (WINDOW // 2)
            scale = base_scale[None, :] ** power[:, None]
            scale = jnp.concatenate([scale, scale], -1)
            return (freqs, scale)

        def local_attention(q, k, v):
            b, h, n, d = q.shape
            w = WINDOW
            nw = n // w
            bq = q.reshape(b, h, nw, w, d)
            bk = k.reshape(b, h, nw, w, d)
            bv = v.reshape(b, h, nw, w, d)

            def look(t):
                p = jnp.pad(t, ((0, 0), (0, 0), (1, 0), (0, 0), (0, 0)))
                return jnp.concatenate([p[:, :, :nw], p[:, :, 1:]], axis=3)
            bk2, bv2 = (look(bk), look(bv))
            seq = jnp.arange(n).reshape(nw, w)
            seq_p = jnp.pad(seq, ((1, 0), (0, 0)), constant_values=-1)
            jt = jnp.concatenate([seq_p[:nw], seq_p[1:]], axis=1)
            it = seq[:, :, None]
            jb = jt[:, None, :]
            mask = (it < jb) | (it > jb + w) | (jb == -1)
            sim = jnp.einsum('bhwie,bhwje->bhwij', bq, bk2) * QK_SCALE
            sim = jnp.where(mask, -jnp.finfo(sim.dtype).max, sim)
            attn = jax.nn.softmax(sim, -1)
            out = jnp.einsum('bhwij,bhwje->bhwie', attn, bv2)
            return out.reshape(b, h, n, d)

        def attn_layer(x, Wqkv, qs, ksc, Wo):
            b, n, _ = x.shape
            qkv = x @ Wqkv
            q, k, v = jnp.split(qkv, 3, -1)
            sh = lambda t: t.reshape(b, n, HEADS, DIM_HEAD).transpose(0, 2, 1, 3)
            q, k, v = (sh(q), sh(k), sh(v))
            q = l2norm(q) * qs
            k = l2norm(k) * ksc
            freqs, scale = rotary_tables(n)
            cos, sin = (jnp.cos(freqs), jnp.sin(freqs))
            q = q * cos * scale + rotate_half(q) * sin * scale
            inv = 1.0 / scale
            k = k * cos * inv + rotate_half(k) * sin * inv
            out = local_attention(q, k, v)
            out = out.transpose(0, 2, 1, 3).reshape(b, n, INNER)
            return out @ Wo

        def ffn_layer(x, g, bln, W1, b1, W2, b2):
            mu = x.mean(-1, keepdims=True)
            var = ((x - mu) ** 2).mean(-1, keepdims=True)
            xn = (x - mu) / jnp.sqrt(var + 1e-05) * g + bln
            hg = xn @ W1 + b1
            a, gate = jnp.split(hg, 2, -1)
            return a * jax.nn.gelu(gate, approximate=False) @ W2 + b2
        for i in range(DEPTH):
            x = attn_layer(shift_tokens(x), Wqkv[i], q_scale[i], k_scale[i], Wo[i]) + x
            x = ffn_layer(shift_tokens(x), ln_g[i], ln_b[i], W1[i], b1[i], W2[i], b2[i]) + x
        return x
    x = _layernorm(x + _L0_attn_ref(x, L0_attn_gamma, L0_attn_beta, L0_attn_Wqkv, L0_attn_Wout), axis=-1)
    x = _layernorm(x + _L0_xattn_ref(x, ctx_2048, L0_xattn_Wq, L0_xattn_Wkv, L0_xattn_null_kv, L0_xattn_Wout, L0_xattn_ln_scale, L0_xattn_ln_bias), axis=-1)
    x = _layernorm(x + _L0_ffn_ref(x, L0_ffn_Wqkv, L0_ffn_q_scale, L0_ffn_k_scale, L0_ffn_Wo, L0_ffn_ln_g, L0_ffn_ln_b, L0_ffn_W1, L0_ffn_b1, L0_ffn_W2, L0_ffn_b2), axis=-1)
    return x

_drawn_inputs = setup_inputs


def setup_inputs(seed=0):
    import zlib

    import numpy as np

    out = dict(_drawn_inputs(seed))
    spreads = {'L0_attn_gamma': (1.0, 0.6),
     'L0_attn_beta': (0.0, 0.1),
     'L0_xattn_ln_scale': (1.0, 0.2),
     'L0_xattn_ln_bias': (0.0, 0.1),
     'L0_ffn_q_scale': (1.0, 0.6),
     'L0_ffn_k_scale': (1.0, 0.6),
     'L0_ffn_ln_g': (1.0, 0.6),
     'L0_ffn_ln_b': (0.0, 0.8),
     'L0_ffn_b1': (0.0, 0.8),
     'L0_ffn_b2': (0.0, 0.1)}
    factors = {'L0_xattn_null_kv': 3.142, 'L0_ffn_W1': 3.689, 'L0_ffn_W2': 3.58}
    for name, (base, spread) in spreads.items():
        noise = np.random.default_rng([zlib.crc32(name.encode()), seed]).standard_normal(out[name].shape)
        drawn = base * np.exp(spread * noise) if base else spread * noise
        out[name] = jnp.asarray(drawn.astype(out[name].dtype))
    for name, factor in factors.items():
        out[name] = (out[name] * factor).astype(out[name].dtype)
    return out
```

```python
from contextlib import ExitStack

import numpy as np

import concourse.bass as bass
from concourse import mybir

F32 = mybir.dt.float32
F32R = mybir.dt.float32r
BF16 = mybir.dt.bfloat16
ALU = mybir.AluOpType
ACT = mybir.ActivationFunctionType
AX = mybir.AxisListType

P = 128
B = 16
D = 128
H = 16
DH = 64
INNER = H * DH
CTX = 256
CK = CTX // P
M = 77
NULLK = M + 1
HD = D // H
LAYERS = 6
FF = 341
FB = 3
WINDOW = 32
HQ = 4
QUARTERS = H // HQ
QW = HQ * DH
G = 4
GROUPS = B // G
PER = 2 * QUARTERS
OUTER = B // 2
STEPS = B * QUARTERS
CREDIT = 8
MASKED = -1e30
FBLK = [(j * P, min(P, FF - j * P)) for j in range(FB)]


class At:

    def __init__(self, i, k):
        self.s = i * PER + k
        self.batch = i * 2 + k // QUARTERS
        self.two = i + k // PER
        self.q = k % QUARTERS
        self.pair = k % 2
        self.bpair = (k // QUARTERS) % 2


def quarter_steps(eng, body, tail):
    for k in range(PER):
        body(0, k, lambda lag: k - lag >= 0)
    with eng.Fori(1, OUTER) as i:
        for k in range(PER):
            body(i, k, lambda lag: True)
    for k in range(tail):
        body(OUTER, k, lambda lag: k - lag < 0)


def build(nc, t, out):
    ctx = ExitStack()
    with ctx:
        def sb(name, shape, dt=F32):
            return ctx.enter_context(nc.sbuf_tensor(name, shape, dt))

        def sem(name):
            return ctx.enter_context(nc.semaphore(name))

        x = sb("x", [P, B + 1, D])
        ident = sb("ident", [P, P])
        shift = sb("shift", [P, P])
        ident_bf = sb("ident_bf", [P, P], BF16)
        mask_bf = sb("mask_bf", [P, HQ, P], BF16)
        half = sb("half", [P, G])
        lnstat = sb("lnstat", [P, G, 6])
        lnmv = sb("lnmv", [P, G, 2])
        lnseen = sb("lnseen", [P, 1])
        lnvar = sb("lnvar", [P, G])
        lnrs = sb("lnrs", [P, G])
        lnz = sb("lnz", [P, G, D])
        lnx = sb("lnx", [P, G, D])
        gam = sb("gam", [P, 1])
        bet = sb("bet", [P, 1])
        wqkv1 = sb("wqkv1", [P, 3 * D])
        wout1 = sb("wout1", [P, D])
        blockmask = sb("blockmask", [P, P])
        headmask = sb("headmask", [P, H])
        xnT = sb("xnT", [P, G, P])
        qk1 = sb("qk1", [P, G, 2 * D])
        neg = sb("neg", [P, G, 2 * D])
        v1 = sb("v1", [P, G, D + 1])
        kvm = sb("kvm", [P, G, D + H])
        q1T = sb("q1T", [P, G, P])
        den1 = sb("den1", [P, G, H])
        o1 = sb("o1", [P, G, D])
        o1T = sb("o1T", [P, G, P])
        wq2 = sb("wq2", [P, INNER])
        wkv2 = sb("wkv2", [P, CK, 2 * INNER])
        wout2 = sb("wout2", [P, INNER // P, D])
        lns2 = sb("lns2", [P, D])
        lnb2 = sb("lnb2", [P, D])
        cst = sb("cst", [M, 2, CTX])
        ctxT = sb("ctxT", [P, 2, CK, M])
        kz2 = sb("kz2", [P, 2, 2, 2, NULLK])
        vs2 = sb("vs2", [NULLK, 2, QW])
        nullk = sb("nullk", [P, 1])
        ybuf = sb("ybuf", [P, B, D])
        rot_cs = sb("rot_cs", [P, 2, 2, DH])
        qks_all = sb("qks_all", [P, LAYERS, 2, DH])
        rot_tab = sb("rot_tab", [P, 2, 2, DH])
        wst = sb("wst", [P, QUARTERS, 3 * QW])
        wh = sb("wh", [P, QUARTERS, 3 * QW], F32R)
        wl = sb("wl", [P, QUARTERS, 3 * QW], F32R)
        wo = sb("wo", [P, INNER // P, D])
        xin = sb("xin", [P, 2, D])
        xTh = sb("xTh", [P, 2, P], F32R)
        xTl = sb("xTl", [P, 2, P], F32R)
        xTf = sb("xTf", [P, 2, P])
        sq = sb("sq", [P, 2, 2 * QW])
        ta = sb("ta", [P, 2, 2 * QW])
        tb = sb("tb", [P, 2, 2 * QW])
        ssq = sb("ssq", [P, 2, 2 * HQ])
        lnr = sb("lnr", [P, 2, 2 * HQ])
        rn = sb("rn", [P, 2, 2 * HQ])
        lnbias = sb("lnbias", [P, 1])
        qks = sb("qks", [P, 2, 2 * QW])
        qT = sb("qT", [P, 2, 2, P])
        kz = sb("kz", [P, 2, 2, 2, P])
        mx = sb("mx", [P, 2, HQ])
        pr = sb("pr", [P, 2, HQ, P])
        den = sb("den", [P, 2, HQ])
        rden = sb("rden", [P, 2, HQ])
        pT = sb("pT", [P, 2, HQ, P])
        vs = sb("vs", [P, 2, QW])
        oT = sb("oT", [P, 2, INNER // P, P])
        vec_all = sb("vec_all", [P, LAYERS, NVEC])
        vec = sb("vec", [P, NVEC])
        b1a, b1g = vec[:, 2:2 + FB], vec[:, 2 + FB:2 + 2 * FB]
        b2 = sb("b2", [P, LAYERS, D])
        w1st = sb("w1st", [P, 2 * FF])
        w1h = sb("w1h", [P, 2 * FF], F32R)
        w1l = sb("w1l", [P, 2 * FF], F32R)
        w2 = sb("w2", [P, FB, D])
        xfT = sb("xfT", [P, G, P])
        xfTh = sb("xfTh", [P, G, P], F32R)
        xfTl = sb("xfTl", [P, G, P], F32R)
        gel = sb("gel", [P, 2, G * P])
        hT = sb("hT", [P, FB, G * P])

        bank = [ctx.enter_context(nc.psum_tensor(f"bank{i}", [P, 512], F32)) for i in range(8)]
        QKB, TB_, SB_, PTB, VB, OB = bank[0:2], bank[2], bank[3:5], bank[5], bank[6], bank[7]

        ld_x = sem("ld_x")
        ld_c = sem("ld_c")
        ld_tab = sem("ld_tab")
        ld_ctx = [sem("ld_ctx0"), sem("ld_ctx1")]
        ld_wq = sem("ld_wq")
        ld_w1 = sem("ld_w1")
        ld_wo = sem("ld_wo")
        ld_w2 = sem("ld_w2")
        st_out = sem("st_out")
        pool_const = sem("pool_const")
        dve_const = sem("dve_const")
        ln_stats = sem("ln_stats")
        ln_mv = sem("ln_mv")
        ln_var = sem("ln_var")
        ln_rs = sem("ln_rs")
        ln_out = sem("ln_out")
        g_T = sem("g_T")
        g_xnT = sem("g_xnT")
        g_qkv = sem("g_qkv")
        g_min = sem("g_min")
        g_exp = sem("g_exp")
        g_qk1 = sem("g_qk1")
        g_v1 = sem("g_v1")
        g_kv = sem("g_kv")
        g_kvm = sem("g_kvm")
        g_q1T_ps = sem("g_q1T_ps")
        g_q1T = sem("g_q1T")
        g_o = sem("g_o")
        g_den = sem("g_den")
        g_rden = sem("g_rden")
        g_o1 = sem("g_o1")
        g_o1T_ps = sem("g_o1T_ps")
        g_o1T = sem("g_o1T")
        g_y = sem("g_y")
        g_z = sem("g_z")
        g_x = sem("g_x")
        x_in = sem("x_in")
        xT_ps = sem("xT_ps")
        xT_hi = sem("xT_hi")
        xT_done = sem("xT_done")
        c_ps = sem("c_ps")
        c_done = sem("c_done")
        step_sems = {}

        def step_sem(name):
            step_sems[name] = sem(name)
            return step_sems[name]

        qk_ps = step_sem("qk_ps")
        sq_done = step_sem("sq_done")
        rot_done = step_sem("rot_done")
        ssq_raw = step_sem("ssq_raw")
        ssq_done = step_sem("ssq_done")
        ln_done = step_sem("ln_done")
        rn_done = step_sem("rn_done")
        add_done = step_sem("add_done")
        qks_done = step_sem("qks_done")
        t_ps = step_sem("t_ps")
        qT_done = step_sem("qT_done")
        kT_done = step_sem("kT_done")
        kz_done = step_sem("kz_done")
        s_ps = step_sem("s_ps")
        mx_done = step_sem("mx_done")
        sub_done = step_sem("sub_done")
        exp_done = step_sem("exp_done")
        den_done = step_sem("den_done")
        rden_done = step_sem("rden_done")
        pr_done = step_sem("pr_done")
        pT_ps = step_sem("pT_ps")
        pT_done = step_sem("pT_done")
        v_ps = step_sem("v_ps")
        v_done = step_sem("v_done")
        o_ps = step_sem("o_ps")
        oT_done = step_sem("oT_done")
        y_ps = step_sem("y_ps")
        y_done = step_sem("y_done")
        post2 = sem("post2")
        kept = sem("kept")
        last_z = sem("last_z")
        tab_cos = sem("tab_cos")
        tab_done = sem("tab_done")
        wq_hi = sem("wq_hi")
        wq_split = sem("wq_split")
        w1_hi = sem("w1_hi")
        w1_split = sem("w1_split")
        f_shift = sem("f_shift")
        f_z = sem("f_z")
        f_z0 = sem("f_z0")
        f_b2 = sem("f_b2")
        f_T = sem("f_T")
        f_xT = sem("f_xT")
        f_hi = sem("f_hi")
        f_split = sem("f_split")
        f_ab = sem("f_ab")
        f_gel = sem("f_gel")
        f_h = sem("f_h")
        f_y = sem("f_y")
        f_x = sem("f_x")

        block = ctx.enter_context(nc.Block())

        def start_with_credit(eng, names, local=()):
            for n in names:
                eng.sem_inc(step_sems[n], CREDIT)
            for n in local:
                eng.sem_inc(step_sems[n], CREDIT + STEPS)

        class Phase:

            def __init__(self, local, base, bbase):
                self.local = local
                self.keys = P if local else NULLK
                self.base = base
                self.bbase = bbase

            def n(self, at, back=0):
                return at.s + (self.base + (CREDIT + 1 - back))

            def nb(self, at, back=0):
                return at.batch + (self.bbase + (CREDIT + 1 - back))

        def phase2():
            p = Phase(False, 0, 0)
            p.xb = 0
            return p

        def phase3(l):
            p = Phase(True, l * STEPS + STEPS, l * B + B)
            p.xb = l * (B + 1) + (B + 1)
            return p

        @block.sync
        def _(sp):
            xv = t["x"].rearrange("b p d -> p b d")
            for g in range(GROUPS):
                sp.dma_start(x[:, g * G:(g + 1) * G, :], xv[:, g * G:(g + 1) * G, :]).then_inc(ld_x, 16)
            col = lambda a: a.rearrange("(p o) -> p o", o=1)
            row = lambda a: a.rearrange("(o p) -> o p", o=1)
            first = [
                (gam[:, :], col(t["L0_attn_gamma"])), (bet[:, :], col(t["L0_attn_beta"])),
                (wqkv1[:, :], t["L0_attn_Wqkv"]), (wout1[:, :], t["L0_attn_Wout"]),
                (blockmask[:, :], t["c_blockmask"]), (headmask[:, :], t["c_headmask"]),
                (wq2[:, :], t["L0_xattn_Wq"]),
                (wkv2[:, :, :], t["L0_xattn_Wkv"].rearrange("(c p) n -> p c n", p=P)),
                (wout2[:, :, :], t["L0_xattn_Wout"].rearrange("(j p) n -> p j n", p=P)),
                (lns2[:, :], row(t["L0_xattn_ln_scale"]).to_broadcast([P, D])),
                (lnb2[:, :], row(t["L0_xattn_ln_bias"]).to_broadcast([P, D])),
                (nullk[0:DH, :], col(t["L0_xattn_null_kv"][0])),
                (nullk[DH:P, :], col(t["L0_xattn_null_kv"][0])),
            ]
            for dst, src in first:
                sp.dma_start(dst, src).then_inc(ld_c, 16)
            for r in range(2):
                for h in range(HQ):
                    sp.dma_start(vs2[M:M + 1, r, h * DH:(h + 1) * DH],
                                 t["L0_xattn_null_kv"][1:2, :]).then_inc(ld_c, 16)
            assert N_LD_C == len(first) + 2 * HQ

            def load_wq(l):
                for j in range(3):
                    sp.dma_start(wst[:, :, j * QW:(j + 1) * QW],
                                 t["L0_ffn_Wqkv"][l, :, j * INNER:(j + 1) * INNER]
                                 .rearrange("p (q n) -> p q n", q=QUARTERS)).then_inc(ld_wq, 16)

            def load_w1(l):
                sp.dma_start(w1st[:, :], t["L0_ffn_W1"][l]).then_inc(ld_w1, 16)

            def load_wo(l):
                sp.dma_start(wo[:, :, :], t["L0_ffn_Wo"][l].rearrange("(j p) n -> p j n", p=P)).then_inc(ld_wo, 16)

            def load_w2(l):
                sp.dma_start(w2[:, 0:2, :], t["L0_ffn_W2"][l, 0:2 * P, :].rearrange("(j p) n -> p j n", p=P)
                             ).then_inc(ld_w2, 16)
                sp.dma_start(w2[0:FF - 2 * P, 2, :], t["L0_ffn_W2"][l, 2 * P:FF, :]).then_inc(ld_w2, 16)

            def load_ctx(b, slot):
                sp.dma_start(cst[:, slot, :], t["ctx_2048"][b]).then_inc(ld_ctx[slot], 16)

            for b in range(2):
                load_ctx(b, b)
            load_wq(0)
            every = lambda a, n: a.rearrange("l n -> (l n)").rearrange("(o n) -> o n", o=1).to_broadcast([P, n])
            tables = [
                (rot_cs[:, :, :, :], t["c_rot"]), (vec_all[:, :, :], t["vectors"]),
                (qks_all[:, :, :, :].rearrange("p l a d -> p (l a d)"), every(t["qk_scales"], LAYERS * 2 * DH)),
                (b2[:, :, :].rearrange("p l d -> p (l d)"), every(t["L0_ffn_b2"], LAYERS * D)),
            ]
            for dst, src in tables:
                sp.dma_start(dst, src).then_inc(ld_tab, 16)
            assert N_LD_TAB == len(tables)
            load_w1(0)
            load_wo(0)
            load_w2(0)
            with sp.Fori(0, OUTER) as i:
                for b in range(2):
                    sp.wait_ge(c_ps, i * 2 + (b + 1))
                    load_ctx((i * 2 + (b + 2)) % B, b)
            with sp.Fori(0, LAYERS) as l:
                sp.wait_ge(wq_split, l + 1)
                load_wq((l + 1) % LAYERS)
                sp.wait_ge(w1_split, l + 1)
                load_w1((l + 1) % LAYERS)
                sp.wait_ge(y_done, l * B + (2 * B + CREDIT))
                load_wo((l + 1) % LAYERS)
                sp.wait_ge(f_x, l * GROUPS + (GROUPS + 1))
                load_w2((l + 1) % LAYERS)
            ov = out.rearrange("b p d -> p b d")
            for g in range(GROUPS):
                sp.wait_ge(ln_out, LN_FINAL + g + 1)
                sp.dma_start(ov[:, g * G:(g + 1) * G, :], x[:, g * G:(g + 1) * G, :]).then_inc(st_out, 16)
            for b in range(2):
                sp.wait_ge(ld_ctx[b], 16 * (OUTER + 1))
            sp.wait_ge(ld_wq, 16 * 3 * (LAYERS + 1))
            sp.wait_ge(ld_w1, 16 * (LAYERS + 1))
            sp.wait_ge(ld_wo, 16 * (LAYERS + 1))
            sp.wait_ge(ld_w2, 16 * 2 * (LAYERS + 1))
            sp.wait_ge(st_out, 16 * GROUPS)

        @block.gpsimd
        def _(pool):
            pool.memset(ident[:], 0.0).then_inc(pool_const, 1)
            pool.memset(shift[:], 0.0).then_inc(pool_const, 1)
            pool.memset(ident_bf[:], 0.0).then_inc(pool_const, 1)
            pool.memset(mask_bf[:], 0.0).then_inc(pool_const, 1)
            pool.memset(half[:], -0.5).then_inc(pool_const, 1)
            pool.wait_ge(pool_const, 5)
            pool.affine_select(out=ident[:], in_=ident[:], compare_op=ALU.not_equal, fill=1.0, base=0,
                               pattern=[[-1, P]], channel_multiplier=1).then_inc(pool_const, 1)
            pool.affine_select(out=shift[:], in_=shift[:], compare_op=ALU.not_equal, fill=1.0, base=1,
                               pattern=[[-1, P]], channel_multiplier=1).then_inc(pool_const, 1)
            pool.affine_select(out=ident_bf[:], in_=ident_bf[:], compare_op=ALU.not_equal, fill=1.0, base=0,
                               pattern=[[-1, P]], channel_multiplier=1).then_inc(pool_const, 1)
            pool.affine_select(out=mask_bf[:], in_=mask_bf[:], compare_op=ALU.is_ge, fill=MASKED, base=0,
                               pattern=[[0, HQ], [-1, P]], channel_multiplier=1).then_inc(pool_const, 1)
            pool.wait_ge(pool_const, 9)
            pool.affine_select(out=mask_bf[:], in_=mask_bf[:], compare_op=ALU.is_ge, fill=MASKED, base=WINDOW,
                               pattern=[[0, HQ], [1, P]], channel_multiplier=-1).then_inc(pool_const, 1)
            start_with_credit(pool, ["pr_done"], ["add_done", "qks_done"])

            def rsqrt_of(count):
                pool.wait_ge(ln_var, count)
                pool.tensor_tensor(lnrs[:, :], lnvar[:, :], half[:, :], ALU.pow).then_inc(ln_rs, 1)

            with pool.Fori(0, 2 * GROUPS) as n:
                rsqrt_of(n + 1)

            def normalise(ph, at):
                pool.wait_ge(rden_done, ph.n(at))
                w = pr[:, at.pair, :, 0:ph.keys]
                pool.tensor_tensor(w, w, rden[:, at.pair, :].unsqueeze(2).to_broadcast([P, HQ, ph.keys]),
                                   ALU.mult).then_inc(pr_done, 1)

            def body2(i, k, live):
                if live(2):
                    normalise(phase2(), At(i, k - 2))

            quarter_steps(pool, body2, 2)
            with pool.Fori(0, 2 * GROUPS) as n:
                rsqrt_of(n + (LN_POST2 + 1))

            def split_wq(l):
                pool.wait_ge(wq_hi, l + 1)
                pool.tensor_tensor(wl[:, :, :], wst[:, :, :], wh[:, :, :].bitcast(F32), ALU.subtract
                                   ).then_inc(wq_split, 1)

            split_wq(0)
            with pool.Fori(0, LAYERS) as l:
                ph = phase3(l)
                pool.wait_ge(w1_hi, l + 1)
                pool.tensor_tensor(w1l[:, :], w1st[:, :], w1h[:, :].bitcast(F32), ALU.subtract).then_inc(w1_split, 1)

                def add(at):
                    pool.wait_ge(rot_done, ph.n(at))
                    pool.tensor_tensor(ta[:, at.pair, :], ta[:, at.pair, :], tb[:, at.pair, :], ALU.add
                                       ).then_inc(add_done, 1)

                def scale(at):
                    pool.wait_ge(rn_done, ph.n(at))
                    pool.wait_ge(add_done, ph.n(at))
                    pool.wait_ge(t_ps, ph.n(at, 2))
                    pool.tensor_tensor(qks[:, at.pair, :].rearrange("p (h d) -> p h d", d=DH),
                                       ta[:, at.pair, :].rearrange("p (h d) -> p h d", d=DH),
                                       rn[:, at.pair, :].unsqueeze(2).to_broadcast([P, 2 * HQ, DH]),
                                       ALU.mult).then_inc(qks_done, 1)

                def body(i, k, live):
                    if live(0):
                        add(At(i, k))
                    if live(2):
                        normalise(ph, At(i, k - 2))
                    if live(0):
                        scale(At(i, k))

                quarter_steps(pool, body, 2)
                with pool.Fori(0, GROUPS) as g:
                    rsqrt_of(l * GROUPS + g + (LN_FF + 1))
                    pool.wait_ge(f_z, l * GROUPS + g + 2)
                    pool.wait_ge(f_z0, l * GROUPS + g + 1)
                    pool.tensor_tensor(x[:, bass.ds(g * G, G), :], x[:, bass.ds(g * G, G), :],
                                       b2[:, bass.ds(l, 1), :].to_broadcast([P, G, D]), ALU.add).then_inc(f_b2, 1)
                split_wq(l + 1)
            with pool.Fori(0, GROUPS) as n:
                rsqrt_of(n + (LN_FINAL + 1))

        @block.vector
        def _(dve):
            dve.memset(v1[:, :, D:D + 1], 1.0).then_inc(dve_const, 1)
            dve.memset(kz[:], 0.0).then_inc(dve_const, 1)
            dve.memset(kz2[:], 0.0).then_inc(dve_const, 1)
            dve.memset(x[:, B:B + 1, :], 0.0).then_inc(dve_const, 1)
            dve.memset(lnbias[:], float(np.log(2.0 ** 8))).then_inc(dve_const, 1)
            start_with_credit(dve, ["kz_done", "mx_done", "sub_done", "den_done", "rden_done", "y_done"],
                              ["rot_done", "ssq_raw", "ssq_done"])
            dve.sem_inc(f_z, 1)
            dve.sem_inc(f_x, 1)
            dve.wait_ge(ld_c, 16 * N_LD_C)
            dve.wait_ge(dve_const, 5)
            for h in range(2):
                dve.tensor_copy(kz2[h * DH:(h + 1) * DH, :, :, h, M:NULLK].rearrange("p a b o -> p (a b) o"),
                                nullk[h * DH:(h + 1) * DH, :].unsqueeze(1).to_broadcast([DH, 4, 1])
                                ).then_inc(dve_const, 1)

            def norm(count, src, dst, eps, n=None):
                for j in range(G):
                    ins = dve.bn_stats(lnstat[:, j, :], src(j))
                ins.then_inc(ln_stats, 1)
                dve.wait_ge(ln_stats, count)
                dve.tensor_copy(lnseen[:, :], lnstat[:, 0, 0:1])
                for j in range(G):
                    ins = dve.bn_aggr(lnmv[:, j, :], lnstat[:, j, :])
                ins.then_inc(ln_mv, 1)
                dve.wait_ge(ln_mv, count)
                dve.tensor_scalar(lnvar[:, :].unsqueeze(2), lnmv[:, :, 1:2], eps, None, ALU.add
                                  ).then_inc(ln_var, 1)
                dve.wait_ge(ln_rs, count)
                for j in range(G):
                    ins = dve.tensor_scalar(dst(j), src(j), lnmv[:, j, 0:1], lnrs[:, j:j + 1],
                                            ALU.subtract, ALU.mult)
                ins.then_inc(ln_out, 1)

            def xg(g):
                return lambda j: x[:, bass.ds(g * G + j, 1), :].rearrange("p o d -> p (o d)")

            zg = lambda j: lnz[:, j, :]
            ng = lambda j: lnx[:, j, :]

            dve.wait_ge(ld_x, 16 * GROUPS)
            with dve.Fori(0, GROUPS) as g:
                norm(g * 2 + 1, xg(g), ng, 1e-5)
                dve.wait_ge(g_qkv, g + 1)
                for j in range(G):
                    ins = dve.tensor_scalar(neg[:, j, :], bank[1 + j][:, 0:2 * D], 0.0, None, ALU.min)
                ins.then_inc(g_min, 1)
                dve.wait_ge(g_exp, g + 1)
                for j in range(G):
                    ins = dve.scalar_tensor_tensor(qk1[:, j, :], bank[1 + j][:, 0:2 * D], 0.0, neg[:, j, :],
                                                   ALU.max, ALU.add)
                ins.then_inc(g_qk1, 1)
                dve.wait_ge(g_kv, g + 1)
                for j in range(G):
                    kv = bank[5 + j // 2][:, (j % 2) * 160:(j % 2) * 160 + D + 1]
                    dve.tensor_tensor(kvm[:, j, 0:D], kv[:, 0:D], blockmask[:, :], ALU.mult)
                    ins = dve.tensor_scalar(kvm[:, j, D:D + H], headmask[:, :], kv[:, D:D + 1], None, ALU.mult)
                ins.then_inc(g_kvm, 1)
                dve.wait_ge(g_o, g + 1)
                for j in range(G):
                    o = bank[5 + j // 2][:, (j % 2) * 160:(j % 2) * 160 + D + H]
                    ins = dve.tensor_scalar(den1[:, j, :], o[:, D:D + H], 1e-6, None, ALU.add)
                ins.then_inc(g_den, 1)
                dve.wait_ge(g_den, g + 1)
                dve.reciprocal(den1[:, :, :], den1[:, :, :]).then_inc(g_rden, 1)
                dve.wait_ge(g_rden, g + 1)
                for j in range(G):
                    o = bank[5 + j // 2][:, (j % 2) * 160:(j % 2) * 160 + D]
                    ins = dve.tensor_tensor(o1[:, j, :].rearrange("p (h e) -> p h e", e=HD),
                                            o.rearrange("p (h e) -> p h e", e=HD),
                                            den1[:, j, :].unsqueeze(2).to_broadcast([P, H, HD]), ALU.mult)
                ins.then_inc(g_o1, 1)
                dve.wait_ge(g_y, g + 1)
                dve.scalar_tensor_tensor(lnz[:, :, :], x[:, bass.ds(g * G, G), :], 2.0,
                                         bank[7][:, :].rearrange("p (j d) -> p j d", d=D),
                                         ALU.mult, ALU.add).then_inc(g_z, 1)
                dve.wait_ge(g_z, g + 1)
                norm(g * 2 + 2, zg, xg(g), 1e-5)

            def xT_split(ph, at, n):
                dve.wait_ge(xT_ps, n)
                dve.wait_ge(v_ps, ph.n(at, 5))
                ps = VB[:, 384:512]
                if ph.local:
                    dve.tensor_copy(xTh[:, at.bpair, :], ps).then_inc(xT_hi, 1)
                    dve.wait_ge(xT_hi, n)
                    dve.tensor_tensor(xTl[:, at.bpair, :], ps, xTh[:, at.bpair, :].bitcast(F32), ALU.subtract
                                      ).then_inc(xT_done, 1)
                else:
                    dve.tensor_copy(xTf[:, at.bpair, :], ps).then_inc(xT_hi, 1)
                    dve.wait_ge(xT_hi, n)
                    dve.wait_ge(c_ps, n)
                    dve.tensor_copy(ctxT[:, at.bpair, :, :],
                                    TB_[:, 0:CK * M].rearrange("p (c m) -> p c m", m=M)).then_inc(xT_done, 1)

            def row_max(ph, at):
                dve.wait_ge(s_ps, ph.n(at))
                sim = SB_[at.pair][:, 0:HQ * ph.keys].rearrange("p (h j) -> p h j", j=ph.keys)
                dve.tensor_reduce(mx[:, at.pair, :], sim, AX.X, ALU.max).then_inc(mx_done, 1)
                dve.wait_ge(mx_done, ph.n(at))
                dve.wait_ge(pT_ps, ph.n(at, 2))
                dve.tensor_tensor(pr[:, at.pair, :, 0:ph.keys], sim,
                                  mx[:, at.pair, :].unsqueeze(2).to_broadcast([P, HQ, ph.keys]),
                                  ALU.subtract).then_inc(sub_done, 1)

            def row_sum(ph, at):
                dve.wait_ge(exp_done, ph.n(at))
                dve.tensor_reduce(den[:, at.pair, :], pr[:, at.pair, :, 0:ph.keys], AX.X, ALU.add
                                  ).then_inc(den_done, 1)
                dve.wait_ge(den_done, ph.n(at))
                dve.wait_ge(pr_done, ph.n(at, 2))
                dve.reciprocal(rden[:, at.pair, :], den[:, at.pair, :]).then_inc(rden_done, 1)

            def residual2(ph, at):
                dve.wait_ge(y_ps, ph.nb(at))
                dve.tensor_copy(ybuf[:, bass.ds(at.batch, 1), :].rearrange("p o d -> p (o d)"), VB[:, 256:384]
                                ).then_inc(y_done, 1)

            def body2(i, k, live):
                ph = phase2()
                if live(4) and At(i, k - 4).q == 3:
                    residual2(ph, At(i, k - 4))
                if live(2):
                    row_max(ph, At(i, k - 2))
                if live(0) and k % QUARTERS == 3:
                    nxt = At(i, k + 1)
                    xT_split(ph, nxt, nxt.batch + 1)
                if live(0):
                    at = At(i, k)
                    dve.wait_ge(qk_ps, ph.n(at))
                    dve.wait_ge(s_ps, ph.n(at, 2))
                    kps = QKB[at.pair][:, 256:256 + 2 * M].rearrange("p (b m) -> p b m", m=M)
                    for h in range(2):
                        r = slice(h * DH, (h + 1) * DH)
                        ins = dve.tensor_copy(kz2[r, at.pair, :, h, 0:M], kps[r, :, :])
                    ins.then_inc(kz_done, 1)
                if live(2):
                    row_sum(ph, At(i, k - 2))

            dve.wait_ge(dve_const, 7)
            xT_split(phase2(), At(0, 0), 1)
            quarter_steps(dve, body2, 4)

            with dve.Fori(0, GROUPS) as g:
                norm(g * 2 + (LN_POST2 + 1), lambda j: ybuf[:, bass.ds(g * G + j, 1), :].rearrange("p o d -> p (o d)"),
                     ng, 1e-6)
                dve.wait_ge(ln_out, g * 2 + (LN_POST2 + 1))
                dve.tensor_tensor(lnx[:, :, :], lnx[:, :, :], lns2[:, :].unsqueeze(1).to_broadcast([P, G, D]),
                                  ALU.mult).then_inc(post2, 1)
                dve.wait_ge(post2, g * 3 + 1)
                dve.tensor_tensor(lnz[:, :, :], lnx[:, :, :], lnb2[:, :].unsqueeze(1).to_broadcast([P, G, D]),
                                  ALU.add).then_inc(post2, 1)
                dve.wait_ge(post2, g * 3 + 2)
                dve.tensor_tensor(lnz[:, :, :], lnz[:, :, :], x[:, bass.ds(g * G, G), :], ALU.add
                                  ).then_inc(post2, 1)
                dve.wait_ge(post2, g * 3 + 3)
                norm(g * 2 + (LN_POST2 + 2), zg, xg(g), 1e-5)

            dve.wait_ge(ld_tab, 16 * N_LD_TAB)
            with dve.Fori(0, LAYERS) as l:
                ph = phase3(l)
                dve.wait_ge(f_x, l * GROUPS + 1)
                sc = qks_all[:, bass.ds(l, 1), :, :].rearrange("p o a d -> p (o a) d")
                dve.tensor_copy(vec[:, :].unsqueeze(1), vec_all[:, bass.ds(l, 1), :])
                dve.tensor_tensor(rot_tab[:, 0, :, :], rot_cs[:, 0, :, :], sc, ALU.mult)
                dve.tensor_tensor(rot_tab[:, 1, :, 0:32], rot_cs[:, 1, :, 0:32], sc[:, :, 32:64], ALU.mult)
                dve.tensor_tensor(rot_tab[:, 1, :, 32:64], rot_cs[:, 1, :, 32:64], sc[:, :, 0:32], ALU.mult
                                  ).then_inc(tab_done, 1)
                dve.wait_ge(tab_done, l + 1)

                def rotate(at):
                    dve.wait_ge(sq_done, ph.n(at))
                    dve.wait_ge(qks_done, ph.n(at, 2))
                    src = QKB[at.pair][:, :].rearrange("p (a h d) -> p a h d", a=2, d=DH)
                    cosp = ta[:, at.pair, :].rearrange("p (a h d) -> p a h d", a=2, d=DH)
                    sinp = tb[:, at.pair, :].rearrange("p (a h d) -> p a h d", a=2, d=DH)
                    dve.tensor_tensor(cosp, src,
                                      rot_tab[:, 0, :, :].unsqueeze(2).to_broadcast([P, 2, HQ, DH]), ALU.mult)
                    for lo, hi in ((0, 32), (32, 0)):
                        ins = dve.tensor_tensor(
                            sinp[:, :, :, lo:lo + 32], src[:, :, :, hi:hi + 32],
                            rot_tab[:, 1, :, lo:lo + 32].unsqueeze(2).to_broadcast([P, 2, HQ, 32]), ALU.mult)
                    ins.then_inc(rot_done, 1)

                def norms(at):
                    dve.wait_ge(sq_done, ph.n(at))
                    dve.tensor_reduce(ssq[:, at.pair, :], sq[:, at.pair, :].rearrange("p (h d) -> p h d", d=DH),
                                      AX.X, ALU.add).then_inc(ssq_raw, 1)
                    dve.wait_ge(ssq_raw, ph.n(at))
                    dve.tensor_scalar(ssq[:, at.pair, :], ssq[:, at.pair, :], 1e-24, None, ALU.max
                                      ).then_inc(ssq_done, 1)

                def residual(at):
                    dve.wait_ge(y_ps, ph.nb(at))
                    xb = x[:, bass.ds(at.batch, 1), :].rearrange("p o d -> p (o d)")
                    dve.tensor_tensor(xb, xb, VB[:, 256:384], ALU.add).then_inc(y_done, 1)

                def body(i, k, live):
                    if live(4) and At(i, k - 4).q == 3:
                        residual(At(i, k - 4))
                    if live(2):
                        row_max(ph, At(i, k - 2))
                    if live(0):
                        rotate(At(i, k))
                        norms(At(i, k))
                    if live(2):
                        row_sum(ph, At(i, k - 2))
                    if live(0) and k % QUARTERS == 3:
                        nxt = At(i, k + 1)
                        xT_split(ph, nxt, nxt.batch + (ph.xb + 1))

                xT_split(ph, At(0, 0), ph.xb + 1)
                quarter_steps(dve, body, 4)

                def front(g):
                    c = l * GROUPS + g + 1
                    dve.wait_ge(f_shift, c)
                    dve.tensor_copy(lnz[:, :, 64:128], bank[0][:, 0:G * 64].rearrange("p (j d) -> p j d", d=64)
                                    ).then_inc(f_z, 1)
                    dve.wait_ge(f_z, c + 1)
                    dve.wait_ge(f_z0, c)
                    norm(l * GROUPS + g + (LN_FF + 1), zg, ng, 1e-5)

                def split(g):
                    c = l * GROUPS + g + 1
                    dve.wait_ge(f_xT, c + 1)
                    dve.tensor_copy(xfTh[:, :, :], xfT[:, :, :]).then_inc(f_hi, 1)
                    dve.wait_ge(f_hi, c)
                    dve.tensor_tensor(xfTl[:, :, :], xfT[:, :, :], xfTh[:, :, :].bitcast(F32), ALU.subtract
                                      ).then_inc(f_split, 1)

                def back(g):
                    for j, (c0, cn) in enumerate(FBLK):
                        dve.wait_ge(f_gel, (l * GROUPS + g) * FB + (j + 1))
                        dve.scalar_tensor_tensor(hT[0:cn, j, :], bank[2 + 2 * (j % 2)][0:cn, :],
                                                 b1a[0:cn, j:j + 1], gel[0:cn, j % 2, :],
                                                 ALU.add, ALU.mult).then_inc(f_h, 1)
                    dve.wait_ge(f_y, l * GROUPS + g + 1)
                    dve.wait_ge(f_b2, l * GROUPS + g + 1)
                    xs = x[:, bass.ds(g * G, G), :]
                    dve.tensor_tensor(xs, xs, bank[6][:, :].rearrange("p (j d) -> p j d", d=D), ALU.add
                                      ).then_inc(f_x, 1)

                front(0)
                split(0)
                with dve.Fori(1, GROUPS) as g:
                    front(g)
                    back(g - 1)
                    split(g)
                back(GROUPS - 1)

            dve.wait_ge(kept, GROUPS)
            with dve.Fori(0, GROUPS) as g:
                xs = x[:, bass.ds(g * G, G), :]
                dve.wait_ge(ln_out, g + LN_FINAL)
                dve.tensor_tensor(lnz[:, :, :], xs, ybuf[:, bass.ds(g * G, G), :], ALU.add).then_inc(last_z, 1)
                dve.wait_ge(last_z, g + 1)
                norm(g + (LN_FINAL + 1), zg, xg(g), 1e-5)

        @block.scalar
        def _(act):
            start_with_credit(act, ["qT_done", "exp_done", "pT_done", "v_done", "oT_done"],
                              ["sq_done", "ln_done", "rn_done", "kT_done"])
            act.sem_inc(f_xT, 1)
            act.wait_ge(ld_c, 16 * N_LD_C)
            with act.Fori(0, GROUPS) as g:
                act.wait_ge(g_T, g + 1)
                act.activation(xnT[:, :, :], bank[0][:, :].rearrange("p (j t) -> p j t", t=P), ACT.Identity,
                               bias=bet[:, 0:1], scale=gam[:, 0:1]).then_inc(g_xnT, 1)
                act.wait_ge(g_min, g + 1)
                act.activation(neg[:, :, :], neg[:, :, :], ACT.Exp).then_inc(g_exp, 1)
                act.wait_ge(dve_const, 7)
                act.wait_ge(g_qk1, g + 1)
                for j in range(G):
                    ins = act.activation(v1[:, j, 0:D], bank[1 + j][:, 2 * D:3 * D], ACT.Copy)
                ins.then_inc(g_v1, 1)
                act.wait_ge(g_q1T_ps, g + 1)
                act.activation(q1T[:, :, :], bank[0][:, :].rearrange("p (j t) -> p j t", t=P), ACT.Copy
                               ).then_inc(g_q1T, 1)
                act.wait_ge(g_o1T_ps, g + 1)
                act.activation(o1T[:, :, :], bank[0][:, :].rearrange("p (j t) -> p j t", t=P), ACT.Copy
                               ).then_inc(g_o1T, 1)

            def take_x(ph, at, n):
                act.wait_ge(xT_ps, n - 2) if not isinstance(n, int) or n > 2 else None
                act.activation(xin[:, at.bpair, :], x[:, bass.ds(at.batch, 1), :].rearrange("p o d -> p (o d)"),
                               ACT.Copy).then_inc(x_in, 1)

            def exps(ph, at):
                act.wait_ge(sub_done, ph.n(at))
                w = pr[:, at.pair, :, 0:ph.keys]
                act.activation(w, w, ACT.Exp).then_inc(exp_done, 1)

            def take_pT(ph, at):
                act.wait_ge(pT_ps, ph.n(at))
                act.wait_ge(o_ps, ph.n(at, 2))
                act.activation(pT[0:ph.keys, at.pair, :, :],
                               PTB[0:ph.keys, :].rearrange("p (h t) -> p h t", t=P), ACT.Copy
                               ).then_inc(pT_done, 1)

            def take_v(ph, at):
                act.wait_ge(v_ps, ph.n(at))
                act.wait_ge(o_ps, ph.n(at, 2))
                if ph.local:
                    dst, rows = vs[:, at.pair, :], P
                else:
                    dst, rows = vs2[0:M, at.pair, :], M
                act.activation(dst, VB[0:rows, 0:QW], ACT.Copy).then_inc(v_done, 1)

            def take_o(ph, at):
                act.wait_ge(o_ps, ph.n(at))
                act.wait_ge(y_ps, ph.nb(at, 2))
                act.activation(oT[:, at.bpair, 2 * at.q:2 * at.q + 2, :],
                               OB[:, 0:2 * P].rearrange("p (j t) -> p j t", t=P), ACT.Copy
                               ).then_inc(oT_done, 1)

            def body2(i, k, live):
                ph = phase2()
                if live(0):
                    at = At(i, k)
                    act.wait_ge(qk_ps, ph.n(at))
                    act.wait_ge(kz_done, ph.n(at))
                    act.wait_ge(s_ps, ph.n(at, 2))
                    act.activation(qT[:, at.pair, :, :],
                                   QKB[at.pair][:, 0:2 * P].rearrange("p (j t) -> p j t", t=P), ACT.Copy,
                                   scale=DH ** -0.5).then_inc(qT_done, 1)
                if live(0) and k % QUARTERS == 2:
                    nxt = At(i, k + 2)
                    take_x(ph, nxt, nxt.batch + 1)
                if live(2):
                    exps(ph, At(i, k - 2))
                if live(3):
                    take_pT(ph, At(i, k - 3))
                    take_v(ph, At(i, k - 3))
                    take_o(ph, At(i, k - 3))

            act.wait_ge(ln_out, LN_POST2)
            take_x(phase2(), At(0, 0), 1)
            quarter_steps(act, body2, 3)

            def split_wq(l, n):
                act.wait_ge(ld_wq, n)
                act.activation(wh[:, :, :], wst[:, :, :], ACT.Copy).then_inc(wq_hi, 1)

            split_wq(0, 16 * 3)
            with act.Fori(0, GROUPS) as g:
                act.wait_ge(ln_out, g * 2 + (LN_POST2 + 2))
                act.activation(ybuf[:, bass.ds(g * G, G), :], x[:, bass.ds(g * G, G), :], ACT.Copy).then_inc(kept, 1)
            with act.Fori(0, LAYERS) as l:
                ph = phase3(l)

                def squares(at):
                    act.wait_ge(qk_ps, ph.n(at))
                    act.wait_ge(ssq_done, ph.n(at, 2))
                    act.activation(sq[:, at.pair, :], QKB[at.pair][:, :], ACT.Square).then_inc(sq_done, 1)

                def inverse_norm(at):
                    act.wait_ge(ssq_done, ph.n(at))
                    act.activation(lnr[:, at.pair, :], ssq[:, at.pair, :], ACT.Ln, scale=2.0 ** 16
                                   ).then_inc(ln_done, 1)
                    act.wait_ge(ln_done, ph.n(at))
                    act.wait_ge(qks_done, ph.n(at, 2))
                    act.activation(rn[:, at.pair, :], lnr[:, at.pair, :], ACT.Exp, scale=-0.5,
                                   bias=lnbias[:, 0:1]).then_inc(rn_done, 1)

                def take_T(at):
                    act.wait_ge(t_ps, ph.n(at))
                    act.wait_ge(s_ps, ph.n(at, 2))
                    act.activation(qT[:, at.pair, :, :], TB_[:, 0:2 * P].rearrange("p (j t) -> p j t", t=P),
                                   ACT.Copy).then_inc(qT_done, 1)
                    for h in range(2):
                        r = slice(h * DH, (h + 1) * DH)
                        ins = act.activation(kz[r, at.pair, :, h, :],
                                             TB_[r, 2 * P:4 * P].rearrange("p (j t) -> p j t", t=P), ACT.Copy)
                    ins.then_inc(kT_done, 1)

                def body(i, k, live):
                    if live(0):
                        squares(At(i, k))
                    if live(2):
                        exps(ph, At(i, k - 2))
                    if live(3):
                        take_pT(ph, At(i, k - 3))
                    if live(1):
                        take_T(At(i, k - 1))
                    if live(0):
                        inverse_norm(At(i, k))
                    if live(3):
                        take_v(ph, At(i, k - 3))
                        take_o(ph, At(i, k - 3))
                    if live(0) and k % QUARTERS == 2:
                        nxt = At(i, k + 2)
                        take_x(ph, nxt, nxt.batch + (ph.xb + 1))

                act.preload_act_table_set("natural_log_exp_and_others")
                act.wait_ge(ln_out, 4 * GROUPS)
                act.wait_ge(f_x, l * GROUPS + 1)
                take_x(ph, At(0, 0), ph.xb + 1)
                act.wait_ge(ld_w1, l * 16 + 16)
                act.activation(w1h[:, :], w1st[:, :], ACT.Copy).then_inc(w1_hi, 1)
                quarter_steps(act, body, 3)

                def front(g):
                    act.activation(lnz[:, :, 0:64], x[:, bass.ds(g * G, G), 0:64], ACT.Copy).then_inc(f_z0, 1)

                def take_T_ff(g):
                    act.wait_ge(f_T, l * GROUPS + g + 1)
                    act.activation(xfT[:, :, :], bank[1][:, :].rearrange("p (j t) -> p j t", t=P), ACT.Identity,
                                   bias=vec[:, 1:2], scale=vec[:, 0:1]).then_inc(f_xT, 1)

                def back(g):
                    for j, (c0, cn) in enumerate(FBLK):
                        c = (l * GROUPS + g) * FB + (j + 1)
                        act.wait_ge(f_ab, c)
                        act.activation(gel[0:cn, j % 2, :], bank[3 + 2 * (j % 2)][0:cn, :], ACT.Gelu,
                                       bias=b1g[0:cn, j:j + 1]).then_inc(f_gel, 1)

                act.preload_act_table(ACT.Gelu)
                act.wait_ge(tab_done, l + 1)
                act.wait_ge(y_done, l * B + (2 * B + CREDIT))
                front(0)
                take_T_ff(0)
                with act.Fori(1, GROUPS) as g:
                    act.wait_ge(ln_out, l * GROUPS + g + LN_FF)
                    front(g)
                    back(g - 1)
                    take_T_ff(g)
                back(GROUPS - 1)
                split_wq(l + 1, (l * 3 + 6) * 16)

        @block.tensor
        def _(pe):
            start_with_credit(pe, ["qk_ps", "s_ps", "pT_ps", "v_ps", "o_ps", "y_ps"], ["t_ps"])
            pe.wait_ge(pool_const, 10)
            pe.wait_ge(ld_c, 16 * N_LD_C)
            pe.wait_ge(dve_const, 7)
            with pe.Fori(0, GROUPS) as g:
                pe.wait_ge(ln_out, g * 2 + 1)
                for j in range(G):
                    mm = pe.transpose(bank[0][:, j * P:(j + 1) * P], lnx[:, j, :], ident[:, :])
                mm.then_inc(g_T, 1)
                pe.wait_ge(g_xnT, g + 1)
                for j in range(G):
                    mm = pe.matmul(bank[1 + j][:, 0:3 * D], xnT[:, j, :], wqkv1[:, :], start=True, stop=True)
                mm.then_inc(g_qkv, 1)
                pe.wait_ge(g_qk1, g + 1)
                for j in range(G):
                    mm = pe.transpose(bank[0][:, j * P:(j + 1) * P], qk1[:, j, 0:D], ident[:, :])
                mm.then_inc(g_q1T_ps, 1)
                pe.wait_ge(g_v1, g + 1)
                for j in range(G):
                    c = (j % 2) * 160
                    mm = pe.matmul(bank[5 + j // 2][:, c:c + D + 1], qk1[:, j, D:2 * D], v1[:, j, :],
                                   start=True, stop=True)
                mm.then_inc(g_kv, 1)
                pe.wait_ge(g_kvm, g + 1)
                pe.wait_ge(g_q1T, g + 1)
                for j in range(G):
                    c = (j % 2) * 160
                    mm = pe.matmul(bank[5 + j // 2][:, c:c + D + H], q1T[:, j, :], kvm[:, j, :],
                                   start=True, stop=True)
                mm.then_inc(g_o, 1)
                pe.wait_ge(g_o1, g + 1)
                for j in range(G):
                    mm = pe.transpose(bank[0][:, j * P:(j + 1) * P], o1[:, j, :], ident[:, :])
                mm.then_inc(g_o1T_ps, 1)
                pe.wait_ge(g_o1T, g + 1)
                for j in range(G):
                    mm = pe.matmul(bank[7][:, j * P:(j + 1) * P], o1T[:, j, :], wout1[:, :], start=True, stop=True)
                mm.then_inc(g_y, 1)

            def transpose_x(ph, at, n):
                pe.wait_ge(x_in, n)
                ps = VB[:, 384:512]
                for h, (r, moving) in enumerate(((slice(0, 64), ident), (slice(64, 128), shift if ph.local else ident))):
                    mm = pe.matmul(ps[r, :], xin[:, at.bpair, r], moving[:, :], start=True, stop=True)
                mm.then_inc(xT_ps, 1)

            def sims(ph, at):
                pe.wait_ge(qT_done, ph.n(at))
                pe.wait_ge(kT_done if ph.local else kz_done, ph.n(at))
                pe.wait_ge(sub_done, ph.n(at, 2))
                ps, w = SB_[at.pair], 2 * ph.keys
                keys = kz if ph.local else kz2
                if ph.local:
                    pe.matmul(ps[:, :], ident_bf[:, :], mask_bf[:, :, :].rearrange("p h j -> p (h j)"),
                              start=True, stop=False)
                for j in range(2):
                    mm = pe.matmul(ps[:, j * w:(j + 1) * w], qT[:, at.pair, j, :],
                                   keys[:, at.pair, j, :, :].rearrange("p h j -> p (h j)"),
                                   start=not ph.local, stop=not ph.local or j == 1)
                mm.then_inc(s_ps, 1)

            def transpose_p(ph, at):
                pe.wait_ge(pr_done, ph.n(at))
                pe.wait_ge(pT_done, ph.n(at, 1))
                for h in range(HQ):
                    mm = pe.transpose(PTB[0:ph.keys, h * P:(h + 1) * P], pr[:, at.pair, h, 0:ph.keys], ident[:, :])
                mm.then_inc(pT_ps, 1)

            def weighted_v(ph, at):
                pe.wait_ge(pT_done, ph.n(at))
                pe.wait_ge(v_done, ph.n(at))
                pe.wait_ge(oT_done, ph.n(at, 1))
                val = vs if ph.local else vs2
                for h in range(HQ):
                    r = slice((h % 2) * DH, (h % 2 + 1) * DH)
                    mm = pe.matmul(OB[r, (h // 2) * P:(h // 2 + 1) * P], val[:, at.pair, h * DH:(h + 1) * DH],
                                   pT[0:ph.keys, at.pair, h, :], start=True, stop=True)
                mm.then_inc(o_ps, 1)

            def project_o(ph, at):
                pe.wait_ge(oT_done, ph.n(at))
                w = wo if ph.local else wout2
                for j in range(INNER // P):
                    mm = pe.matmul(VB[:, 256:384], oT[:, at.bpair, j, :], w[:, j, :],
                                   start=(j == 0), stop=(j == INNER // P - 1))
                mm.then_inc(y_ps, 1)

            def context_T(at, n):
                pe.wait_ge(ld_ctx[at.bpair], at.two * 16 + 16)
                pe.wait_ge(xT_done, n - 1) if not isinstance(n, int) or n > 1 else None
                for c in range(CK):
                    mm = pe.transpose(TB_[:, c * M:(c + 1) * M], cst[:, at.bpair, c * P:(c + 1) * P], ident[0:M, 0:M])
                mm.then_inc(c_ps, 1)

            def project2(ph, at):
                pe.wait_ge(qT_done, ph.n(at, 2))
                pe.wait_ge(kz_done, ph.n(at, 2))
                ps = QKB[at.pair]
                for j in range(2):
                    c = (2 * at.q + j) * P
                    pe.matmul(ps[:, j * P:(j + 1) * P], wq2[:, c:c + P], xTf[:, at.bpair, :], start=True, stop=True)
                for j in range(2):
                    c = (2 * at.q + j) * P
                    for ck in range(CK):
                        mm = pe.matmul(ps[:, 256 + j * M:256 + (j + 1) * M], wkv2[:, ck, c:c + P],
                                       ctxT[:, at.bpair, ck, :], start=(ck == 0), stop=(ck == CK - 1))
                mm.then_inc(qk_ps, 1)

            def values2(ph, at):
                pe.wait_ge(v_done, ph.n(at, 1))
                for ck in range(CK):
                    mm = pe.matmul(VB[0:M, 0:QW], ctxT[:, at.bpair, ck, :],
                                   wkv2[:, ck, INNER + at.q * QW:INNER + (at.q + 1) * QW],
                                   start=(ck == 0), stop=(ck == CK - 1))
                mm.then_inc(v_ps, 1)

            def free_vb(ph, at):
                if at.q == 0:
                    pe.wait_ge(y_done, ph.nb(at, 1))

            def body2(i, k, live):
                ph = phase2()
                if live(4) and At(i, k - 4).q == 3:
                    at = At(i, k - 4)
                    pe.wait_ge(v_done, ph.n(at))
                    project_o(ph, at)
                if live(0):
                    at = At(i, k)
                    if at.q == 0:
                        pe.wait_ge(xT_done, at.batch + 1)
                    project2(ph, at)
                if live(3):
                    transpose_p(ph, At(i, k - 3))
                if live(0) and k % QUARTERS == 3:
                    nxt = At(i, k + 1)
                    pe.wait_ge(v_done, ph.n(At(i, k), 4))
                    pe.wait_ge(y_done, ph.nb(At(i, k), 1))
                    transpose_x(ph, nxt, nxt.batch + 1)
                    context_T(nxt, nxt.batch + 1)
                if live(3):
                    at = At(i, k - 3)
                    free_vb(ph, at)
                    if live(0) and k % QUARTERS == 3:
                        pe.wait_ge(xT_done, At(i, k + 1).batch + 1)
                    values2(ph, at)
                    weighted_v(ph, at)
                if live(1):
                    sims(ph, At(i, k - 1))

            pe.wait_ge(g_z, GROUPS)
            transpose_x(phase2(), At(0, 0), 1)
            context_T(At(0, 0), 1)
            quarter_steps(pe, body2, 4)

            with pe.Fori(0, LAYERS) as l:
                ph = phase3(l)

                def three(ps, xh, xl, whi, wlo, last=True):
                    pe.matmul(ps, xh, whi, start=True, stop=False)
                    pe.matmul(ps, xh, wlo, start=False, stop=False)
                    return pe.matmul(ps, xl, whi, start=False, stop=True)

                def project_qk(at):
                    pe.wait_ge(sq_done, ph.n(at, 2))
                    pe.wait_ge(rot_done, ph.n(at, 2))
                    three(QKB[at.pair][:, :], xTh[:, at.bpair, :], xTl[:, at.bpair, :],
                          wh[:, at.q, 0:2 * QW], wl[:, at.q, 0:2 * QW]).then_inc(qk_ps, 1)

                def project_v(at):
                    pe.wait_ge(v_done, ph.n(at, 1))
                    three(VB[:, 0:QW], xTh[:, at.bpair, :], xTl[:, at.bpair, :],
                          wh[:, at.q, 2 * QW:3 * QW], wl[:, at.q, 2 * QW:3 * QW]).then_inc(v_ps, 1)

                def transpose_qk(at):
                    pe.wait_ge(qks_done, ph.n(at))
                    pe.wait_ge(qT_done, ph.n(at, 1))
                    pe.wait_ge(kT_done, ph.n(at, 1))
                    for j in range(4):
                        mm = pe.transpose(TB_[:, j * P:(j + 1) * P], qks[:, at.pair, j * P:(j + 1) * P], ident[:, :])
                    mm.then_inc(t_ps, 1)

                def body(i, k, live):
                    if live(4) and At(i, k - 4).q == 3:
                        at = At(i, k - 4)
                        pe.wait_ge(v_done, ph.n(at))
                        project_o(ph, at)
                    if live(0):
                        at = At(i, k)
                        if at.q == 0:
                            pe.wait_ge(xT_done, at.batch + (ph.xb + 1))
                        project_qk(at)
                    if live(3):
                        transpose_p(ph, At(i, k - 3))
                    if live(0) and k % QUARTERS == 3:
                        nxt = At(i, k + 1)
                        pe.wait_ge(v_done, ph.n(At(i, k), 4))
                        pe.wait_ge(y_done, ph.nb(At(i, k), 1))
                        transpose_x(ph, nxt, nxt.batch + (ph.xb + 1))
                    if live(1):
                        transpose_qk(At(i, k - 1))
                    if live(3):
                        at = At(i, k - 3)
                        free_vb(ph, at)
                        if live(0) and k % QUARTERS == 3:
                            pe.wait_ge(xT_done, At(i, k + 1).batch + (ph.xb + 1))
                        project_v(at)
                        weighted_v(ph, at)
                    if live(1):
                        sims(ph, At(i, k - 1))

                pe.wait_ge(f_x, l * GROUPS + 1)
                pe.wait_ge(wq_split, l + 1)
                pe.wait_ge(ld_wo, l * 16 + 16)
                transpose_x(ph, At(0, 0), ph.xb + 1)
                quarter_steps(pe, body, 4)

                def shifted(g):
                    pe.wait_ge(f_z, l * GROUPS + g + 1)
                    pe.matmul(bank[0][:, 0:G * 64].rearrange("p (j d) -> p j d", d=64), shift[:, :],
                              x[:, bass.ds(g * G, G), 64:128], start=True, stop=True).then_inc(f_shift, 1)

                def front_T(g):
                    pe.wait_ge(ln_out, l * GROUPS + g + (LN_FF + 1))
                    pe.wait_ge(f_xT, l * GROUPS + g + 1)
                    for j in range(G):
                        mm = pe.transpose(bank[1][:, j * P:(j + 1) * P], lnx[:, j, :], ident[:, :])
                    mm.then_inc(f_T, 1)

                def hidden(g):
                    pe.wait_ge(f_split, l * GROUPS + g + 1)
                    for j, (c0, cn) in enumerate(FBLK):
                        if j == 2:
                            pe.wait_ge(f_h, (l * GROUPS + g) * FB + 1)
                        for a in range(2):
                            c = a * FF + c0
                            mm = three(bank[2 + 2 * (j % 2) + a][0:cn, :], w1h[:, c:c + cn], w1l[:, c:c + cn],
                                       xfTh[:, :, :].rearrange("p j t -> p (j t)"),
                                       xfTl[:, :, :].rearrange("p j t -> p (j t)"))
                        mm.then_inc(f_ab, 1)

                def down(g):
                    pe.wait_ge(f_h, (l * GROUPS + g) * FB + FB)
                    for b in range(G):
                        for j, (c0, cn) in enumerate(FBLK):
                            mm = pe.matmul(bank[6][:, b * P:(b + 1) * P], hT[0:cn, j, b * P:(b + 1) * P],
                                           w2[0:cn, j, :], start=(j == 0), stop=(j == FB - 1))
                    mm.then_inc(f_y, 1)

                pe.wait_ge(y_done, l * B + (2 * B + CREDIT))
                pe.wait_ge(w1_split, l + 1)
                pe.wait_ge(ld_w2, l * 32 + 32)
                shifted(0)
                front_T(0)
                with pe.Fori(1, GROUPS) as g:
                    shifted(g)
                    hidden(g - 1)
                    front_T(g)
                    pe.wait_ge(f_x, l * GROUPS + g)
                    down(g - 1)
                hidden(GROUPS - 1)
                pe.wait_ge(f_x, l * GROUPS + GROUPS)
                down(GROUPS - 1)


N_LD_C = 13 + 2 * HQ
N_LD_TAB = 4
NVEC = 2 + 2 * FB
LN_POST2 = 2 * GROUPS
LN_FF = 4 * GROUPS
LN_FINAL = LN_FF + LAYERS * GROUPS

INPUTS = ["x", "ctx_2048", "L0_attn_gamma", "L0_attn_beta", "L0_attn_Wqkv", "L0_attn_Wout", "L0_xattn_Wq",
          "L0_xattn_Wkv", "L0_xattn_null_kv", "L0_xattn_Wout", "L0_xattn_ln_scale", "L0_xattn_ln_bias",
          "L0_ffn_Wqkv", "L0_ffn_Wo", "L0_ffn_W1", "L0_ffn_W2", "L0_ffn_b2"]


def laid_out(inputs):
    scales = np.stack([inputs["L0_ffn_q_scale"], inputs["L0_ffn_k_scale"]], 1).reshape(LAYERS, 2 * DH)
    b1 = np.zeros((LAYERS, 2, FB * P), inputs["L0_ffn_b1"].dtype)
    b1[:, :, :FF] = np.asarray(inputs["L0_ffn_b1"]).reshape(LAYERS, 2, FF)
    rows = [np.asarray(inputs["L0_ffn_ln_g"])[:, None], np.asarray(inputs["L0_ffn_ln_b"])[:, None],
            b1.reshape(LAYERS, 2 * FB, P)]
    named = {"qk_scales": scales, "vectors": np.concatenate(rows, 1).transpose(2, 0, 1)}
    return {name: np.ascontiguousarray(a) for name, a in named.items()}


def shape_constants():
    f = np.float32
    rows = np.arange(P) // HD
    blockmask = (rows[:, None] == rows[None, :]).astype(f)
    headmask = (rows[:, None] == np.arange(H)[None, :]).astype(f)
    half = np.arange(0, DH, 2, dtype=f)
    inv_freq = (f(1.0) / f(10000.0) ** (half / f(DH))).astype(f)
    pos = np.arange(P, dtype=f)
    freqs = pos[:, None] * inv_freq[None, :]
    freqs = np.concatenate([freqs, freqs], -1)
    base = (half + f(0.4 * DH)) / f(1.4 * DH)
    scale = base[None, :] ** ((pos - P // 2) / (WINDOW // 2))[:, None]
    scale = np.concatenate([scale, scale], -1).astype(f)
    sign = np.where(np.arange(DH) < DH // 2, f(-1), f(1))[None, :]
    rot = np.empty((P, 2, 2, DH), f)
    qk_scale = f(8.0)
    rot[:, 0, 0] = np.cos(freqs) * scale * qk_scale
    rot[:, 0, 1] = np.cos(freqs) / scale
    rot[:, 1, 0] = sign * np.sin(freqs) * scale * qk_scale
    rot[:, 1, 1] = sign * np.sin(freqs) / scale
    return {"c_blockmask": blockmask, "c_headmask": headmask, "c_rot": rot}


def kernel(**inputs):
    import concourse.bacc as bacc
    from concourse.bass_utils import run_bass_kernel_spmd

    nc = bacc.Bacc("TRN2", target_bir_lowering=False, num_devices=1)
    arrays = {name: np.ascontiguousarray(inputs[name]) for name in INPUTS}
    arrays = arrays | laid_out(inputs) | shape_constants()
    feeds, t = {}, {}
    for name, a in arrays.items():
        feeds[f"in_{name}"] = a
        t[name] = nc.dram_tensor(f"in_{name}", a.shape, mybir.dt.from_np(a.dtype), kind="ExternalInput").ap()
    out = nc.dram_tensor("out_y", (B, P, D), F32, kind="ExternalOutput").ap()
    build(nc, t, out)
    r = run_bass_kernel_spmd(nc, [feeds], core_ids=[0])
    return r.results[0]["out_y"]
```

```python
from contextlib import ExitStack

import numpy as np

import concourse.bass as bass
from concourse import mybir

F32 = mybir.dt.float32
F32R = mybir.dt.float32r
BF16 = mybir.dt.bfloat16
ALU = mybir.AluOpType
ACT = mybir.ActivationFunctionType
AX = mybir.AxisListType

P = 128
B = 16
D = 128
H = 16
DH = 64
INNER = H * DH
CTX = 256
CK = CTX // P
M = 77
NULLK = M + 1
HD = D // H
LAYERS = 6
FF = 341
FB = 3
WINDOW = 32
HQ = 4
QUARTERS = H // HQ
QW = HQ * DH
G = 4
GROUPS = B // G
PER = 2 * QUARTERS
OUTER = B // 2
STEPS = B * QUARTERS
CREDIT = 8
MASKED = -1e30
FBLK = [(j * P, min(P, FF - j * P)) for j in range(FB)]


class At:

    def __init__(self, i, k):
        self.s = i * PER + k
        self.batch = i * 2 + k // QUARTERS
        self.two = i + k // PER
        self.q = k % QUARTERS
        self.pair = k % 2
        self.bpair = (k // QUARTERS) % 2


def quarter_steps(eng, body, tail):
    for k in range(PER):
        body(0, k, lambda lag: k - lag >= 0)
    with eng.Fori(1, OUTER) as i:
        for k in range(PER):
            body(i, k, lambda lag: True)
    for k in range(tail):
        body(OUTER, k, lambda lag: k - lag < 0)


def build(nc, t, out):
    ctx = ExitStack()
    with ctx:
        def sb(name, shape, dt=F32):
            return ctx.enter_context(nc.sbuf_tensor(name, shape, dt))

        def sem(name):
            return ctx.enter_context(nc.semaphore(name))

        x = sb("x", [P, B + 1, D])
        ident = sb("ident", [P, P])
        shift = sb("shift", [P, P])
        ident_bf = sb("ident_bf", [P, P], BF16)
        mask_bf = sb("mask_bf", [P, HQ, P], BF16)
        half = sb("half", [P, G])
        lnstat = sb("lnstat", [P, G, 6])
        lnmv = sb("lnmv", [P, G, 2])
        lnseen = sb("lnseen", [P, 1])
        lnvar = sb("lnvar", [P, G])
        lnrs = sb("lnrs", [P, G])
        lnz = sb("lnz", [P, G, D])
        lnx = sb("lnx", [P, G, D])
        gam = sb("gam", [P, 1])
        bet = sb("bet", [P, 1])
        wqkv1 = sb("wqkv1", [P, 3 * D])
        wout1 = sb("wout1", [P, D])
        blockmask = sb("blockmask", [P, P])
        headmask = sb("headmask", [P, H])
        xnT = sb("xnT", [P, G, P])
        qk1 = sb("qk1", [P, G, 2 * D])
        neg = sb("neg", [P, G, 2 * D])
        v1 = sb("v1", [P, G, D + 1])
        kvm = sb("kvm", [P, G, D + H])
        q1T = sb("q1T", [P, G, P])
        den1 = sb("den1", [P, G, H])
        o1 = sb("o1", [P, G, D])
        o1T = sb("o1T", [P, G, P])
        wq2 = sb("wq2", [P, INNER])
        wkv2 = sb("wkv2", [P, CK, 2 * INNER])
        wout2 = sb("wout2", [P, INNER // P, D])
        lns2 = sb("lns2", [P, D])
        lnb2 = sb("lnb2", [P, D])
        cst = sb("cst", [M, 2, CTX])
        ctxT = sb("ctxT", [P, 2, CK, M])
        kz2 = sb("kz2", [P, 2, 2, 2, NULLK])
        vs2 = sb("vs2", [NULLK, 2, QW])
        nullk = sb("nullk", [P, 1])
        ybuf = sb("ybuf", [P, B, D])
        rot_cs = sb("rot_cs", [P, 2, 2, DH])
        qks_all = sb("qks_all", [P, LAYERS, 2, DH])
        rot_tab = sb("rot_tab", [P, 2, 2, DH])
        wst = sb("wst", [P, QUARTERS, 3 * QW])
        wh = sb("wh", [P, QUARTERS, 3 * QW], F32R)
        wl = sb("wl", [P, QUARTERS, 3 * QW], F32R)
        wo = sb("wo", [P, INNER // P, D])
        xin = sb("xin", [P, 2, D])
        xTh = sb("xTh", [P, 2, P], F32R)
        xTl = sb("xTl", [P, 2, P], F32R)
        xTf = sb("xTf", [P, 2, P])
        sq = sb("sq", [P, 2, 2 * QW])
        ta = sb("ta", [P, 2, 2 * QW])
        tb = sb("tb", [P, 2, 2 * QW])
        ssq = sb("ssq", [P, 2, 2 * HQ])
        lnr = sb("lnr", [P, 2, 2 * HQ])
        rn = sb("rn", [P, 2, 2 * HQ])
        lnbias = sb("lnbias", [P, 1])
        qks = sb("qks", [P, 2, 2 * QW])
        qT = sb("qT", [P, 2, 2, P])
        kz = sb("kz", [P, 2, 2, 2, P])
        mx = sb("mx", [P, 2, HQ])
        pr = sb("pr", [P, 2, HQ, P])
        den = sb("den", [P, 2, HQ])
        rden = sb("rden", [P, 2, HQ])
        pT = sb("pT", [P, 2, HQ, P])
        vs = sb("vs", [P, 2, QW])
        oT = sb("oT", [P, 2, INNER // P, P])
        yst = sb("yst", [P, 2, D])
        vec_all = sb("vec_all", [P, LAYERS, NVEC])
        vec = sb("vec", [P, NVEC])
        b1a, b1g = vec[:, 2:2 + FB], vec[:, 2 + FB:2 + 2 * FB]
        b2 = sb("b2", [P, LAYERS, D])
        w1st = sb("w1st", [P, 2 * FF])
        w1h = sb("w1h", [P, 2 * FF], F32R)
        w1l = sb("w1l", [P, 2 * FF], F32R)
        w2 = sb("w2", [P, FB, D])
        xfT = sb("xfT", [P, G, P])
        xfTh = sb("xfTh", [P, G, P], F32R)
        xfTl = sb("xfTl", [P, G, P], F32R)
        gel = sb("gel", [P, 2, G * P])
        hT = sb("hT", [P, FB, G * P])

        bank = [ctx.enter_context(nc.psum_tensor(f"bank{i}", [P, 512], F32)) for i in range(8)]
        QKB, TB_, SB_, PTB, VB, OB = bank[0:2], bank[2], bank[3:5], bank[5], bank[6], bank[7]

        ld_x = sem("ld_x")
        ld_c = sem("ld_c")
        ld_tab = sem("ld_tab")
        ld_ctx = [sem("ld_ctx0"), sem("ld_ctx1")]
        ld_wq = sem("ld_wq")
        ld_w1 = sem("ld_w1")
        ld_wo = sem("ld_wo")
        ld_w2 = sem("ld_w2")
        st_out = sem("st_out")
        pool_const = sem("pool_const")
        dve_const = sem("dve_const")
        ln_stats = sem("ln_stats")
        ln_mv = sem("ln_mv")
        ln_var = sem("ln_var")
        ln_rs = sem("ln_rs")
        ln_out = sem("ln_out")
        g_T = sem("g_T")
        g_xnT = sem("g_xnT")
        g_qkv = sem("g_qkv")
        g_min = sem("g_min")
        g_exp = sem("g_exp")
        g_qk1 = sem("g_qk1")
        g_v1 = sem("g_v1")
        g_kv = sem("g_kv")
        g_kvm = sem("g_kvm")
        g_q1T_ps = sem("g_q1T_ps")
        g_q1T = sem("g_q1T")
        g_o = sem("g_o")
        g_den = sem("g_den")
        g_rden = sem("g_rden")
        g_o1 = sem("g_o1")
        g_o1T_ps = sem("g_o1T_ps")
        g_o1T = sem("g_o1T")
        g_y = sem("g_y")
        g_z = sem("g_z")
        g_x = sem("g_x")
        x_in = sem("x_in")
        xT_ps = sem("xT_ps")
        xT_hi = sem("xT_hi")
        xT_done = sem("xT_done")
        c_ps = sem("c_ps")
        c_done = sem("c_done")
        step_sems = {}

        def step_sem(name):
            step_sems[name] = sem(name)
            return step_sems[name]

        qk_ps = step_sem("qk_ps")
        sq_done = step_sem("sq_done")
        rot_done = step_sem("rot_done")
        ssq_raw = step_sem("ssq_raw")
        ssq_done = step_sem("ssq_done")
        ln_done = step_sem("ln_done")
        rn_done = step_sem("rn_done")
        add_done = step_sem("add_done")
        qks_done = step_sem("qks_done")
        t_ps = step_sem("t_ps")
        qT_done = step_sem("qT_done")
        kT_done = step_sem("kT_done")
        kz_done = step_sem("kz_done")
        s_ps = step_sem("s_ps")
        mx_done = step_sem("mx_done")
        sub_done = step_sem("sub_done")
        exp_done = step_sem("exp_done")
        den_done = step_sem("den_done")
        rden_done = step_sem("rden_done")
        pr_done = step_sem("pr_done")
        pT_ps = step_sem("pT_ps")
        pT_done = step_sem("pT_done")
        v_ps = step_sem("v_ps")
        v_done = step_sem("v_done")
        o_ps = step_sem("o_ps")
        oT_done = step_sem("oT_done")
        y_ps = step_sem("y_ps")
        y_out = step_sem("y_out")
        y_done = step_sem("y_done")
        post2 = sem("post2")
        kept = sem("kept")
        last_z = sem("last_z")
        tab_cos = sem("tab_cos")
        tab_done = sem("tab_done")
        wq_hi = sem("wq_hi")
        wq_split = sem("wq_split")
        w1_hi = sem("w1_hi")
        w1_split = sem("w1_split")
        f_shift = sem("f_shift")
        f_z = sem("f_z")
        f_z0 = sem("f_z0")
        f_b2 = sem("f_b2")
        f_T = sem("f_T")
        f_xT = sem("f_xT")
        f_hi = sem("f_hi")
        f_split = sem("f_split")
        f_ab = sem("f_ab")
        f_gel = sem("f_gel")
        f_h = sem("f_h")
        f_y = sem("f_y")
        f_x = sem("f_x")

        block = ctx.enter_context(nc.Block())

        def start_with_credit(eng, names, local=()):
            for n in names:
                eng.sem_inc(step_sems[n], CREDIT)
            for n in local:
                eng.sem_inc(step_sems[n], CREDIT + STEPS)

        class Phase:

            def __init__(self, local, base, bbase):
                self.local = local
                self.keys = P if local else NULLK
                self.base = base
                self.bbase = bbase
                self.at_sims = 2 if local else 1
                self.at_softmax = self.at_values = self.at_sims + 1
                self.at_out = self.at_sims + 2
                self.at_wo = self.at_sims + 3

            def n(self, at, back=0):
                return at.s + (self.base + (CREDIT + 1 - back))

            def nb(self, at, back=0):
                return at.batch + (self.bbase + (CREDIT + 1 - back))

        def phase2():
            p = Phase(False, 0, 0)
            p.xb = 0
            return p

        def phase3(l):
            p = Phase(True, l * STEPS + STEPS, l * B + B)
            p.xb = l * (B + 1) + (B + 1)
            return p

        @block.sync
        def _(sp):
            xv = t["x"].rearrange("b p d -> p b d")
            for g in range(GROUPS):
                sp.dma_start(x[:, g * G:(g + 1) * G, :], xv[:, g * G:(g + 1) * G, :]).then_inc(ld_x, 16)
            col = lambda a: a.rearrange("(p o) -> p o", o=1)
            row = lambda a: a.rearrange("(o p) -> o p", o=1)
            first = [
                (gam[:, :], col(t["L0_attn_gamma"])), (bet[:, :], col(t["L0_attn_beta"])),
                (wqkv1[:, :], t["L0_attn_Wqkv"]), (wout1[:, :], t["L0_attn_Wout"]),
                (blockmask[:, :], t["c_blockmask"]), (headmask[:, :], t["c_headmask"]),
                (wq2[:, :], t["L0_xattn_Wq"]),
                (wkv2[:, :, :], t["L0_xattn_Wkv"].rearrange("(c p) n -> p c n", p=P)),
                (wout2[:, :, :], t["L0_xattn_Wout"].rearrange("(j p) n -> p j n", p=P)),
                (lns2[:, :], row(t["L0_xattn_ln_scale"]).to_broadcast([P, D])),
                (lnb2[:, :], row(t["L0_xattn_ln_bias"]).to_broadcast([P, D])),
                (nullk[0:DH, :], col(t["L0_xattn_null_kv"][0])),
                (nullk[DH:P, :], col(t["L0_xattn_null_kv"][0])),
            ]
            for dst, src in first:
                sp.dma_start(dst, src).then_inc(ld_c, 16)
            for r in range(2):
                for h in range(HQ):
                    sp.dma_start(vs2[M:M + 1, r, h * DH:(h + 1) * DH],
                                 t["L0_xattn_null_kv"][1:2, :]).then_inc(ld_c, 16)
            assert N_LD_C == len(first) + 2 * HQ

            def load_wq(l):
                for j in range(3):
                    sp.dma_start(wst[:, :, j * QW:(j + 1) * QW],
                                 t["L0_ffn_Wqkv"][l, :, j * INNER:(j + 1) * INNER]
                                 .rearrange("p (q n) -> p q n", q=QUARTERS)).then_inc(ld_wq, 16)

            def load_w1(l):
                sp.dma_start(w1st[:, :], t["L0_ffn_W1"][l]).then_inc(ld_w1, 16)

            def load_wo(l):
                sp.dma_start(wo[:, :, :], t["L0_ffn_Wo"][l].rearrange("(j p) n -> p j n", p=P)).then_inc(ld_wo, 16)

            def load_w2(l):
                sp.dma_start(w2[:, 0:2, :], t["L0_ffn_W2"][l, 0:2 * P, :].rearrange("(j p) n -> p j n", p=P)
                             ).then_inc(ld_w2, 16)
                sp.dma_start(w2[0:FF - 2 * P, 2, :], t["L0_ffn_W2"][l, 2 * P:FF, :]).then_inc(ld_w2, 16)

            def load_ctx(b, slot):
                sp.dma_start(cst[:, slot, :], t["ctx_2048"][b]).then_inc(ld_ctx[slot], 16)

            for b in range(2):
                load_ctx(b, b)
            load_wq(0)
            every = lambda a, n: a.rearrange("l n -> (l n)").rearrange("(o n) -> o n", o=1).to_broadcast([P, n])
            tables = [
                (rot_cs[:, :, :, :], t["c_rot"]), (vec_all[:, :, :], t["vectors"]),
                (qks_all[:, :, :, :].rearrange("p l a d -> p (l a d)"), every(t["qk_scales"], LAYERS * 2 * DH)),
                (b2[:, :, :].rearrange("p l d -> p (l d)"), every(t["L0_ffn_b2"], LAYERS * D)),
            ]
            for dst, src in tables:
                sp.dma_start(dst, src).then_inc(ld_tab, 16)
            assert N_LD_TAB == len(tables)
            load_w1(0)
            load_wo(0)
            load_w2(0)
            with sp.Fori(0, OUTER) as i:
                for b in range(2):
                    sp.wait_ge(c_ps, i * 2 + (b + 1))
                    load_ctx((i * 2 + (b + 2)) % B, b)
            with sp.Fori(0, LAYERS) as l:
                sp.wait_ge(wq_split, l + 1)
                load_wq((l + 1) % LAYERS)
                sp.wait_ge(w1_split, l + 1)
                load_w1((l + 1) % LAYERS)
                sp.wait_ge(y_done, l * B + (2 * B + CREDIT))
                load_wo((l + 1) % LAYERS)
                sp.wait_ge(f_x, l * GROUPS + (GROUPS + 1))
                load_w2((l + 1) % LAYERS)
            ov = out.rearrange("b p d -> p b d")
            for g in range(GROUPS):
                sp.wait_ge(ln_out, LN_FINAL + g + 1)
                sp.dma_start(ov[:, g * G:(g + 1) * G, :], x[:, g * G:(g + 1) * G, :]).then_inc(st_out, 16)
            for b in range(2):
                sp.wait_ge(ld_ctx[b], 16 * (OUTER + 1))
            sp.wait_ge(ld_wq, 16 * 3 * (LAYERS + 1))
            sp.wait_ge(ld_w1, 16 * (LAYERS + 1))
            sp.wait_ge(ld_wo, 16 * (LAYERS + 1))
            sp.wait_ge(ld_w2, 16 * 2 * (LAYERS + 1))
            sp.wait_ge(st_out, 16 * GROUPS)

        @block.gpsimd
        def _(pool):
            pool.memset(ident[:], 0.0).then_inc(pool_const, 1)
            pool.memset(shift[:], 0.0).then_inc(pool_const, 1)
            pool.memset(ident_bf[:], 0.0).then_inc(pool_const, 1)
            pool.memset(mask_bf[:], 0.0).then_inc(pool_const, 1)
            pool.memset(half[:], -0.5).then_inc(pool_const, 1)
            pool.wait_ge(pool_const, 5)
            pool.affine_select(out=ident[:], in_=ident[:], compare_op=ALU.not_equal, fill=1.0, base=0,
                               pattern=[[-1, P]], channel_multiplier=1).then_inc(pool_const, 1)
            pool.affine_select(out=shift[:], in_=shift[:], compare_op=ALU.not_equal, fill=1.0, base=1,
                               pattern=[[-1, P]], channel_multiplier=1).then_inc(pool_const, 1)
            pool.affine_select(out=ident_bf[:], in_=ident_bf[:], compare_op=ALU.not_equal, fill=1.0, base=0,
                               pattern=[[-1, P]], channel_multiplier=1).then_inc(pool_const, 1)
            pool.affine_select(out=mask_bf[:], in_=mask_bf[:], compare_op=ALU.is_ge, fill=MASKED, base=0,
                               pattern=[[0, HQ], [-1, P]], channel_multiplier=1).then_inc(pool_const, 1)
            pool.wait_ge(pool_const, 9)
            pool.affine_select(out=mask_bf[:], in_=mask_bf[:], compare_op=ALU.is_ge, fill=MASKED, base=WINDOW,
                               pattern=[[0, HQ], [1, P]], channel_multiplier=-1).then_inc(pool_const, 1)
            start_with_credit(pool, ["pr_done", "y_done"], ["add_done", "qks_done"])

            def rsqrt_of(count):
                pool.wait_ge(ln_var, count)
                pool.tensor_tensor(lnrs[:, :], lnvar[:, :], half[:, :], ALU.pow).then_inc(ln_rs, 1)

            with pool.Fori(0, 2 * GROUPS) as n:
                rsqrt_of(n + 1)

            def normalise(ph, at):
                pool.wait_ge(rden_done, ph.n(at))
                w = pr[:, at.pair, :, 0:ph.keys]
                pool.tensor_tensor(w, w, rden[:, at.pair, :].unsqueeze(2).to_broadcast([P, HQ, ph.keys]),
                                   ALU.mult).then_inc(pr_done, 1)

            def body2(i, k, live):
                ph = phase2()
                if live(ph.at_out):
                    normalise(ph, At(i, k - ph.at_out))
                if live(ph.at_wo) and At(i, k - ph.at_wo).q == 3:
                    at = At(i, k - ph.at_wo)
                    pool.wait_ge(y_out, ph.nb(at))
                    pool.tensor_copy(ybuf[:, bass.ds(at.batch, 1), :].rearrange("p o d -> p (o d)"),
                                     yst[:, at.bpair, :]).then_inc(y_done, 1)

            quarter_steps(pool, body2, phase2().at_wo)
            with pool.Fori(0, 2 * GROUPS) as n:
                rsqrt_of(n + (LN_POST2 + 1))

            def split_wq(l):
                pool.wait_ge(wq_hi, l + 1)
                pool.tensor_tensor(wl[:, :, :], wst[:, :, :], wh[:, :, :].bitcast(F32), ALU.subtract
                                   ).then_inc(wq_split, 1)

            split_wq(0)
            with pool.Fori(0, LAYERS) as l:
                ph = phase3(l)
                pool.wait_ge(w1_hi, l + 1)
                pool.tensor_tensor(w1l[:, :], w1st[:, :], w1h[:, :].bitcast(F32), ALU.subtract).then_inc(w1_split, 1)

                def add(at):
                    pool.wait_ge(rot_done, ph.n(at))
                    pool.tensor_tensor(ta[:, at.pair, :], ta[:, at.pair, :], tb[:, at.pair, :], ALU.add
                                       ).then_inc(add_done, 1)

                def scale(at):
                    pool.wait_ge(rn_done, ph.n(at))
                    pool.wait_ge(add_done, ph.n(at))
                    pool.wait_ge(t_ps, ph.n(at, 2))
                    pool.tensor_tensor(qks[:, at.pair, :].rearrange("p (h d) -> p h d", d=DH),
                                       ta[:, at.pair, :].rearrange("p (h d) -> p h d", d=DH),
                                       rn[:, at.pair, :].unsqueeze(2).to_broadcast([P, 2 * HQ, DH]),
                                       ALU.mult).then_inc(qks_done, 1)

                def residual(at):
                    pool.wait_ge(y_out, ph.nb(at))
                    xb = x[:, bass.ds(at.batch, 1), :].rearrange("p o d -> p (o d)")
                    pool.tensor_tensor(xb, xb, yst[:, at.bpair, :], ALU.add).then_inc(y_done, 1)

                def xT_low(at, n):
                    pool.wait_ge(xT_hi, n)
                    pool.tensor_tensor(xTl[:, at.bpair, :], xTf[:, at.bpair, :], xTh[:, at.bpair, :].bitcast(F32),
                                       ALU.subtract).then_inc(xT_done, 1)

                def body(i, k, live):
                    if live(ph.at_out):
                        normalise(ph, At(i, k - ph.at_out))
                    if live(1):
                        scale(At(i, k - 1))
                    if live(ph.at_wo) and At(i, k - ph.at_wo).q == 3:
                        residual(At(i, k - ph.at_wo))
                    if live(0):
                        add(At(i, k))
                    if live(0) and k % QUARTERS == 2:
                        nxt = At(i, k + 2)
                        xT_low(nxt, nxt.batch + (ph.xb + 1))

                xT_low(At(0, 0), ph.xb + 1)
                quarter_steps(pool, body, ph.at_wo)
                with pool.Fori(0, GROUPS) as g:
                    rsqrt_of(l * GROUPS + g + (LN_FF + 1))
                    pool.wait_ge(f_z, l * GROUPS + g + 2)
                    pool.wait_ge(f_z0, l * GROUPS + g + 1)
                    pool.tensor_tensor(x[:, bass.ds(g * G, G), :], x[:, bass.ds(g * G, G), :],
                                       b2[:, bass.ds(l, 1), :].to_broadcast([P, G, D]), ALU.add).then_inc(f_b2, 1)
                split_wq(l + 1)
            with pool.Fori(0, GROUPS) as n:
                rsqrt_of(n + (LN_FINAL + 1))

        @block.vector
        def _(dve):
            dve.memset(v1[:, :, D:D + 1], 1.0).then_inc(dve_const, 1)
            dve.memset(kz[:], 0.0).then_inc(dve_const, 1)
            dve.memset(kz2[:], 0.0).then_inc(dve_const, 1)
            dve.memset(x[:, B:B + 1, :], 0.0).then_inc(dve_const, 1)
            dve.memset(lnbias[:], float(np.log(2.0 ** 8))).then_inc(dve_const, 1)
            start_with_credit(dve, ["kz_done", "mx_done", "sub_done", "den_done", "rden_done"],
                              ["rot_done", "ssq_raw", "ssq_done"])
            dve.sem_inc(f_z, 1)
            dve.sem_inc(f_x, 1)
            dve.wait_ge(ld_c, 16 * N_LD_C)
            dve.wait_ge(dve_const, 5)
            for h in range(2):
                dve.tensor_copy(kz2[h * DH:(h + 1) * DH, :, :, h, M:NULLK].rearrange("p a b o -> p (a b) o"),
                                nullk[h * DH:(h + 1) * DH, :].unsqueeze(1).to_broadcast([DH, 4, 1])
                                ).then_inc(dve_const, 1)

            def norm(count, src, dst, eps, n=None):
                for j in range(G):
                    ins = dve.bn_stats(lnstat[:, j, :], src(j))
                ins.then_inc(ln_stats, 1)
                dve.wait_ge(ln_stats, count)
                dve.tensor_copy(lnseen[:, :], lnstat[:, 0, 0:1])
                for j in range(G):
                    ins = dve.bn_aggr(lnmv[:, j, :], lnstat[:, j, :])
                ins.then_inc(ln_mv, 1)
                dve.wait_ge(ln_mv, count)
                dve.tensor_scalar(lnvar[:, :].unsqueeze(2), lnmv[:, :, 1:2], eps, None, ALU.add
                                  ).then_inc(ln_var, 1)
                dve.wait_ge(ln_rs, count)
                for j in range(G):
                    ins = dve.tensor_scalar(dst(j), src(j), lnmv[:, j, 0:1], lnrs[:, j:j + 1],
                                            ALU.subtract, ALU.mult)
                ins.then_inc(ln_out, 1)

            def xg(g):
                return lambda j: x[:, bass.ds(g * G + j, 1), :].rearrange("p o d -> p (o d)")

            zg = lambda j: lnz[:, j, :]
            ng = lambda j: lnx[:, j, :]

            dve.wait_ge(ld_x, 16 * GROUPS)
            with dve.Fori(0, GROUPS) as g:
                norm(g * 2 + 1, xg(g), ng, 1e-5)
                dve.wait_ge(g_qkv, g + 1)
                for j in range(G):
                    ins = dve.tensor_scalar(neg[:, j, :], bank[1 + j][:, 0:2 * D], 0.0, None, ALU.min)
                ins.then_inc(g_min, 1)
                dve.wait_ge(g_exp, g + 1)
                for j in range(G):
                    ins = dve.scalar_tensor_tensor(qk1[:, j, :], bank[1 + j][:, 0:2 * D], 0.0, neg[:, j, :],
                                                   ALU.max, ALU.add)
                ins.then_inc(g_qk1, 1)
                dve.wait_ge(g_kv, g + 1)
                for j in range(G):
                    kv = bank[5 + j // 2][:, (j % 2) * 160:(j % 2) * 160 + D + 1]
                    dve.tensor_tensor(kvm[:, j, 0:D], kv[:, 0:D], blockmask[:, :], ALU.mult)
                    ins = dve.tensor_scalar(kvm[:, j, D:D + H], headmask[:, :], kv[:, D:D + 1], None, ALU.mult)
                ins.then_inc(g_kvm, 1)
                dve.wait_ge(g_o, g + 1)
                for j in range(G):
                    o = bank[5 + j // 2][:, (j % 2) * 160:(j % 2) * 160 + D + H]
                    ins = dve.tensor_scalar(den1[:, j, :], o[:, D:D + H], 1e-6, None, ALU.add)
                ins.then_inc(g_den, 1)
                dve.wait_ge(g_den, g + 1)
                dve.reciprocal(den1[:, :, :], den1[:, :, :]).then_inc(g_rden, 1)
                dve.wait_ge(g_rden, g + 1)
                for j in range(G):
                    o = bank[5 + j // 2][:, (j % 2) * 160:(j % 2) * 160 + D]
                    ins = dve.tensor_tensor(o1[:, j, :].rearrange("p (h e) -> p h e", e=HD),
                                            o.rearrange("p (h e) -> p h e", e=HD),
                                            den1[:, j, :].unsqueeze(2).to_broadcast([P, H, HD]), ALU.mult)
                ins.then_inc(g_o1, 1)
                dve.wait_ge(g_y, g + 1)
                dve.scalar_tensor_tensor(lnz[:, :, :], x[:, bass.ds(g * G, G), :], 2.0,
                                         bank[7][:, :].rearrange("p (j d) -> p j d", d=D),
                                         ALU.mult, ALU.add).then_inc(g_z, 1)
                dve.wait_ge(g_z, g + 1)
                norm(g * 2 + 2, zg, xg(g), 1e-5)

            def row_max(ph, at):
                dve.wait_ge(s_ps, ph.n(at))
                sim = SB_[at.pair][:, 0:HQ * ph.keys].rearrange("p (h j) -> p h j", j=ph.keys)
                dve.tensor_reduce(mx[:, at.pair, :], sim, AX.X, ALU.max).then_inc(mx_done, 1)
                dve.wait_ge(mx_done, ph.n(at))
                dve.wait_ge(pT_ps, ph.n(at, 2))
                dve.tensor_tensor(pr[:, at.pair, :, 0:ph.keys], sim,
                                  mx[:, at.pair, :].unsqueeze(2).to_broadcast([P, HQ, ph.keys]),
                                  ALU.subtract).then_inc(sub_done, 1)

            def row_sum(ph, at):
                dve.wait_ge(exp_done, ph.n(at))
                dve.tensor_reduce(den[:, at.pair, :], pr[:, at.pair, :, 0:ph.keys], AX.X, ALU.add
                                  ).then_inc(den_done, 1)
                dve.wait_ge(den_done, ph.n(at))
                dve.wait_ge(pr_done, ph.n(at, 2))
                dve.reciprocal(rden[:, at.pair, :], den[:, at.pair, :]).then_inc(rden_done, 1)

            def body2(i, k, live):
                ph = phase2()
                if live(ph.at_softmax):
                    row_max(ph, At(i, k - ph.at_softmax))
                if live(0):
                    at = At(i, k)
                    dve.wait_ge(qk_ps, ph.n(at))
                    dve.wait_ge(s_ps, ph.n(at, 2))
                    kps = QKB[at.pair][:, 256:256 + 2 * M].rearrange("p (b m) -> p b m", m=M)
                    for h in range(2):
                        r = slice(h * DH, (h + 1) * DH)
                        ins = dve.tensor_copy(kz2[r, at.pair, :, h, 0:M], kps[r, :, :])
                    ins.then_inc(kz_done, 1)
                if live(ph.at_softmax):
                    row_sum(ph, At(i, k - ph.at_softmax))

            dve.wait_ge(dve_const, 7)
            quarter_steps(dve, body2, phase2().at_softmax)
            dve.wait_ge(y_done, CREDIT + B)

            with dve.Fori(0, GROUPS) as g:
                norm(g * 2 + (LN_POST2 + 1), lambda j: ybuf[:, bass.ds(g * G + j, 1), :].rearrange("p o d -> p (o d)"),
                     ng, 1e-6)
                dve.wait_ge(ln_out, g * 2 + (LN_POST2 + 1))
                dve.tensor_tensor(lnx[:, :, :], lnx[:, :, :], lns2[:, :].unsqueeze(1).to_broadcast([P, G, D]),
                                  ALU.mult).then_inc(post2, 1)
                dve.wait_ge(post2, g * 3 + 1)
                dve.tensor_tensor(lnz[:, :, :], lnx[:, :, :], lnb2[:, :].unsqueeze(1).to_broadcast([P, G, D]),
                                  ALU.add).then_inc(post2, 1)
                dve.wait_ge(post2, g * 3 + 2)
                dve.tensor_tensor(lnz[:, :, :], lnz[:, :, :], x[:, bass.ds(g * G, G), :], ALU.add
                                  ).then_inc(post2, 1)
                dve.wait_ge(post2, g * 3 + 3)
                norm(g * 2 + (LN_POST2 + 2), zg, xg(g), 1e-5)

            dve.wait_ge(ld_tab, 16 * N_LD_TAB)
            with dve.Fori(0, LAYERS) as l:
                ph = phase3(l)
                dve.wait_ge(f_x, l * GROUPS + 1)
                sc = qks_all[:, bass.ds(l, 1), :, :].rearrange("p o a d -> p (o a) d")
                dve.tensor_copy(vec[:, :].unsqueeze(1), vec_all[:, bass.ds(l, 1), :])
                dve.tensor_tensor(rot_tab[:, 0, :, :], rot_cs[:, 0, :, :], sc, ALU.mult)
                dve.tensor_tensor(rot_tab[:, 1, :, 0:32], rot_cs[:, 1, :, 0:32], sc[:, :, 32:64], ALU.mult)
                dve.tensor_tensor(rot_tab[:, 1, :, 32:64], rot_cs[:, 1, :, 32:64], sc[:, :, 0:32], ALU.mult
                                  ).then_inc(tab_done, 1)
                dve.wait_ge(tab_done, l + 1)

                def rotate(at):
                    dve.wait_ge(sq_done, ph.n(at))
                    dve.wait_ge(qks_done, ph.n(at, 2))
                    src = QKB[at.pair][:, :].rearrange("p (a h d) -> p a h d", a=2, d=DH)
                    cosp = ta[:, at.pair, :].rearrange("p (a h d) -> p a h d", a=2, d=DH)
                    sinp = tb[:, at.pair, :].rearrange("p (a h d) -> p a h d", a=2, d=DH)
                    dve.tensor_tensor(cosp, src,
                                      rot_tab[:, 0, :, :].unsqueeze(2).to_broadcast([P, 2, HQ, DH]), ALU.mult)
                    for lo, hi in ((0, 32), (32, 0)):
                        ins = dve.tensor_tensor(
                            sinp[:, :, :, lo:lo + 32], src[:, :, :, hi:hi + 32],
                            rot_tab[:, 1, :, lo:lo + 32].unsqueeze(2).to_broadcast([P, 2, HQ, 32]), ALU.mult)
                    ins.then_inc(rot_done, 1)

                def norms(at):
                    dve.wait_ge(sq_done, ph.n(at))
                    dve.tensor_reduce(ssq[:, at.pair, :], sq[:, at.pair, :].rearrange("p (h d) -> p h d", d=DH),
                                      AX.X, ALU.add).then_inc(ssq_raw, 1)
                    dve.wait_ge(ssq_raw, ph.n(at))
                    dve.tensor_scalar(ssq[:, at.pair, :], ssq[:, at.pair, :], 1e-24, None, ALU.max
                                      ).then_inc(ssq_done, 1)

                def body(i, k, live):
                    if live(ph.at_softmax):
                        row_max(ph, At(i, k - ph.at_softmax))
                    if live(0):
                        rotate(At(i, k))
                        norms(At(i, k))
                    if live(ph.at_softmax):
                        row_sum(ph, At(i, k - ph.at_softmax))

                quarter_steps(dve, body, ph.at_softmax)

                def front(g):
                    c = l * GROUPS + g + 1
                    dve.wait_ge(f_shift, c)
                    dve.tensor_copy(lnz[:, :, 64:128], bank[0][:, 0:G * 64].rearrange("p (j d) -> p j d", d=64)
                                    ).then_inc(f_z, 1)
                    dve.wait_ge(f_z, c + 1)
                    dve.wait_ge(f_z0, c)
                    norm(l * GROUPS + g + (LN_FF + 1), zg, ng, 1e-5)

                def split(g):
                    c = l * GROUPS + g + 1
                    dve.wait_ge(f_xT, c + 1)
                    dve.tensor_copy(xfTh[:, :, :], xfT[:, :, :]).then_inc(f_hi, 1)
                    dve.wait_ge(f_hi, c)
                    dve.tensor_tensor(xfTl[:, :, :], xfT[:, :, :], xfTh[:, :, :].bitcast(F32), ALU.subtract
                                      ).then_inc(f_split, 1)

                def back(g):
                    for j, (c0, cn) in enumerate(FBLK):
                        dve.wait_ge(f_gel, (l * GROUPS + g) * FB + (j + 1))
                        dve.scalar_tensor_tensor(hT[0:cn, j, :], bank[2 + 2 * (j % 2)][0:cn, :],
                                                 b1a[0:cn, j:j + 1], gel[0:cn, j % 2, :],
                                                 ALU.add, ALU.mult).then_inc(f_h, 1)
                    dve.wait_ge(f_y, l * GROUPS + g + 1)
                    dve.wait_ge(f_b2, l * GROUPS + g + 1)
                    xs = x[:, bass.ds(g * G, G), :]
                    dve.tensor_tensor(xs, xs, bank[6][:, :].rearrange("p (j d) -> p j d", d=D), ALU.add
                                      ).then_inc(f_x, 1)

                front(0)
                split(0)
                with dve.Fori(1, GROUPS) as g:
                    front(g)
                    back(g - 1)
                    split(g)
                back(GROUPS - 1)

            dve.wait_ge(kept, GROUPS)
            with dve.Fori(0, GROUPS) as g:
                xs = x[:, bass.ds(g * G, G), :]
                dve.wait_ge(ln_out, g + LN_FINAL)
                dve.tensor_tensor(lnz[:, :, :], xs, ybuf[:, bass.ds(g * G, G), :], ALU.add).then_inc(last_z, 1)
                dve.wait_ge(last_z, g + 1)
                norm(g + (LN_FINAL + 1), zg, xg(g), 1e-5)

        @block.scalar
        def _(act):
            start_with_credit(act, ["y_out", "qT_done", "exp_done", "pT_done", "v_done", "oT_done"],
                              ["sq_done", "ln_done", "rn_done", "kT_done"])
            act.sem_inc(f_xT, 1)
            act.wait_ge(ld_c, 16 * N_LD_C)
            with act.Fori(0, GROUPS) as g:
                act.wait_ge(g_T, g + 1)
                act.activation(xnT[:, :, :], bank[0][:, :].rearrange("p (j t) -> p j t", t=P), ACT.Identity,
                               bias=bet[:, 0:1], scale=gam[:, 0:1]).then_inc(g_xnT, 1)
                act.wait_ge(g_min, g + 1)
                act.activation(neg[:, :, :], neg[:, :, :], ACT.Exp).then_inc(g_exp, 1)
                act.wait_ge(dve_const, 7)
                act.wait_ge(g_qk1, g + 1)
                for j in range(G):
                    ins = act.activation(v1[:, j, 0:D], bank[1 + j][:, 2 * D:3 * D], ACT.Copy)
                ins.then_inc(g_v1, 1)
                act.wait_ge(g_q1T_ps, g + 1)
                act.activation(q1T[:, :, :], bank[0][:, :].rearrange("p (j t) -> p j t", t=P), ACT.Copy
                               ).then_inc(g_q1T, 1)
                act.wait_ge(g_o1T_ps, g + 1)
                act.activation(o1T[:, :, :], bank[0][:, :].rearrange("p (j t) -> p j t", t=P), ACT.Copy
                               ).then_inc(g_o1T, 1)

            def take_x(ph, at, n):
                act.wait_ge(xT_ps, n - 2) if not isinstance(n, int) or n > 2 else None
                act.activation(xin[:, at.bpair, :], x[:, bass.ds(at.batch, 1), :].rearrange("p o d -> p (o d)"),
                               ACT.Copy).then_inc(x_in, 1)

            def exps(ph, at):
                act.wait_ge(sub_done, ph.n(at))
                w = pr[:, at.pair, :, 0:ph.keys]
                act.activation(w, w, ACT.Exp).then_inc(exp_done, 1)

            def take_pT(ph, at):
                act.wait_ge(pT_ps, ph.n(at))
                act.wait_ge(o_ps, ph.n(at, 2))
                act.activation(pT[0:ph.keys, at.pair, :, :],
                               PTB[0:ph.keys, :].rearrange("p (h t) -> p h t", t=P), ACT.Copy
                               ).then_inc(pT_done, 1)

            def take_v(ph, at):
                act.wait_ge(v_ps, ph.n(at))
                act.wait_ge(o_ps, ph.n(at, 2))
                if ph.local:
                    dst, rows = vs[:, at.pair, :], P
                else:
                    dst, rows = vs2[0:M, at.pair, :], M
                act.activation(dst, VB[0:rows, 0:QW], ACT.Copy).then_inc(v_done, 1)

            def take_o(ph, at):
                act.wait_ge(o_ps, ph.n(at))
                act.wait_ge(y_ps, ph.nb(at, 2))
                act.activation(oT[:, at.bpair, 2 * at.q:2 * at.q + 2, :],
                               OB[:, 0:2 * P].rearrange("p (j t) -> p j t", t=P), ACT.Copy
                               ).then_inc(oT_done, 1)

            def take_y(ph, at):
                act.wait_ge(y_ps, ph.nb(at))
                act.wait_ge(y_done, ph.nb(at, 2))
                act.activation(yst[:, at.bpair, :], VB[:, 256:384], ACT.Copy).then_inc(y_out, 1)

            def take_xT(ph, at, n):
                act.wait_ge(xT_ps, n)
                act.wait_ge(v_ps, ph.n(at, 5))
                ins = act.activation(xTf[:, at.bpair, :], VB[:, 384:512], ACT.Copy)
                if ph.local:
                    act.activation(xTh[:, at.bpair, :], VB[:, 384:512], ACT.Copy).then_inc(xT_hi, 1)
                else:
                    ins.then_inc(xT_hi, 1)
                    act.wait_ge(c_ps, n)
                    act.activation(ctxT[:, at.bpair, :, :],
                                   TB_[:, 0:CK * M].rearrange("p (c m) -> p c m", m=M), ACT.Copy
                                   ).then_inc(xT_done, 1)

            def body2(i, k, live):
                ph = phase2()
                if live(0):
                    at = At(i, k)
                    act.wait_ge(qk_ps, ph.n(at))
                    act.wait_ge(kz_done, ph.n(at))
                    act.wait_ge(s_ps, ph.n(at, 2))
                    act.activation(qT[:, at.pair, :, :],
                                   QKB[at.pair][:, 0:2 * P].rearrange("p (j t) -> p j t", t=P), ACT.Copy,
                                   scale=DH ** -0.5).then_inc(qT_done, 1)
                if live(0) and k % QUARTERS == 1:
                    nxt = At(i, k + 3)
                    take_x(ph, nxt, nxt.batch + 1)
                if live(ph.at_wo) and At(i, k - ph.at_wo).q == 3:
                    take_y(ph, At(i, k - ph.at_wo))
                if live(ph.at_softmax):
                    exps(ph, At(i, k - ph.at_softmax))
                if live(ph.at_out):
                    take_pT(ph, At(i, k - ph.at_out))
                if live(ph.at_values):
                    take_v(ph, At(i, k - ph.at_values))
                if live(ph.at_out):
                    take_o(ph, At(i, k - ph.at_out))
                if live(0) and k % QUARTERS == 2:
                    nxt = At(i, k + 2)
                    take_xT(ph, nxt, nxt.batch + 1)

            act.wait_ge(ln_out, LN_POST2)
            take_x(phase2(), At(0, 0), 1)
            take_xT(phase2(), At(0, 0), 1)
            quarter_steps(act, body2, phase2().at_wo)

            def split_wq(l, n):
                act.wait_ge(ld_wq, n)
                act.activation(wh[:, :, :], wst[:, :, :], ACT.Copy).then_inc(wq_hi, 1)

            split_wq(0, 16 * 3)
            with act.Fori(0, GROUPS) as g:
                act.wait_ge(ln_out, g * 2 + (LN_POST2 + 2))
                act.activation(ybuf[:, bass.ds(g * G, G), :], x[:, bass.ds(g * G, G), :], ACT.Copy).then_inc(kept, 1)
            with act.Fori(0, LAYERS) as l:
                ph = phase3(l)

                def squares(at):
                    act.wait_ge(qk_ps, ph.n(at))
                    act.wait_ge(ssq_done, ph.n(at, 2))
                    act.activation(sq[:, at.pair, :], QKB[at.pair][:, :], ACT.Square).then_inc(sq_done, 1)

                def inverse_norm(at):
                    act.wait_ge(ssq_done, ph.n(at))
                    act.activation(lnr[:, at.pair, :], ssq[:, at.pair, :], ACT.Ln, scale=2.0 ** 16
                                   ).then_inc(ln_done, 1)
                    act.wait_ge(ln_done, ph.n(at))
                    act.wait_ge(qks_done, ph.n(at, 2))
                    act.activation(rn[:, at.pair, :], lnr[:, at.pair, :], ACT.Exp, scale=-0.5,
                                   bias=lnbias[:, 0:1]).then_inc(rn_done, 1)

                def take_T(at):
                    act.wait_ge(t_ps, ph.n(at))
                    act.wait_ge(s_ps, ph.n(at, 2))
                    act.activation(qT[:, at.pair, :, :], TB_[:, 0:2 * P].rearrange("p (j t) -> p j t", t=P),
                                   ACT.Copy).then_inc(qT_done, 1)
                    for h in range(2):
                        r = slice(h * DH, (h + 1) * DH)
                        ins = act.activation(kz[r, at.pair, :, h, :],
                                             TB_[r, 2 * P:4 * P].rearrange("p (j t) -> p j t", t=P), ACT.Copy)
                    ins.then_inc(kT_done, 1)

                def body(i, k, live):
                    if live(2):
                        take_T(At(i, k - 2))
                    if live(0) and k % QUARTERS == 1:
                        nxt = At(i, k + 3)
                        take_x(ph, nxt, nxt.batch + (ph.xb + 1))
                    if live(0):
                        squares(At(i, k))
                    if live(ph.at_softmax):
                        exps(ph, At(i, k - ph.at_softmax))
                    if live(ph.at_wo) and At(i, k - ph.at_wo).q == 3:
                        take_y(ph, At(i, k - ph.at_wo))
                    if live(ph.at_out):
                        take_pT(ph, At(i, k - ph.at_out))
                    if live(ph.at_values):
                        take_v(ph, At(i, k - ph.at_values))
                    if live(0):
                        inverse_norm(At(i, k))
                    if live(ph.at_out):
                        take_o(ph, At(i, k - ph.at_out))
                    if live(0) and k % QUARTERS == 2:
                        nxt = At(i, k + 2)
                        take_xT(ph, nxt, nxt.batch + (ph.xb + 1))

                act.preload_act_table_set("natural_log_exp_and_others")
                act.wait_ge(ln_out, 4 * GROUPS)
                act.wait_ge(f_x, l * GROUPS + 1)
                take_x(ph, At(0, 0), ph.xb + 1)
                take_xT(ph, At(0, 0), ph.xb + 1)
                act.wait_ge(ld_w1, l * 16 + 16)
                act.activation(w1h[:, :], w1st[:, :], ACT.Copy).then_inc(w1_hi, 1)
                quarter_steps(act, body, ph.at_wo)

                def front(g):
                    act.activation(lnz[:, :, 0:64], x[:, bass.ds(g * G, G), 0:64], ACT.Copy).then_inc(f_z0, 1)

                def take_T_ff(g):
                    act.wait_ge(f_T, l * GROUPS + g + 1)
                    act.activation(xfT[:, :, :], bank[1][:, :].rearrange("p (j t) -> p j t", t=P), ACT.Identity,
                                   bias=vec[:, 1:2], scale=vec[:, 0:1]).then_inc(f_xT, 1)

                def back(g):
                    for j, (c0, cn) in enumerate(FBLK):
                        c = (l * GROUPS + g) * FB + (j + 1)
                        act.wait_ge(f_ab, c)
                        act.activation(gel[0:cn, j % 2, :], bank[3 + 2 * (j % 2)][0:cn, :], ACT.Gelu,
                                       bias=b1g[0:cn, j:j + 1]).then_inc(f_gel, 1)

                act.preload_act_table(ACT.Gelu)
                act.wait_ge(tab_done, l + 1)
                act.wait_ge(y_done, l * B + (2 * B + CREDIT))
                front(0)
                take_T_ff(0)
                with act.Fori(1, GROUPS) as g:
                    act.wait_ge(ln_out, l * GROUPS + g + LN_FF)
                    front(g)
                    back(g - 1)
                    take_T_ff(g)
                back(GROUPS - 1)
                split_wq(l + 1, (l * 3 + 6) * 16)

        @block.tensor
        def _(pe):
            start_with_credit(pe, ["qk_ps", "s_ps", "pT_ps", "v_ps", "o_ps", "y_ps"], ["t_ps"])
            pe.wait_ge(pool_const, 10)
            pe.wait_ge(ld_c, 16 * N_LD_C)
            pe.wait_ge(dve_const, 7)
            with pe.Fori(0, GROUPS) as g:
                pe.wait_ge(ln_out, g * 2 + 1)
                for j in range(G):
                    mm = pe.transpose(bank[0][:, j * P:(j + 1) * P], lnx[:, j, :], ident[:, :])
                mm.then_inc(g_T, 1)
                pe.wait_ge(g_xnT, g + 1)
                for j in range(G):
                    mm = pe.matmul(bank[1 + j][:, 0:3 * D], xnT[:, j, :], wqkv1[:, :], start=True, stop=True)
                mm.then_inc(g_qkv, 1)
                pe.wait_ge(g_qk1, g + 1)
                for j in range(G):
                    mm = pe.transpose(bank[0][:, j * P:(j + 1) * P], qk1[:, j, 0:D], ident[:, :])
                mm.then_inc(g_q1T_ps, 1)
                pe.wait_ge(g_v1, g + 1)
                for j in range(G):
                    c = (j % 2) * 160
                    mm = pe.matmul(bank[5 + j // 2][:, c:c + D + 1], qk1[:, j, D:2 * D], v1[:, j, :],
                                   start=True, stop=True)
                mm.then_inc(g_kv, 1)
                pe.wait_ge(g_kvm, g + 1)
                pe.wait_ge(g_q1T, g + 1)
                for j in range(G):
                    c = (j % 2) * 160
                    mm = pe.matmul(bank[5 + j // 2][:, c:c + D + H], q1T[:, j, :], kvm[:, j, :],
                                   start=True, stop=True)
                mm.then_inc(g_o, 1)
                pe.wait_ge(g_o1, g + 1)
                for j in range(G):
                    mm = pe.transpose(bank[0][:, j * P:(j + 1) * P], o1[:, j, :], ident[:, :])
                mm.then_inc(g_o1T_ps, 1)
                pe.wait_ge(g_o1T, g + 1)
                for j in range(G):
                    mm = pe.matmul(bank[7][:, j * P:(j + 1) * P], o1T[:, j, :], wout1[:, :], start=True, stop=True)
                mm.then_inc(g_y, 1)

            def transpose_x(ph, at, n):
                pe.wait_ge(x_in, n)
                if not isinstance(n, int) or n > 1:
                    pe.wait_ge(xT_hi, n - 1)
                ps = VB[:, 384:512]
                for h, (r, moving) in enumerate(((slice(0, 64), ident), (slice(64, 128), shift if ph.local else ident))):
                    mm = pe.matmul(ps[r, :], xin[:, at.bpair, r], moving[:, :], start=True, stop=True)
                mm.then_inc(xT_ps, 1)

            def sims(ph, at):
                pe.wait_ge(qT_done, ph.n(at))
                pe.wait_ge(kT_done if ph.local else kz_done, ph.n(at))
                pe.wait_ge(sub_done, ph.n(at, 2))
                ps, w = SB_[at.pair], 2 * ph.keys
                keys = kz if ph.local else kz2
                if ph.local:
                    pe.matmul(ps[:, :], ident_bf[:, :], mask_bf[:, :, :].rearrange("p h j -> p (h j)"),
                              start=True, stop=False)
                for j in range(2):
                    mm = pe.matmul(ps[:, j * w:(j + 1) * w], qT[:, at.pair, j, :],
                                   keys[:, at.pair, j, :, :].rearrange("p h j -> p (h j)"),
                                   start=not ph.local, stop=not ph.local or j == 1)
                mm.then_inc(s_ps, 1)

            def transpose_p(ph, at):
                pe.wait_ge(pr_done, ph.n(at))
                pe.wait_ge(pT_done, ph.n(at, 1))
                for h in range(HQ):
                    mm = pe.transpose(PTB[0:ph.keys, h * P:(h + 1) * P], pr[:, at.pair, h, 0:ph.keys], ident[:, :])
                mm.then_inc(pT_ps, 1)

            def weighted_v(ph, at):
                pe.wait_ge(pT_done, ph.n(at))
                pe.wait_ge(v_done, ph.n(at))
                pe.wait_ge(oT_done, ph.n(at, 1))
                val = vs if ph.local else vs2
                for h in range(HQ):
                    r = slice((h % 2) * DH, (h % 2 + 1) * DH)
                    mm = pe.matmul(OB[r, (h // 2) * P:(h // 2 + 1) * P], val[:, at.pair, h * DH:(h + 1) * DH],
                                   pT[0:ph.keys, at.pair, h, :], start=True, stop=True)
                mm.then_inc(o_ps, 1)

            def after_xT(ph, i, k, live):
                if live(1) and k % QUARTERS == 3:
                    pe.wait_ge(xT_hi, At(i, k + 1).batch + (ph.xb + 1))

            def project_o(ph, i, k, live):
                if not live(ph.at_wo) or (k - ph.at_wo) % QUARTERS != 3:
                    return
                after_xT(ph, i, k, live)
                at = At(i, k - ph.at_wo)
                pe.wait_ge(oT_done, ph.n(at))
                pe.wait_ge(v_done, ph.n(at, -1 if live(ph.at_values + 1) else 0))
                w = wo if ph.local else wout2
                for j in range(INNER // P):
                    mm = pe.matmul(VB[:, 256:384], oT[:, at.bpair, j, :], w[:, j, :],
                                   start=(j == 0), stop=(j == INNER // P - 1))
                mm.then_inc(y_ps, 1)

            def before_values(ph, i, k, live):
                if live(ph.at_wo) and (k - ph.at_wo) % QUARTERS == 3:
                    pe.wait_ge(y_out, ph.nb(At(i, k - ph.at_wo)))
                else:
                    after_xT(ph, i, k, live)

            def context_T(at, n):
                pe.wait_ge(ld_ctx[at.bpair], at.two * 16 + 16)
                pe.wait_ge(xT_done, n - 1) if not isinstance(n, int) or n > 1 else None
                for c in range(CK):
                    mm = pe.transpose(TB_[:, c * M:(c + 1) * M], cst[:, at.bpair, c * P:(c + 1) * P], ident[0:M, 0:M])
                mm.then_inc(c_ps, 1)

            def project2(ph, at):
                pe.wait_ge(qT_done, ph.n(at, 2))
                pe.wait_ge(kz_done, ph.n(at, 2))
                ps = QKB[at.pair]
                for j in range(2):
                    c = (2 * at.q + j) * P
                    pe.matmul(ps[:, j * P:(j + 1) * P], wq2[:, c:c + P], xTf[:, at.bpair, :], start=True, stop=True)
                for j in range(2):
                    c = (2 * at.q + j) * P
                    for ck in range(CK):
                        mm = pe.matmul(ps[:, 256 + j * M:256 + (j + 1) * M], wkv2[:, ck, c:c + P],
                                       ctxT[:, at.bpair, ck, :], start=(ck == 0), stop=(ck == CK - 1))
                mm.then_inc(qk_ps, 1)

            def values2(ph, at):
                pe.wait_ge(v_done, ph.n(at, 1))
                for ck in range(CK):
                    mm = pe.matmul(VB[0:M, 0:QW], ctxT[:, at.bpair, ck, :],
                                   wkv2[:, ck, INNER + at.q * QW:INNER + (at.q + 1) * QW],
                                   start=(ck == 0), stop=(ck == CK - 1))
                mm.then_inc(v_ps, 1)

            def body2(i, k, live):
                ph = phase2()
                project_o(ph, i, k, live)
                if live(0):
                    at = At(i, k)
                    if at.q == 0:
                        pe.wait_ge(xT_done, at.batch + 1)
                    project2(ph, at)
                if live(ph.at_out):
                    transpose_p(ph, At(i, k - ph.at_out))
                if live(ph.at_values):
                    before_values(ph, i, k, live)
                    values2(ph, At(i, k - ph.at_values))
                if live(ph.at_out):
                    weighted_v(ph, At(i, k - ph.at_out))
                if live(ph.at_sims):
                    sims(ph, At(i, k - ph.at_sims))
                if live(0) and k % QUARTERS == 2:
                    nxt = At(i, k + 2)
                    if live(ph.at_values):
                        pe.wait_ge(v_done, ph.n(At(i, k - ph.at_values)))
                    transpose_x(ph, nxt, nxt.batch + 1)
                    context_T(nxt, nxt.batch + 1)

            pe.wait_ge(g_z, GROUPS)
            transpose_x(phase2(), At(0, 0), 1)
            context_T(At(0, 0), 1)
            quarter_steps(pe, body2, phase2().at_wo)

            with pe.Fori(0, LAYERS) as l:
                ph = phase3(l)

                def three(ps, xh, xl, whi, wlo, last=True):
                    pe.matmul(ps, xh, whi, start=True, stop=False)
                    pe.matmul(ps, xh, wlo, start=False, stop=False)
                    return pe.matmul(ps, xl, whi, start=False, stop=True)

                def project_qk(at):
                    pe.wait_ge(sq_done, ph.n(at, 2))
                    pe.wait_ge(rot_done, ph.n(at, 2))
                    three(QKB[at.pair][:, :], xTh[:, at.bpair, :], xTl[:, at.bpair, :],
                          wh[:, at.q, 0:2 * QW], wl[:, at.q, 0:2 * QW]).then_inc(qk_ps, 1)

                def project_v(at):
                    pe.wait_ge(v_done, ph.n(at, 1))
                    three(VB[:, 0:QW], xTh[:, at.bpair, :], xTl[:, at.bpair, :],
                          wh[:, at.q, 2 * QW:3 * QW], wl[:, at.q, 2 * QW:3 * QW]).then_inc(v_ps, 1)

                def transpose_qk(at):
                    pe.wait_ge(qks_done, ph.n(at))
                    pe.wait_ge(qT_done, ph.n(at, 1))
                    pe.wait_ge(kT_done, ph.n(at, 1))
                    for j in range(4):
                        mm = pe.transpose(TB_[:, j * P:(j + 1) * P], qks[:, at.pair, j * P:(j + 1) * P], ident[:, :])
                    mm.then_inc(t_ps, 1)

                def body(i, k, live):
                    project_o(ph, i, k, live)
                    if live(0):
                        at = At(i, k)
                        if at.q == 0:
                            pe.wait_ge(xT_done, at.batch + (ph.xb + 1))
                        project_qk(at)
                    if live(ph.at_sims):
                        sims(ph, At(i, k - ph.at_sims))
                    if live(ph.at_out):
                        transpose_p(ph, At(i, k - ph.at_out))
                    if live(ph.at_values):
                        before_values(ph, i, k, live)
                        project_v(At(i, k - ph.at_values))
                    if live(1):
                        transpose_qk(At(i, k - 1))
                    if live(ph.at_out):
                        weighted_v(ph, At(i, k - ph.at_out))
                    if live(0) and k % QUARTERS == 2:
                        nxt = At(i, k + 2)
                        if live(ph.at_values):
                            pe.wait_ge(v_done, ph.n(At(i, k - ph.at_values)))
                        transpose_x(ph, nxt, nxt.batch + (ph.xb + 1))

                pe.wait_ge(f_x, l * GROUPS + 1)
                pe.wait_ge(wq_split, l + 1)
                pe.wait_ge(ld_wo, l * 16 + 16)
                transpose_x(ph, At(0, 0), ph.xb + 1)
                quarter_steps(pe, body, ph.at_wo)

                def shifted(g):
                    pe.wait_ge(f_z, l * GROUPS + g + 1)
                    pe.matmul(bank[0][:, 0:G * 64].rearrange("p (j d) -> p j d", d=64), shift[:, :],
                              x[:, bass.ds(g * G, G), 64:128], start=True, stop=True).then_inc(f_shift, 1)

                def front_T(g):
                    pe.wait_ge(ln_out, l * GROUPS + g + (LN_FF + 1))
                    pe.wait_ge(f_xT, l * GROUPS + g + 1)
                    for j in range(G):
                        mm = pe.transpose(bank[1][:, j * P:(j + 1) * P], lnx[:, j, :], ident[:, :])
                    mm.then_inc(f_T, 1)

                def hidden(g):
                    pe.wait_ge(f_split, l * GROUPS + g + 1)
                    for j, (c0, cn) in enumerate(FBLK):
                        if j == 2:
                            pe.wait_ge(f_h, (l * GROUPS + g) * FB + 1)
                        for a in range(2):
                            c = a * FF + c0
                            mm = three(bank[2 + 2 * (j % 2) + a][0:cn, :], w1h[:, c:c + cn], w1l[:, c:c + cn],
                                       xfTh[:, :, :].rearrange("p j t -> p (j t)"),
                                       xfTl[:, :, :].rearrange("p j t -> p (j t)"))
                        mm.then_inc(f_ab, 1)

                def down(g):
                    pe.wait_ge(f_h, (l * GROUPS + g) * FB + FB)
                    for b in range(G):
                        for j, (c0, cn) in enumerate(FBLK):
                            mm = pe.matmul(bank[6][:, b * P:(b + 1) * P], hT[0:cn, j, b * P:(b + 1) * P],
                                           w2[0:cn, j, :], start=(j == 0), stop=(j == FB - 1))
                    mm.then_inc(f_y, 1)

                pe.wait_ge(y_done, l * B + (2 * B + CREDIT))
                pe.wait_ge(w1_split, l + 1)
                pe.wait_ge(ld_w2, l * 32 + 32)
                shifted(0)
                front_T(0)
                with pe.Fori(1, GROUPS) as g:
                    shifted(g)
                    hidden(g - 1)
                    front_T(g)
                    pe.wait_ge(f_x, l * GROUPS + g)
                    down(g - 1)
                hidden(GROUPS - 1)
                pe.wait_ge(f_x, l * GROUPS + GROUPS)
                down(GROUPS - 1)


N_LD_C = 13 + 2 * HQ
N_LD_TAB = 4
NVEC = 2 + 2 * FB
LN_POST2 = 2 * GROUPS
LN_FF = 4 * GROUPS
LN_FINAL = LN_FF + LAYERS * GROUPS

INPUTS = ["x", "ctx_2048", "L0_attn_gamma", "L0_attn_beta", "L0_attn_Wqkv", "L0_attn_Wout", "L0_xattn_Wq",
          "L0_xattn_Wkv", "L0_xattn_null_kv", "L0_xattn_Wout", "L0_xattn_ln_scale", "L0_xattn_ln_bias",
          "L0_ffn_Wqkv", "L0_ffn_Wo", "L0_ffn_W1", "L0_ffn_W2", "L0_ffn_b2"]


def laid_out(inputs):
    scales = np.stack([inputs["L0_ffn_q_scale"], inputs["L0_ffn_k_scale"]], 1).reshape(LAYERS, 2 * DH)
    b1 = np.zeros((LAYERS, 2, FB * P), inputs["L0_ffn_b1"].dtype)
    b1[:, :, :FF] = np.asarray(inputs["L0_ffn_b1"]).reshape(LAYERS, 2, FF)
    rows = [np.asarray(inputs["L0_ffn_ln_g"])[:, None], np.asarray(inputs["L0_ffn_ln_b"])[:, None],
            b1.reshape(LAYERS, 2 * FB, P)]
    named = {"qk_scales": scales, "vectors": np.concatenate(rows, 1).transpose(2, 0, 1)}
    return {name: np.ascontiguousarray(a) for name, a in named.items()}


def shape_constants():
    f = np.float32
    rows = np.arange(P) // HD
    blockmask = (rows[:, None] == rows[None, :]).astype(f)
    headmask = (rows[:, None] == np.arange(H)[None, :]).astype(f)
    half = np.arange(0, DH, 2, dtype=f)
    inv_freq = (f(1.0) / f(10000.0) ** (half / f(DH))).astype(f)
    pos = np.arange(P, dtype=f)
    freqs = pos[:, None] * inv_freq[None, :]
    freqs = np.concatenate([freqs, freqs], -1)
    base = (half + f(0.4 * DH)) / f(1.4 * DH)
    scale = base[None, :] ** ((pos - P // 2) / (WINDOW // 2))[:, None]
    scale = np.concatenate([scale, scale], -1).astype(f)
    sign = np.where(np.arange(DH) < DH // 2, f(-1), f(1))[None, :]
    rot = np.empty((P, 2, 2, DH), f)
    qk_scale = f(8.0)
    rot[:, 0, 0] = np.cos(freqs) * scale * qk_scale
    rot[:, 0, 1] = np.cos(freqs) / scale
    rot[:, 1, 0] = sign * np.sin(freqs) * scale * qk_scale
    rot[:, 1, 1] = sign * np.sin(freqs) / scale
    return {"c_blockmask": blockmask, "c_headmask": headmask, "c_rot": rot}


def kernel(**inputs):
    import concourse.bacc as bacc
    from concourse.bass_utils import run_bass_kernel_spmd

    nc = bacc.Bacc("TRN2", target_bir_lowering=False, num_devices=1)
    arrays = {name: np.ascontiguousarray(inputs[name]) for name in INPUTS}
    arrays = arrays | laid_out(inputs) | shape_constants()
    feeds, t = {}, {}
    for name, a in arrays.items():
        feeds[f"in_{name}"] = a
        t[name] = nc.dram_tensor(f"in_{name}", a.shape, mybir.dt.from_np(a.dtype), kind="ExternalInput").ap()
    out = nc.dram_tensor("out_y", (B, P, D), F32, kind="ExternalOutput").ap()
    build(nc, t, out)
    r = run_bass_kernel_spmd(nc, [feeds], core_ids=[0])
    return r.results[0]["out_y"]
```

```python
from contextlib import ExitStack

import numpy as np

import concourse.bass as bass
from concourse import mybir

F32 = mybir.dt.float32
F32R = mybir.dt.float32r
BF16 = mybir.dt.bfloat16
ALU = mybir.AluOpType
ACT = mybir.ActivationFunctionType
AX = mybir.AxisListType

P = 128
B = 16
D = 128
H = 16
DH = 64
INNER = H * DH
CTX = 256
CK = CTX // P
M = 77
NULLK = M + 1
HD = D // H
LAYERS = 6
FF = 341
FB = 3
WINDOW = 32
HQ = 4
QUARTERS = H // HQ
QW = HQ * DH
HSUM = 2
G = 4
GROUPS = B // G
PER = 2 * QUARTERS
OUTER = B // 2
STEPS = B * QUARTERS
CREDIT = 8
MASKED = -1e30
FBLK = [(j * P, min(P, FF - j * P)) for j in range(FB)]


class At:

    def __init__(self, i, k):
        self.s = i * PER + k
        self.batch = i * 2 + k // QUARTERS
        self.two = i + k // PER
        self.q = k % QUARTERS
        self.pair = k % 2
        self.bpair = (k // QUARTERS) % 2
        self.slot = k % PER


def quarter_steps(eng, body, tail, between=None):
    for k in range(PER):
        body(0, k, lambda lag: k - lag >= 0)
    with eng.Fori(1, OUTER) as i:
        for k in range(PER):
            body(i, k, lambda lag: True)
    for k in range(tail):
        if between is not None:
            between(k)
        body(OUTER, k, lambda lag: k - lag < 0)


def build(nc, t, out):
    ctx = ExitStack()
    with ctx:
        def sb(name, shape, dt=F32):
            return ctx.enter_context(nc.sbuf_tensor(name, shape, dt))

        def sem(name):
            return ctx.enter_context(nc.semaphore(name))

        x = sb("x", [P, B + 1, D])
        ident = sb("ident", [P, P])
        shift = sb("shift", [P, P])
        ident_bf = sb("ident_bf", [P, P], BF16)
        mask_bf = sb("mask_bf", [P, HQ, P], BF16)
        half = sb("half", [P, G])
        lnstat = sb("lnstat", [P, G, 6])
        lnmv = sb("lnmv", [P, G, 2])
        lnseen = sb("lnseen", [P, 1])
        lnvar = sb("lnvar", [P, G])
        lnrs = sb("lnrs", [P, G])
        lnz = sb("lnz", [P, G, D])
        lnx = sb("lnx", [P, G, D])
        gam = sb("gam", [P, 1])
        bet = sb("bet", [P, 1])
        wqkv1 = sb("wqkv1", [P, 3 * D])
        wout1 = sb("wout1", [P, D])
        blockmask = sb("blockmask", [P, P])
        headmask = sb("headmask", [P, H])
        xnT = sb("xnT", [P, G, P])
        qk1 = sb("qk1", [P, G, 2 * D])
        neg = sb("neg", [P, G, 2 * D])
        v1 = sb("v1", [P, G, D + 1])
        kvm = sb("kvm", [P, G, D + H])
        q1T = sb("q1T", [P, G, P])
        den1 = sb("den1", [P, G, H])
        o1 = sb("o1", [P, G, D])
        o1T = sb("o1T", [P, G, P])
        wq2 = sb("wq2", [P, INNER])
        wkv2 = sb("wkv2", [P, CK, 2 * INNER])
        wout2 = sb("wout2", [P, INNER // P, D])
        lns2 = sb("lns2", [P, D])
        lnb2 = sb("lnb2", [P, D])
        cst = sb("cst", [M, 2, CTX])
        ctxT = sb("ctxT", [P, 2, CK, M])
        kz2 = sb("kz2", [P, 2, 2, 2, NULLK])
        nullk = sb("nullk", [P, 1])
        ybuf = sb("ybuf", [P, B, D])
        rot_cs = sb("rot_cs", [P, 2, 2, DH])
        qks_all = sb("qks_all", [P, LAYERS, 2, DH])
        rot_tab = sb("rot_tab", [P, 2, 2, DH])
        wst = sb("wst", [P, QUARTERS, 3 * QW])
        wh = sb("wh", [P, QUARTERS, 3 * QW], F32R)
        wl = sb("wl", [P, QUARTERS, 3 * QW], F32R)
        wo = sb("wo", [P, INNER // P, D])
        xin = sb("xin", [P, 2, D])
        xTh = sb("xTh", [P, 2, P], F32R)
        xTl = sb("xTl", [P, 2, P], F32R)
        xTf = sb("xTf", [P, 2, P])
        sq = sb("sq", [P, 2, 2 * QW])
        ta = sb("ta", [P, 2, 2 * QW])
        tb = sb("tb", [P, 2, 2 * QW])
        ssq = sb("ssq", [P, 2, 2 * HQ])
        lnr = sb("lnr", [P, 2, 2 * HQ])
        rn = sb("rn", [P, 2, 2 * HQ])
        lnbias = sb("lnbias", [P, 1])
        qks = sb("qks", [P, 2, 2 * QW])
        qT = sb("qT", [P, 2, 2, P])
        kz = sb("kz", [P, 2, 2, 2, P])
        mx = sb("mx", [P, 2, HQ])
        pr = sb("pr", [P, 2, HQ, P])
        den = sb("den", [P, 2, HQ])
        rden = sb("rden", [P, 2, HQ])
        pT = sb("pT", [P, 2, HQ, P])
        vs = sb("vs", [P, PER, QW])
        oT = sb("oT", [P, 2, INNER // P, P])
        yst = sb("yst", [P, 2, D])
        vec_all = sb("vec_all", [P, LAYERS, NVEC])
        vec = sb("vec", [P, NVEC])
        b1a, b1g = vec[:, 2:2 + FB], vec[:, 2 + FB:2 + 2 * FB]
        b2_all = sb("b2_all", [P, LAYERS, D])
        b2 = sb("b2", [P, D])
        w1st = sb("w1st", [P, 2 * FF])
        w1h = sb("w1h", [P, 2 * FF], F32R)
        w1l = sb("w1l", [P, 2 * FF], F32R)
        w2 = sb("w2", [P, FB, D])
        xfT = sb("xfT", [P, G, P])
        xfTh = sb("xfTh", [P, G, P], F32R)
        xfTl = sb("xfTl", [P, G, P], F32R)
        gel = sb("gel", [P, 2, G * P])
        hT = sb("hT", [P, FB, G * P])

        bank = [ctx.enter_context(nc.psum_tensor(f"bank{i}", [P, 512], F32)) for i in range(8)]
        QKB, TB_, SB_, PTB = bank[0:2], bank[2], bank[3:5], bank[5]
        VB, OB = bank[6][:, 0:QW], bank[6][:, QW:2 * QW]
        YB, XB = bank[7][:, 0:D], bank[7][:, D:2 * D]

        ld_x0 = sem("ld_x0")
        ld_x = sem("ld_x")
        ld_first = sem("ld_first")
        ld_c = sem("ld_c")
        ld_tab = sem("ld_tab")
        ld_ctx = [sem("ld_ctx0"), sem("ld_ctx1")]
        ld_wq = sem("ld_wq")
        ld_w1 = sem("ld_w1")
        ld_wo = sem("ld_wo")
        ld_w2 = sem("ld_w2")
        st_out = sem("st_out")
        pool_const = sem("pool_const")
        dve_const = sem("dve_const")
        ln_stats = sem("ln_stats")
        ln_mv = sem("ln_mv")
        ln_var = sem("ln_var")
        ln_rs = sem("ln_rs")
        ln_out = sem("ln_out")
        g_T = sem("g_T")
        g_xnT = sem("g_xnT")
        g_qkv = sem("g_qkv")
        g_min = sem("g_min")
        g_exp = sem("g_exp")
        g_qk1 = sem("g_qk1")
        g_v1 = sem("g_v1")
        g_kv = sem("g_kv")
        g_kvm = sem("g_kvm")
        g_q1T_ps = sem("g_q1T_ps")
        g_q1T = sem("g_q1T")
        g_o = sem("g_o")
        g_den = sem("g_den")
        g_rden = sem("g_rden")
        g_o1 = sem("g_o1")
        g_o1T_ps = sem("g_o1T_ps")
        g_o1T = sem("g_o1T")
        g_y = sem("g_y")
        g_z = sem("g_z")
        x_in = sem("x_in")
        xT_ps = sem("xT_ps")
        xT_hi = sem("xT_hi")
        xT_done = sem("xT_done")
        c_ps = sem("c_ps")
        step_sems = {}

        def step_sem(name):
            step_sems[name] = sem(name)
            return step_sems[name]

        qk_ps = step_sem("qk_ps")
        sq_done = step_sem("sq_done")
        rot_done = step_sem("rot_done")
        ssq_raw = step_sem("ssq_raw")
        ssq_done = step_sem("ssq_done")
        ln_done = step_sem("ln_done")
        rn_done = step_sem("rn_done")
        add_done = step_sem("add_done")
        qks_done = step_sem("qks_done")
        t_ps = step_sem("t_ps")
        qT_done = step_sem("qT_done")
        kT_done = step_sem("kT_done")
        kz_done = step_sem("kz_done")
        s_ps = step_sem("s_ps")
        mx_done = step_sem("mx_done")
        sub_done = step_sem("sub_done")
        exp_done = step_sem("exp_done")
        sum_done = step_sem("sum_done")
        den_done = step_sem("den_done")
        rden_done = step_sem("rden_done")
        pr_done = step_sem("pr_done")
        pT_ps = step_sem("pT_ps")
        pT_done = step_sem("pT_done")
        v_ps = step_sem("v_ps")
        v_done = step_sem("v_done")
        o_ps = step_sem("o_ps")
        oT_done = step_sem("oT_done")
        y_ps = step_sem("y_ps")
        y_out = step_sem("y_out")
        y_done = step_sem("y_done")
        post2 = sem("post2")
        kept = sem("kept")
        last_z = sem("last_z")
        tab_done = sem("tab_done")
        wq_hi = sem("wq_hi")
        wq_split = sem("wq_split")
        w1_hi = sem("w1_hi")
        w1_split = sem("w1_split")
        f_shift = sem("f_shift")
        f_z = sem("f_z")
        f_z0 = sem("f_z0")
        f_b2 = sem("f_b2")
        f_T = sem("f_T")
        f_xT = sem("f_xT")
        f_hi = sem("f_hi")
        f_split = sem("f_split")
        f_ab = sem("f_ab")
        f_gel = sem("f_gel")
        f_h = sem("f_h")
        f_y = sem("f_y")
        f_x = sem("f_x")

        block = ctx.enter_context(nc.Block())

        def start_with_credit(eng, names, local=()):
            for n in names:
                eng.sem_inc(step_sems[n], CREDIT)
            for n in local:
                eng.sem_inc(step_sems[n], CREDIT + STEPS)

        class Phase:

            def __init__(self, local, base, bbase):
                self.local = local
                self.keys = P if local else NULLK
                self.base = base
                self.bbase = bbase
                self.at_sims = 2 if local else 1
                self.at_softmax = self.at_sims + 1
                self.at_out = self.at_sims + 2
                self.at_wo = 5

            def n(self, at, back=0):
                return at.s + (self.base + (CREDIT + 1 - back))

            def nb(self, at, back=0):
                return at.batch + (self.bbase + (CREDIT + 1 - back))

        def phase2():
            p = Phase(False, 0, 0)
            p.xb = 0
            return p

        def phase3(l):
            p = Phase(True, l * STEPS + STEPS, l * B + B)
            p.xb = l * (B + 1) + (B + 1)
            return p

        @block.sync
        def _(sp):
            xv = t["x"].rearrange("b p d -> p b d")
            sp.dma_start(x[:, 0:G, :], xv[:, 0:G, :]).then_inc(ld_x0, 16)
            col = lambda a: a.rearrange("(p o) -> p o", o=1)
            row = lambda a: a.rearrange("(o p) -> o p", o=1)
            first = [
                (gam[:, :], col(t["L0_attn_gamma"])), (bet[:, :], col(t["L0_attn_beta"])),
                (wqkv1[:, :], t["L0_attn_Wqkv"]), (wout1[:, :], t["L0_attn_Wout"]),
                (blockmask[:, :], t["c_blockmask"]), (headmask[:, :], t["c_headmask"]),
            ]
            for dst, src in first:
                sp.dma_start(dst, src).then_inc(ld_first, 16)
            assert N_LD_FIRST == len(first)
            for g in range(1, GROUPS):
                sp.dma_start(x[:, g * G:(g + 1) * G, :], xv[:, g * G:(g + 1) * G, :]).then_inc(ld_x, 16)
            second = [
                (wq2[:, :], t["L0_xattn_Wq"]),
                (wkv2[:, :, :], t["L0_xattn_Wkv"].rearrange("(c p) n -> p c n", p=P)),
                (wout2[:, :, :], t["L0_xattn_Wout"].rearrange("(j p) n -> p j n", p=P)),
                (lns2[:, :], row(t["L0_xattn_ln_scale"]).to_broadcast([P, D])),
                (lnb2[:, :], row(t["L0_xattn_ln_bias"]).to_broadcast([P, D])),
                (nullk[0:DH, :], col(t["L0_xattn_null_kv"][0])),
                (nullk[DH:P, :], col(t["L0_xattn_null_kv"][0])),
            ]
            for dst, src in second:
                sp.dma_start(dst, src).then_inc(ld_c, 16)
            sp.dma_start(vs[M:M + 1, :, :].rearrange("o r (h d) -> o (r h) d", d=DH),
                         t["L0_xattn_null_kv"][1:2, :].unsqueeze(1).to_broadcast([1, PER * HQ, DH])
                         ).then_inc(ld_c, 16)
            assert N_LD_C == len(second) + 1

            def load_wq(l):
                for j in range(3):
                    sp.dma_start(wst[:, :, j * QW:(j + 1) * QW],
                                 t["L0_ffn_Wqkv"][l, :, j * INNER:(j + 1) * INNER]
                                 .rearrange("p (q n) -> p q n", q=QUARTERS)).then_inc(ld_wq, 16)

            def load_w1(l):
                sp.dma_start(w1st[:, :], t["L0_ffn_W1"][l]).then_inc(ld_w1, 16)

            def load_wo(l):
                sp.dma_start(wo[:, :, :], t["L0_ffn_Wo"][l].rearrange("(j p) n -> p j n", p=P)).then_inc(ld_wo, 16)

            def load_w2(l):
                sp.dma_start(w2[:, 0:2, :], t["L0_ffn_W2"][l, 0:2 * P, :].rearrange("(j p) n -> p j n", p=P)
                             ).then_inc(ld_w2, 16)
                sp.dma_start(w2[0:FF - 2 * P, 2, :], t["L0_ffn_W2"][l, 2 * P:FF, :]).then_inc(ld_w2, 16)

            def load_ctx(b, slot):
                sp.dma_start(cst[:, slot, :], t["ctx_2048"][b]).then_inc(ld_ctx[slot], 16)

            for b in range(2):
                load_ctx(b, b)
            load_wq(0)
            every = lambda a, n: a.rearrange("l n -> (l n)").rearrange("(o n) -> o n", o=1).to_broadcast([P, n])
            tables = [
                (rot_cs[:, :, :, :], t["c_rot"]), (vec_all[:, :, :], t["vectors"]),
                (qks_all[:, :, :, :].rearrange("p l a d -> p (l a d)"), every(t["qk_scales"], LAYERS * 2 * DH)),
                (b2_all[:, :, :].rearrange("p l d -> p (l d)"), every(t["L0_ffn_b2"], LAYERS * D)),
            ]
            for dst, src in tables:
                sp.dma_start(dst, src).then_inc(ld_tab, 16)
            assert N_LD_TAB == len(tables)
            load_w1(0)
            load_wo(0)
            load_w2(0)
            with sp.Fori(0, OUTER) as i:
                for b in range(2):
                    sp.wait_ge(c_ps, i * 2 + (b + 1))
                    load_ctx((i * 2 + (b + 2)) % B, b)
            with sp.Fori(0, LAYERS) as l:
                sp.wait_ge(wq_split, l * QUARTERS + QUARTERS)
                load_wq((l + 1) % LAYERS)
                sp.wait_ge(w1_split, l + 1)
                load_w1((l + 1) % LAYERS)
                sp.wait_ge(y_done, l * B + (2 * B + CREDIT))
                load_wo((l + 1) % LAYERS)
                sp.wait_ge(f_x, l * GROUPS + 2 * GROUPS)
                load_w2((l + 1) % LAYERS)
            ov = out.rearrange("b p d -> p b d")
            for g in range(GROUPS):
                sp.wait_ge(ln_out, LN_FINAL + g + 1)
                sp.dma_start(ov[:, g * G:(g + 1) * G, :], x[:, g * G:(g + 1) * G, :]).then_inc(st_out, 16)
            for b in range(2):
                sp.wait_ge(ld_ctx[b], 16 * (OUTER + 1))
            sp.wait_ge(ld_wq, 16 * 3 * (LAYERS + 1))
            sp.wait_ge(ld_w1, 16 * (LAYERS + 1))
            sp.wait_ge(ld_wo, 16 * (LAYERS + 1))
            sp.wait_ge(ld_w2, 16 * 2 * (LAYERS + 1))
            sp.wait_ge(st_out, 16 * GROUPS)

        @block.gpsimd
        def _(pool):
            pool.memset(ident[:], 0.0).then_inc(pool_const, 1)
            pool.memset(shift[:], 0.0).then_inc(pool_const, 1)
            pool.memset(ident_bf[:], 0.0).then_inc(pool_const, 1)
            pool.memset(mask_bf[:], 0.0).then_inc(pool_const, 1)
            pool.memset(half[:], -0.5).then_inc(pool_const, 1)
            pool.wait_ge(pool_const, 5)
            pool.affine_select(out=ident[:], in_=ident[:], compare_op=ALU.not_equal, fill=1.0, base=0,
                               pattern=[[-1, P]], channel_multiplier=1).then_inc(pool_const, 1)
            pool.affine_select(out=shift[:], in_=shift[:], compare_op=ALU.not_equal, fill=1.0, base=1,
                               pattern=[[-1, P]], channel_multiplier=1).then_inc(pool_const, 1)
            pool.affine_select(out=ident_bf[:], in_=ident_bf[:], compare_op=ALU.not_equal, fill=1.0, base=0,
                               pattern=[[-1, P]], channel_multiplier=1).then_inc(pool_const, 1)
            pool.affine_select(out=mask_bf[:], in_=mask_bf[:], compare_op=ALU.is_ge, fill=MASKED, base=0,
                               pattern=[[0, HQ], [-1, P]], channel_multiplier=1).then_inc(pool_const, 1)
            pool.wait_ge(pool_const, 9)
            pool.affine_select(out=mask_bf[:], in_=mask_bf[:], compare_op=ALU.is_ge, fill=MASKED, base=WINDOW,
                               pattern=[[0, HQ], [1, P]], channel_multiplier=-1).then_inc(pool_const, 1)
            start_with_credit(pool, ["pr_done", "y_done"], ["add_done", "qks_done"])

            def rsqrt_of(count):
                pool.wait_ge(ln_var, count)
                pool.tensor_tensor(lnrs[:, :], lnvar[:, :], half[:, :], ALU.pow).then_inc(ln_rs, 1)

            with pool.Fori(0, 2 * GROUPS) as n:
                rsqrt_of(n + 1)

            def normalise(ph, at):
                pool.wait_ge(rden_done, ph.n(at))
                w = pr[:, at.pair, :, 0:ph.keys]
                pool.tensor_tensor(w, w, rden[:, at.pair, :].unsqueeze(2).to_broadcast([P, HQ, ph.keys]),
                                   ALU.mult).then_inc(pr_done, 1)

            def body2(i, k, live):
                ph = phase2()
                if live(ph.at_out):
                    normalise(ph, At(i, k - ph.at_out))
                if live(ph.at_wo) and At(i, k - ph.at_wo).q == 3:
                    at = At(i, k - ph.at_wo)
                    pool.wait_ge(y_out, ph.nb(at))
                    pool.tensor_copy(ybuf[:, bass.ds(at.batch, 1), :].rearrange("p o d -> p (o d)"),
                                     yst[:, at.bpair, :]).then_inc(y_done, 1)

            quarter_steps(pool, body2, phase2().at_wo)

            def split_wq(l, q):
                pool.wait_ge(wq_hi, l * QUARTERS + q + 1)
                of = lambda w: w[:, bass.ds(q, 1), :].rearrange("p o n -> p (o n)")
                pool.tensor_tensor(of(wl), of(wst), of(wh).bitcast(F32), ALU.subtract).then_inc(wq_split, 1)

            with pool.Fori(0, QUARTERS) as q:
                rsqrt_of(q * 2 + (LN_POST2 + 1))
                rsqrt_of(q * 2 + (LN_POST2 + 2))
                split_wq(0, q)
            with pool.Fori(0, LAYERS) as l:
                ph = phase3(l)
                def add(at):
                    pool.wait_ge(rot_done, ph.n(at))
                    pool.tensor_tensor(ta[:, at.pair, :], ta[:, at.pair, :], tb[:, at.pair, :], ALU.add
                                       ).then_inc(add_done, 1)

                def scale(at):
                    pool.wait_ge(rn_done, ph.n(at))
                    pool.wait_ge(add_done, ph.n(at))
                    pool.wait_ge(t_ps, ph.n(at, 2))
                    pool.tensor_tensor(qks[:, at.pair, :].rearrange("p (h d) -> p h d", d=DH),
                                       ta[:, at.pair, :].rearrange("p (h d) -> p h d", d=DH),
                                       rn[:, at.pair, :].unsqueeze(2).to_broadcast([P, 2 * HQ, DH]),
                                       ALU.mult).then_inc(qks_done, 1)

                def residual(at):
                    pool.wait_ge(y_out, ph.nb(at))
                    xb = x[:, bass.ds(at.batch, 1), :].rearrange("p o d -> p (o d)")
                    pool.tensor_tensor(xb, xb, yst[:, at.bpair, :], ALU.add).then_inc(y_done, 1)

                def xT_low(at, n):
                    pool.wait_ge(xT_hi, n)
                    pool.tensor_tensor(xTl[:, at.bpair, :], xTf[:, at.bpair, :], xTh[:, at.bpair, :].bitcast(F32),
                                       ALU.subtract).then_inc(xT_done, 1)

                def body(i, k, live):
                    if live(ph.at_out):
                        normalise(ph, At(i, k - ph.at_out))
                    if live(1):
                        scale(At(i, k - 1))
                    if live(0):
                        add(At(i, k))
                    if live(ph.at_wo) and At(i, k - ph.at_wo).q == 3:
                        residual(At(i, k - ph.at_wo))
                    if live(0) and k % QUARTERS == 1:
                        nxt = At(i, k + 3)
                        xT_low(nxt, nxt.batch + (ph.xb + 1))

                def roots_ahead(k):
                    if k == 4:
                        rsqrt_of(l * GROUPS + (LN_FF + 1))

                xT_low(At(0, 0), ph.xb + 1)
                pool.wait_ge(w1_hi, l + 1)
                pool.tensor_tensor(w1l[:, :], w1st[:, :], w1h[:, :].bitcast(F32), ALU.subtract).then_inc(w1_split, 1)
                quarter_steps(pool, body, ph.at_wo, roots_ahead)
                def add_b2(g):
                    pool.wait_ge(f_z, l * GROUPS + g + 2)
                    pool.wait_ge(f_z0, l * GROUPS + g + 1)
                    pool.tensor_tensor(x[:, bass.ds(g * G, G), :], x[:, bass.ds(g * G, G), :],
                                       b2[:, :].unsqueeze(1).to_broadcast([P, G, D]), ALU.add).then_inc(f_b2, 1)

                add_b2(0)
                rsqrt_of(l * GROUPS + (LN_FF + 2))
                with pool.Fori(1, GROUPS - 1) as g:
                    add_b2(g)
                    rsqrt_of(l * GROUPS + g + (LN_FF + 2))
                    split_wq(l + 1, g - 1)
                add_b2(GROUPS - 1)
                split_wq(l + 1, GROUPS - 2)
                split_wq(l + 1, GROUPS - 1)
            with pool.Fori(0, GROUPS) as n:
                rsqrt_of(n + (LN_FINAL + 1))

        @block.vector
        def _(dve):
            dve.memset(v1[:, :, D:D + 1], 1.0).then_inc(dve_const, 1)
            dve.memset(kz[:], 0.0).then_inc(dve_const, 1)
            dve.memset(kz2[:], 0.0).then_inc(dve_const, 1)
            dve.memset(x[:, B:B + 1, :], 0.0).then_inc(dve_const, 1)
            dve.memset(lnbias[:], float(np.log(2.0 ** 8))).then_inc(dve_const, 1)
            start_with_credit(dve, ["kz_done", "mx_done", "sub_done", "den_done", "rden_done"],
                              ["rot_done", "ssq_raw", "ssq_done"])
            dve.sem_inc(f_z, 1)
            dve.sem_inc(f_x, GROUPS)
            def norm_stats(count, src, eps):
                for j in range(G):
                    ins = dve.bn_stats(lnstat[:, j, :], src(j))
                ins.then_inc(ln_stats, 1)
                dve.wait_ge(ln_stats, count)
                dve.tensor_copy(lnseen[:, :], lnstat[:, 0, 0:1])
                for j in range(G):
                    ins = dve.bn_aggr(lnmv[:, j, :], lnstat[:, j, :])
                ins.then_inc(ln_mv, 1)
                dve.wait_ge(ln_mv, count)
                dve.tensor_scalar(lnvar[:, :].unsqueeze(2), lnmv[:, :, 1:2], eps, None, ALU.add
                                  ).then_inc(ln_var, 1)

            def norm_apply(count, src, dst):
                dve.wait_ge(ln_rs, count)
                for j in range(G):
                    ins = dve.tensor_scalar(dst(j), src(j), lnmv[:, j, 0:1], lnrs[:, j:j + 1],
                                            ALU.subtract, ALU.mult)
                ins.then_inc(ln_out, 1)

            def norm(count, src, dst, eps):
                norm_stats(count, src, eps)
                norm_apply(count, src, dst)

            def xg(g):
                return lambda j: x[:, bass.ds(g * G + j, 1), :].rearrange("p o d -> p (o d)")

            zg = lambda j: lnz[:, j, :]
            ng = lambda j: lnx[:, j, :]

            def low_side(g):
                dve.wait_ge(g_qkv, g + 1)
                for j in range(G):
                    ins = dve.tensor_scalar(neg[:, j, :], bank[1 + j][:, 0:2 * D], 0.0, None, ALU.min)
                ins.then_inc(g_min, 1)

            def positive(g):
                dve.wait_ge(g_exp, g + 1)
                for j in range(G):
                    ins = dve.scalar_tensor_tensor(qk1[:, j, :], bank[1 + j][:, 0:2 * D], 0.0, neg[:, j, :],
                                                   ALU.max, ALU.add)
                ins.then_inc(g_qk1, 1)

            def mask_kv(g):
                dve.wait_ge(g_kv, g + 1)
                for j in range(G):
                    kv = bank[5 + j // 2][:, (j % 2) * 160:(j % 2) * 160 + D + 1]
                    dve.tensor_tensor(kvm[:, j, 0:D], kv[:, 0:D], blockmask[:, :], ALU.mult)
                    ins = dve.tensor_scalar(kvm[:, j, D:D + H], headmask[:, :], kv[:, D:D + 1], None, ALU.mult)
                ins.then_inc(g_kvm, 1)

            def divide(g):
                dve.wait_ge(g_o, g + 1)
                for j in range(G):
                    o = bank[5 + j // 2][:, (j % 2) * 160:(j % 2) * 160 + D + H]
                    ins = dve.tensor_scalar(den1[:, j, :], o[:, D:D + H], 1e-6, None, ALU.add)
                ins.then_inc(g_den, 1)
                dve.wait_ge(g_den, g + 1)
                dve.reciprocal(den1[:, :, :], den1[:, :, :]).then_inc(g_rden, 1)
                dve.wait_ge(g_rden, g + 1)
                for j in range(G):
                    o = bank[5 + j // 2][:, (j % 2) * 160:(j % 2) * 160 + D]
                    ins = dve.tensor_tensor(o1[:, j, :].rearrange("p (h e) -> p h e", e=HD),
                                            o.rearrange("p (h e) -> p h e", e=HD),
                                            den1[:, j, :].unsqueeze(2).to_broadcast([P, H, HD]), ALU.mult)
                ins.then_inc(g_o1, 1)

            def residual1(g):
                dve.wait_ge(g_y, g + 1)
                dve.scalar_tensor_tensor(lnz[:, :, :], x[:, bass.ds(g * G, G), :], 2.0,
                                         bank[7][:, :].rearrange("p (j d) -> p j d", d=D),
                                         ALU.mult, ALU.add).then_inc(g_z, 1)
                dve.wait_ge(g_z, g + 1)

            dve.wait_ge(ld_x0, 16)
            norm(1, xg(0), ng, 1e-5)
            dve.wait_ge(ld_first, 16 * N_LD_FIRST)
            low_side(0)
            positive(0)
            dve.wait_ge(ld_x, 16 * (GROUPS - 1))
            with dve.Fori(1, GROUPS) as g:
                norm_stats(g * 2, xg(g), 1e-5)
                mask_kv(g - 1)
                norm_apply(g * 2, xg(g), ng)
                divide(g - 1)
                low_side(g)
                residual1(g - 1)
                norm_stats(g * 2 + 1, zg, 1e-5)
                positive(g)
                norm_apply(g * 2 + 1, zg, xg(g - 1))
            mask_kv(GROUPS - 1)
            divide(GROUPS - 1)
            residual1(GROUPS - 1)
            norm(2 * GROUPS, zg, xg(GROUPS - 1), 1e-5)

            def row_max(ph, at):
                dve.wait_ge(s_ps, ph.n(at))
                sim = SB_[at.pair][:, 0:HQ * ph.keys].rearrange("p (h j) -> p h j", j=ph.keys)
                dve.tensor_reduce(mx[:, at.pair, :], sim, AX.X, ALU.max).then_inc(mx_done, 1)

            def less_max(ph, at):
                sim = SB_[at.pair][:, 0:HQ * ph.keys].rearrange("p (h j) -> p h j", j=ph.keys)
                dve.wait_ge(mx_done, ph.n(at))
                dve.wait_ge(pT_ps, ph.n(at, 2))
                dve.tensor_tensor(pr[:, at.pair, :, 0:ph.keys], sim,
                                  mx[:, at.pair, :].unsqueeze(2).to_broadcast([P, HQ, ph.keys]),
                                  ALU.subtract).then_inc(sub_done, 1)

            def row_sum(ph, at):
                dve.wait_ge(exp_done, ph.n(at))
                dve.tensor_reduce(den[:, at.pair, HSUM:HQ], pr[:, at.pair, HSUM:HQ, 0:ph.keys], AX.X, ALU.add
                                  ).then_inc(den_done, 1)

            def inverse_sum(ph, at):
                dve.wait_ge(den_done, ph.n(at))
                dve.wait_ge(sum_done, ph.n(at))
                dve.wait_ge(pr_done, ph.n(at, 2))
                dve.reciprocal(rden[:, at.pair, :], den[:, at.pair, :]).then_inc(rden_done, 1)

            def body2(i, k, live):
                ph = phase2()
                if live(ph.at_softmax):
                    row_max(ph, At(i, k - ph.at_softmax))
                if live(ph.at_softmax):
                    less_max(ph, At(i, k - ph.at_softmax))
                if live(0):
                    at = At(i, k)
                    dve.wait_ge(qk_ps, ph.n(at))
                    dve.wait_ge(s_ps, ph.n(at, 2))
                    kps = QKB[at.pair][:, 256:256 + 2 * M].rearrange("p (b m) -> p b m", m=M)
                    for h in range(2):
                        r = slice(h * DH, (h + 1) * DH)
                        ins = dve.tensor_copy(kz2[r, at.pair, :, h, 0:M], kps[r, :, :])
                    ins.then_inc(kz_done, 1)
                if live(ph.at_softmax):
                    row_sum(ph, At(i, k - ph.at_softmax))
                if live(ph.at_softmax):
                    inverse_sum(ph, At(i, k - ph.at_softmax))

            dve.wait_ge(ld_c, 16 * N_LD_C)
            for h in range(2):
                dve.tensor_copy(kz2[h * DH:(h + 1) * DH, :, :, h, M:NULLK].rearrange("p a b o -> p (a b) o"),
                                nullk[h * DH:(h + 1) * DH, :].unsqueeze(1).to_broadcast([DH, 4, 1])
                                ).then_inc(dve_const, 1)
            dve.wait_ge(dve_const, 7)
            quarter_steps(dve, body2, phase2().at_softmax)
            dve.wait_ge(y_done, CREDIT + B)

            yg = lambda g: (lambda j: ybuf[:, bass.ds(g * G + j, 1), :].rearrange("p o d -> p (o d)"))

            def scale_bias(g, count):
                dve.wait_ge(ln_out, count)
                dve.tensor_tensor(lnx[:, :, :], lnx[:, :, :], lns2[:, :].unsqueeze(1).to_broadcast([P, G, D]),
                                  ALU.mult).then_inc(post2, 1)
                dve.wait_ge(post2, g * 3 + 1)
                dve.tensor_tensor(lnx[:, :, :], lnx[:, :, :], lnb2[:, :].unsqueeze(1).to_broadcast([P, G, D]),
                                  ALU.add).then_inc(post2, 1)

            def residual2(g):
                dve.wait_ge(post2, g * 3 + 2)
                dve.wait_ge(ln_out, g * 2 + (LN_POST2 + 1))
                dve.tensor_tensor(lnz[:, :, :], lnx[:, :, :], x[:, bass.ds(g * G, G), :], ALU.add
                                  ).then_inc(post2, 1)
                dve.wait_ge(post2, g * 3 + 3)

            norm(LN_POST2 + 1, yg(0), ng, 1e-6)
            scale_bias(0, LN_POST2 + 1)
            with dve.Fori(1, GROUPS) as g:
                norm_stats(g * 2 + LN_POST2, yg(g), 1e-6)
                residual2(g - 1)
                norm_apply(g * 2 + LN_POST2, yg(g), ng)
                norm_stats(g * 2 + (LN_POST2 + 1), zg, 1e-5)
                scale_bias(g, g * 2 + LN_POST2)
                norm_apply(g * 2 + (LN_POST2 + 1), zg, xg(g - 1))
            residual2(GROUPS - 1)
            norm(LN_POST2 + 2 * GROUPS, zg, xg(GROUPS - 1), 1e-5)

            dve.wait_ge(ld_tab, 16 * N_LD_TAB)
            with dve.Fori(0, LAYERS) as l:
                ph = phase3(l)
                dve.wait_ge(f_x, l * GROUPS + GROUPS)
                sc = qks_all[:, bass.ds(l, 1), :, :].rearrange("p o a d -> p (o a) d")
                dve.tensor_copy(vec[:, :].unsqueeze(1), vec_all[:, bass.ds(l, 1), :])
                dve.tensor_copy(b2[:, :].unsqueeze(1), b2_all[:, bass.ds(l, 1), :])
                dve.tensor_tensor(rot_tab[:, 0, :, :], rot_cs[:, 0, :, :], sc, ALU.mult)
                dve.tensor_tensor(rot_tab[:, 1, :, 0:32], rot_cs[:, 1, :, 0:32], sc[:, :, 32:64], ALU.mult)
                dve.tensor_tensor(rot_tab[:, 1, :, 32:64], rot_cs[:, 1, :, 32:64], sc[:, :, 0:32], ALU.mult
                                  ).then_inc(tab_done, 1)
                dve.wait_ge(tab_done, l + 1)

                def rotate_cos(at):
                    dve.wait_ge(sq_done, ph.n(at))
                    dve.wait_ge(qks_done, ph.n(at, 2))
                    src = QKB[at.pair][:, :].rearrange("p (a h d) -> p a h d", a=2, d=DH)
                    cosp = ta[:, at.pair, :].rearrange("p (a h d) -> p a h d", a=2, d=DH)
                    dve.tensor_tensor(cosp, src,
                                      rot_tab[:, 0, :, :].unsqueeze(2).to_broadcast([P, 2, HQ, DH]), ALU.mult)

                def rotate_sin(at):
                    src = QKB[at.pair][:, :].rearrange("p (a h d) -> p a h d", a=2, d=DH)
                    sinp = tb[:, at.pair, :].rearrange("p (a h d) -> p a h d", a=2, d=DH)
                    for lo, hi in ((0, 32), (32, 0)):
                        ins = dve.tensor_tensor(
                            sinp[:, :, :, lo:lo + 32], src[:, :, :, hi:hi + 32],
                            rot_tab[:, 1, :, lo:lo + 32].unsqueeze(2).to_broadcast([P, 2, HQ, 32]), ALU.mult)
                    ins.then_inc(rot_done, 1)

                def square_sums(at):
                    dve.wait_ge(sq_done, ph.n(at))
                    dve.tensor_reduce(ssq[:, at.pair, :], sq[:, at.pair, :].rearrange("p (h d) -> p h d", d=DH),
                                      AX.X, ALU.add).then_inc(ssq_raw, 1)

                def guard(at):
                    dve.wait_ge(ssq_raw, ph.n(at))
                    dve.tensor_scalar(ssq[:, at.pair, :], ssq[:, at.pair, :], 1e-24, None, ALU.max
                                      ).then_inc(ssq_done, 1)

                def body(i, k, live):
                    if live(ph.at_softmax):
                        row_max(ph, At(i, k - ph.at_softmax))
                    if live(ph.at_softmax):
                        less_max(ph, At(i, k - ph.at_softmax))
                    if live(0):
                        rotate_cos(At(i, k))
                    if live(0):
                        rotate_sin(At(i, k))
                    if live(0):
                        square_sums(At(i, k))
                    if live(ph.at_softmax):
                        row_sum(ph, At(i, k - ph.at_softmax))
                    if live(0):
                        guard(At(i, k))
                    if live(ph.at_softmax):
                        inverse_sum(ph, At(i, k - ph.at_softmax))

                quarter_steps(dve, body, ph.at_softmax)

                def front(g):
                    c = l * GROUPS + g + 1
                    dve.wait_ge(f_shift, c)
                    dve.wait_ge(ln_out, l * GROUPS + g + LN_FF)
                    dve.tensor_copy(lnz[:, :, 64:128], bank[0][:, 0:G * 64].rearrange("p (j d) -> p j d", d=64)
                                    ).then_inc(f_z, 1)
                    dve.wait_ge(f_z, c + 1)
                    dve.wait_ge(f_z0, c)
                    norm_stats(l * GROUPS + g + (LN_FF + 1), zg, 1e-5)

                def apply(g):
                    norm_apply(l * GROUPS + g + (LN_FF + 1), zg, ng)

                def split(g):
                    c = l * GROUPS + g + 1
                    dve.wait_ge(f_xT, c + 1)
                    dve.tensor_copy(xfTh[:, :, :], xfT[:, :, :]).then_inc(f_hi, 1)
                    dve.wait_ge(f_hi, c)
                    dve.tensor_tensor(xfTl[:, :, :], xfT[:, :, :], xfTh[:, :, :].bitcast(F32), ALU.subtract
                                      ).then_inc(f_split, 1)

                def gated(g, j):
                    cn = FBLK[j][1]
                    dve.wait_ge(f_gel, (l * GROUPS + g) * FB + (j + 1))
                    dve.scalar_tensor_tensor(hT[0:cn, j, :], bank[2 + 2 * (j % 2)][0:cn, :],
                                             b1a[0:cn, j:j + 1], gel[0:cn, j % 2, :],
                                             ALU.add, ALU.mult).then_inc(f_h, 1)

                def residual(g):
                    dve.wait_ge(f_y, l * GROUPS + g + 1)
                    dve.wait_ge(f_b2, l * GROUPS + g + 1)
                    xs = x[:, bass.ds(g * G, G), :]
                    dve.tensor_tensor(xs, xs, bank[6][:, :].rearrange("p (j d) -> p j d", d=D), ALU.add
                                      ).then_inc(f_x, 1)

                front(0)
                apply(0)
                split(0)
                front(1)
                apply(1)

                def ffn_pass(g, last):
                    for j in range(FB):
                        gated(g - 1, j)
                    split(g)
                    if not last:
                        front(g + 1)
                    residual(g - 1)
                    if not last:
                        apply(g + 1)

                with dve.Fori(1, GROUPS - 1) as g:
                    ffn_pass(g, False)
                ffn_pass(GROUPS - 1, True)
                for j in range(FB):
                    gated(GROUPS - 1, j)
                residual(GROUPS - 1)

            dve.wait_ge(kept, GROUPS)
            with dve.Fori(0, GROUPS) as g:
                xs = x[:, bass.ds(g * G, G), :]
                dve.wait_ge(ln_out, g + LN_FINAL)
                dve.tensor_tensor(lnz[:, :, :], xs, ybuf[:, bass.ds(g * G, G), :], ALU.add).then_inc(last_z, 1)
                dve.wait_ge(last_z, g + 1)
                norm(g + (LN_FINAL + 1), zg, xg(g), 1e-5)

        @block.scalar
        def _(act):
            start_with_credit(act, ["y_out", "qT_done", "exp_done", "sum_done", "pT_done", "v_done", "oT_done"],
                              ["sq_done", "ln_done", "rn_done", "kT_done"])
            act.sem_inc(f_xT, 1)
            act.wait_ge(ld_first, 16 * N_LD_FIRST)
            act.wait_ge(dve_const, 5)

            def take_xnT(g):
                act.wait_ge(g_T, g + 1)
                act.activation(xnT[:, :, :], bank[0][:, :].rearrange("p (j t) -> p j t", t=P), ACT.Identity,
                               bias=bet[:, 0:1], scale=gam[:, 0:1]).then_inc(g_xnT, 1)

            def exp_take_v(g):
                act.wait_ge(g_min, g + 1)
                act.activation(neg[:, :, :], neg[:, :, :], ACT.Exp).then_inc(g_exp, 1)
                act.wait_ge(g_qk1, g + 1)
                for j in range(G):
                    ins = act.activation(v1[:, j, 0:D], bank[1 + j][:, 2 * D:3 * D], ACT.Copy)
                ins.then_inc(g_v1, 1)

            def take_q1T(g):
                act.wait_ge(g_q1T_ps, g + 1)
                act.activation(q1T[:, :, :], bank[7][:, :].rearrange("p (j t) -> p j t", t=P), ACT.Copy
                               ).then_inc(g_q1T, 1)

            def take_o1T(g):
                act.wait_ge(g_o1T_ps, g + 1)
                act.activation(o1T[:, :, :], bank[7][:, :].rearrange("p (j t) -> p j t", t=P), ACT.Copy
                               ).then_inc(g_o1T, 1)

            take_xnT(0)
            exp_take_v(0)
            with act.Fori(1, GROUPS) as g:
                take_q1T(g - 1)
                take_xnT(g)
                take_o1T(g - 1)
                exp_take_v(g)
            take_q1T(GROUPS - 1)
            take_o1T(GROUPS - 1)

            def take_x(ph, at, n):
                if not isinstance(n, int) or n > 2:
                    act.wait_ge(xT_ps, n - 2)
                act.activation(xin[:, at.bpair, :], x[:, bass.ds(at.batch, 1), :].rearrange("p o d -> p (o d)"),
                               ACT.Copy).then_inc(x_in, 1)

            def exps(ph, at):
                act.wait_ge(sub_done, ph.n(at))
                w = pr[:, at.pair, HSUM:HQ, 0:ph.keys]
                act.activation(w, w, ACT.Exp).then_inc(exp_done, 1)
                for h in range(HSUM):
                    w = pr[:, at.pair, h, 0:ph.keys]
                    ins = act.activation(w, w, ACT.Exp, accum_out=den[:, at.pair, h:h + 1])
                ins.then_inc(sum_done, 1)

            def take_pT(ph, at):
                act.wait_ge(pT_ps, ph.n(at))
                act.wait_ge(o_ps, ph.n(at, 2))
                act.activation(pT[0:ph.keys, at.pair, :, :],
                               PTB[0:ph.keys, :].rearrange("p (h t) -> p h t", t=P), ACT.Copy
                               ).then_inc(pT_done, 1)

            def take_v(ph, at):
                act.wait_ge(v_ps, ph.n(at))
                act.wait_ge(o_ps, ph.n(at, PER))
                rows = P if ph.local else M
                act.activation(vs[0:rows, at.slot, :], VB[0:rows, :], ACT.Copy).then_inc(v_done, 1)

            def take_o(ph, at):
                act.wait_ge(o_ps, ph.n(at))
                act.wait_ge(y_ps, ph.nb(at, 2))
                act.activation(oT[:, at.bpair, 2 * at.q:2 * at.q + 2, :],
                               OB.rearrange("p (j t) -> p j t", t=P), ACT.Copy
                               ).then_inc(oT_done, 1)

            def take_y(ph, at):
                act.wait_ge(y_ps, ph.nb(at))
                act.wait_ge(y_done, ph.nb(at, 2))
                act.activation(yst[:, at.bpair, :], YB, ACT.Copy).then_inc(y_out, 1)

            def take_xT(ph, at, n):
                act.wait_ge(xT_ps, n)
                act.wait_ge(v_ps, ph.n(at, 5))
                ins = act.activation(xTf[:, at.bpair, :], XB, ACT.Copy)
                if ph.local:
                    act.activation(xTh[:, at.bpair, :], XB, ACT.Copy).then_inc(xT_hi, 1)
                else:
                    ins.then_inc(xT_hi, 1)
                    act.wait_ge(c_ps, n)
                    act.activation(ctxT[:, at.bpair, :, :],
                                   TB_[:, 0:CK * M].rearrange("p (c m) -> p c m", m=M), ACT.Copy
                                   ).then_inc(xT_done, 1)

            def body2(i, k, live):
                ph = phase2()
                if live(0) and k % QUARTERS == 1:
                    nxt = At(i, k + 3)
                    take_xT(ph, nxt, nxt.batch + 1)
                if live(ph.at_softmax):
                    exps(ph, At(i, k - ph.at_softmax))
                if live(ph.at_out):
                    take_pT(ph, At(i, k - ph.at_out))
                if live(0) and k % QUARTERS == 0:
                    nxt = At(i, k + 4)
                    take_x(ph, nxt, nxt.batch + 1)
                if live(0):
                    at = At(i, k)
                    act.wait_ge(qk_ps, ph.n(at))
                    act.wait_ge(kz_done, ph.n(at))
                    act.wait_ge(s_ps, ph.n(at, 2))
                    act.activation(qT[:, at.pair, :, :],
                                   QKB[at.pair][:, 0:2 * P].rearrange("p (j t) -> p j t", t=P), ACT.Copy,
                                   scale=DH ** -0.5).then_inc(qT_done, 1)
                if live(ph.at_wo) and At(i, k - ph.at_wo).q == 3:
                    take_y(ph, At(i, k - ph.at_wo))
                if live(0):
                    take_v(ph, At(i, k))
                if live(ph.at_out):
                    take_o(ph, At(i, k - ph.at_out))

            act.wait_ge(ln_out, LN_POST2)
            take_x(phase2(), At(0, 0), 1)
            take_xT(phase2(), At(0, 0), 1)
            quarter_steps(act, body2, phase2().at_wo)

            def split_wq(q, loads):
                act.wait_ge(ld_wq, loads)
                act.activation(wh[:, q, :] if isinstance(q, int) else wh[:, bass.ds(q, 1), :],
                               wst[:, q, :] if isinstance(q, int) else wst[:, bass.ds(q, 1), :], ACT.Copy
                               ).then_inc(wq_hi, 1)

            for q in range(QUARTERS):
                split_wq(q, 16 * 3)
            def keep(g, count):
                act.wait_ge(ln_out, count)
                act.activation(ybuf[:, bass.ds(g * G, G), :], x[:, bass.ds(g * G, G), :], ACT.Copy).then_inc(kept, 1)

            with act.Fori(0, GROUPS - 1) as g:
                keep(g, g * 2 + (LN_POST2 + 3))
            keep(GROUPS - 1, LN_POST2 + 2 * GROUPS)
            with act.Fori(0, LAYERS) as l:
                ph = phase3(l)

                def squares(at):
                    act.wait_ge(qk_ps, ph.n(at))
                    act.wait_ge(ssq_done, ph.n(at, 2))
                    act.activation(sq[:, at.pair, :], QKB[at.pair][:, :], ACT.Square).then_inc(sq_done, 1)

                def inverse_norm(at):
                    act.wait_ge(ssq_done, ph.n(at))
                    act.activation(lnr[:, at.pair, :], ssq[:, at.pair, :], ACT.Ln, scale=2.0 ** 16
                                   ).then_inc(ln_done, 1)
                    act.wait_ge(ln_done, ph.n(at))
                    act.wait_ge(qks_done, ph.n(at, 2))
                    act.activation(rn[:, at.pair, :], lnr[:, at.pair, :], ACT.Exp, scale=-0.5,
                                   bias=lnbias[:, 0:1]).then_inc(rn_done, 1)

                def take_T(at):
                    act.wait_ge(t_ps, ph.n(at))
                    act.wait_ge(s_ps, ph.n(at, 2))
                    act.activation(qT[:, at.pair, :, :], TB_[:, 0:2 * P].rearrange("p (j t) -> p j t", t=P),
                                   ACT.Copy).then_inc(qT_done, 1)
                    for h in range(2):
                        r = slice(h * DH, (h + 1) * DH)
                        ins = act.activation(kz[r, at.pair, :, h, :],
                                             TB_[r, 2 * P:4 * P].rearrange("p (j t) -> p j t", t=P), ACT.Copy)
                    ins.then_inc(kT_done, 1)

                def body(i, k, live):
                    if live(0) and k % QUARTERS == 1:
                        nxt = At(i, k + 3)
                        take_xT(ph, nxt, nxt.batch + (ph.xb + 1))
                    if live(0):
                        squares(At(i, k))
                    if live(ph.at_softmax):
                        exps(ph, At(i, k - ph.at_softmax))
                    if live(ph.at_out):
                        take_pT(ph, At(i, k - ph.at_out))
                    if live(0) and k % QUARTERS == 0:
                        nxt = At(i, k + 4)
                        take_x(ph, nxt, nxt.batch + (ph.xb + 1))
                    if live(0):
                        take_v(ph, At(i, k))
                    if live(ph.at_wo) and At(i, k - ph.at_wo).q == 3:
                        take_y(ph, At(i, k - ph.at_wo))
                    if live(1):
                        take_T(At(i, k - 1))
                    if live(0):
                        inverse_norm(At(i, k))
                    if live(ph.at_out):
                        take_o(ph, At(i, k - ph.at_out))

                def front(g):
                    act.wait_ge(ln_out, l * GROUPS + g + LN_FF)
                    act.activation(lnz[:, :, 0:64], x[:, bass.ds(g * G, G), 0:64], ACT.Copy).then_inc(f_z0, 1)

                def front_ahead(k):
                    if k == 0:
                        act.wait_ge(y_done, ph.nb(At(1, QUARTERS)))
                        front(0)

                act.preload_act_table_set("natural_log_exp_and_others")
                act.wait_ge(ln_out, 4 * GROUPS)
                act.wait_ge(f_x, l * GROUPS + 1)
                take_x(ph, At(0, 0), ph.xb + 1)
                take_xT(ph, At(0, 0), ph.xb + 1)
                act.wait_ge(ld_w1, l * 16 + 16)
                act.activation(w1h[:, :], w1st[:, :], ACT.Copy).then_inc(w1_hi, 1)
                act.wait_ge(f_x, l * GROUPS + GROUPS)
                quarter_steps(act, body, ph.at_wo, front_ahead)

                def take_T_ff(g):
                    act.wait_ge(f_T, l * GROUPS + g + 1)
                    act.activation(xfT[:, :, :], bank[1][:, :].rearrange("p (j t) -> p j t", t=P), ACT.Identity,
                                   bias=vec[:, 1:2], scale=vec[:, 0:1]).then_inc(f_xT, 1)

                def gelu(g, j):
                    cn = FBLK[j][1]
                    act.wait_ge(f_ab, (l * GROUPS + g) * FB + (j + 1))
                    act.activation(gel[0:cn, j % 2, :], bank[3 + 2 * (j % 2)][0:cn, :], ACT.Gelu,
                                   bias=b1g[0:cn, j:j + 1]).then_inc(f_gel, 1)

                act.wait_ge(tab_done, l + 1)
                act.wait_ge(y_done, l * B + (2 * B + CREDIT))
                take_T_ff(0)
                act.preload_act_table(ACT.Gelu)
                front(1)

                def ffn_pass(g, last):
                    gelu(g - 1, 0)
                    gelu(g - 1, 1)
                    take_T_ff(g)
                    gelu(g - 1, 2)
                    if not last:
                        front(g + 1)
                    split_wq(g - 1, (l * 3 + 6) * 16)

                with act.Fori(1, GROUPS - 1) as g:
                    ffn_pass(g, False)
                ffn_pass(GROUPS - 1, True)
                for j in range(FB):
                    gelu(GROUPS - 1, j)
                split_wq(GROUPS - 1, (l * 3 + 6) * 16)

        @block.tensor
        def _(pe):
            start_with_credit(pe, ["qk_ps", "s_ps", "pT_ps", "v_ps", "o_ps", "y_ps"], ["t_ps"])
            pe.wait_ge(pool_const, 10)
            pe.wait_ge(ld_first, 16 * N_LD_FIRST)
            pe.wait_ge(dve_const, 5)
            def norm_T(g, count):
                pe.wait_ge(ln_out, count)
                if not isinstance(g, int):
                    pe.wait_ge(g_xnT, g)
                for j in range(G):
                    mm = pe.transpose(bank[0][:, j * P:(j + 1) * P], lnx[:, j, :], ident[:, :])
                mm.then_inc(g_T, 1)

            def project1(g):
                pe.wait_ge(g_xnT, g + 1)
                if not isinstance(g, int):
                    pe.wait_ge(g_v1, g)
                for j in range(G):
                    mm = pe.matmul(bank[1 + j][:, 0:3 * D], xnT[:, j, :], wqkv1[:, :], start=True, stop=True)
                mm.then_inc(g_qkv, 1)

            def q_T_and_kv(g, first):
                pe.wait_ge(g_qk1, g + 1)
                if not first:
                    pe.wait_ge(g_z, g)
                for j in range(G):
                    mm = pe.transpose(bank[7][:, j * P:(j + 1) * P], qk1[:, j, 0:D], ident[:, :])
                mm.then_inc(g_q1T_ps, 1)
                pe.wait_ge(g_v1, g + 1)
                for j in range(G):
                    c = (j % 2) * 160
                    mm = pe.matmul(bank[5 + j // 2][:, c:c + D + 1], qk1[:, j, D:2 * D], v1[:, j, :],
                                   start=True, stop=True)
                mm.then_inc(g_kv, 1)

            def q_times_kv(g):
                pe.wait_ge(g_kvm, g + 1)
                pe.wait_ge(g_q1T, g + 1)
                for j in range(G):
                    c = (j % 2) * 160
                    mm = pe.matmul(bank[5 + j // 2][:, c:c + D + H], q1T[:, j, :], kvm[:, j, :],
                                   start=True, stop=True)
                mm.then_inc(g_o, 1)

            def out_T(g):
                pe.wait_ge(g_o1, g + 1)
                for j in range(G):
                    mm = pe.transpose(bank[7][:, j * P:(j + 1) * P], o1[:, j, :], ident[:, :])
                mm.then_inc(g_o1T_ps, 1)

            def project_out1(g):
                pe.wait_ge(g_o1T, g + 1)
                for j in range(G):
                    mm = pe.matmul(bank[7][:, j * P:(j + 1) * P], o1T[:, j, :], wout1[:, :], start=True, stop=True)
                mm.then_inc(g_y, 1)

            norm_T(0, 1)
            project1(0)
            q_T_and_kv(0, True)
            with pe.Fori(1, GROUPS) as g:
                q_times_kv(g - 1)
                norm_T(g, g * 2)
                out_T(g - 1)
                project1(g)
                project_out1(g - 1)
                q_T_and_kv(g, False)
            q_times_kv(GROUPS - 1)
            out_T(GROUPS - 1)
            project_out1(GROUPS - 1)

            def transpose_x(ph, at, n):
                pe.wait_ge(x_in, n)
                if not isinstance(n, int) or n > 1:
                    pe.wait_ge(xT_hi, n - 1)
                ps = XB
                for h, (r, moving) in enumerate(((slice(0, 64), ident), (slice(64, 128), shift if ph.local else ident))):
                    mm = pe.matmul(ps[r, :], xin[:, at.bpair, r], moving[:, :], start=True, stop=True)
                mm.then_inc(xT_ps, 1)

            def sims(ph, at):
                pe.wait_ge(qT_done, ph.n(at))
                pe.wait_ge(kT_done if ph.local else kz_done, ph.n(at))
                pe.wait_ge(sub_done, ph.n(at, 2))
                ps, w = SB_[at.pair], 2 * ph.keys
                keys = kz if ph.local else kz2
                if ph.local:
                    pe.matmul(ps[:, :], ident_bf[:, :], mask_bf[:, :, :].rearrange("p h j -> p (h j)"),
                              start=True, stop=False)
                for j in range(2):
                    mm = pe.matmul(ps[:, j * w:(j + 1) * w], qT[:, at.pair, j, :],
                                   keys[:, at.pair, j, :, :].rearrange("p h j -> p (h j)"),
                                   start=not ph.local, stop=not ph.local or j == 1)
                mm.then_inc(s_ps, 1)

            def transpose_p(ph, at):
                pe.wait_ge(pr_done, ph.n(at))
                pe.wait_ge(pT_done, ph.n(at, 1))
                for h in range(HQ):
                    mm = pe.transpose(PTB[0:ph.keys, h * P:(h + 1) * P], pr[:, at.pair, h, 0:ph.keys], ident[:, :])
                mm.then_inc(pT_ps, 1)

            def weighted_v(ph, at, values):
                pe.wait_ge(pT_done, ph.n(at))
                pe.wait_ge(v_done, values)
                for h in range(HQ):
                    r = slice((h % 2) * DH, (h % 2 + 1) * DH)
                    mm = pe.matmul(OB[r, (h // 2) * P:(h // 2 + 1) * P], vs[0:ph.keys, at.slot, h * DH:(h + 1) * DH],
                                   pT[0:ph.keys, at.pair, h, :], start=True, stop=True)
                mm.then_inc(o_ps, 1)

            def project_o(ph, i, k, live):
                at = At(i, k - ph.at_wo)
                if at.q == 0 and live(0):
                    pe.wait_ge(xT_hi, At(i, k + 3).batch + (ph.xb + 1))
                pe.wait_ge(oT_done, ph.n(at))
                w = wo if ph.local else wout2
                per = INNER // P // QUARTERS
                for j in range(at.q * per, (at.q + 1) * per):
                    mm = pe.matmul(YB, oT[:, at.bpair, j, :], w[:, j, :],
                                   start=(j == 0), stop=(j == INNER // P - 1))
                if at.q == QUARTERS - 1:
                    mm.then_inc(y_ps, 1)

            def before_values(ph, i, k, live):
                if live(ph.at_out + 1):
                    pe.wait_ge(oT_done, ph.n(At(i, k - ph.at_out), 1))

            def before_x(ph, i, k, live):
                if live(ph.at_wo + 1):
                    pe.wait_ge(y_out, ph.nb(At(i, k - ph.at_wo - 1)))

            def context_T(at, n):
                pe.wait_ge(ld_ctx[at.bpair], at.two * 16 + 16)
                if not isinstance(n, int) or n > 1:
                    pe.wait_ge(xT_done, n - 1)
                for c in range(CK):
                    mm = pe.transpose(TB_[:, c * M:(c + 1) * M], cst[:, at.bpair, c * P:(c + 1) * P], ident[0:M, 0:M])
                mm.then_inc(c_ps, 1)

            def project2(ph, at):
                pe.wait_ge(qT_done, ph.n(at, 2))
                pe.wait_ge(kz_done, ph.n(at, 2))
                ps = QKB[at.pair]
                for j in range(2):
                    c = (2 * at.q + j) * P
                    pe.matmul(ps[:, j * P:(j + 1) * P], wq2[:, c:c + P], xTf[:, at.bpair, :], start=True, stop=True)
                for j in range(2):
                    c = (2 * at.q + j) * P
                    for ck in range(CK):
                        mm = pe.matmul(ps[:, 256 + j * M:256 + (j + 1) * M], wkv2[:, ck, c:c + P],
                                       ctxT[:, at.bpair, ck, :], start=(ck == 0), stop=(ck == CK - 1))
                mm.then_inc(qk_ps, 1)

            def values2(ph, at):
                pe.wait_ge(v_done, ph.n(at, 1))
                for ck in range(CK):
                    mm = pe.matmul(VB[0:M, :], ctxT[:, at.bpair, ck, :],
                                   wkv2[:, ck, INNER + at.q * QW:INNER + (at.q + 1) * QW],
                                   start=(ck == 0), stop=(ck == CK - 1))
                mm.then_inc(v_ps, 1)

            def body2(i, k, live):
                ph = phase2()
                if live(0) and k % QUARTERS == 1:
                    nxt = At(i, k + 3)
                    before_x(ph, i, k, live)
                    transpose_x(ph, nxt, nxt.batch + 1)
                    context_T(nxt, nxt.batch + 1)
                if live(ph.at_out):
                    transpose_p(ph, At(i, k - ph.at_out))
                if live(0):
                    at = At(i, k)
                    if at.q == 0:
                        pe.wait_ge(xT_done, at.batch + 1)
                    project2(ph, at)
                if live(0):
                    before_values(ph, i, k, live)
                    values2(ph, At(i, k))
                if live(ph.at_wo):
                    project_o(ph, i, k, live)
                if live(ph.at_sims):
                    sims(ph, At(i, k - ph.at_sims))
                if live(ph.at_out):
                    at = At(i, k - ph.at_out)
                    weighted_v(ph, at, ph.n(At(i, k) if live(0) else at))

            pe.wait_ge(g_z, GROUPS)
            pe.wait_ge(ld_c, 16 * N_LD_C)
            pe.wait_ge(dve_const, 7)
            transpose_x(phase2(), At(0, 0), 1)
            context_T(At(0, 0), 1)
            quarter_steps(pe, body2, phase2().at_wo)

            with pe.Fori(0, LAYERS) as l:
                ph = phase3(l)

                def three(ps, xh, xl, whi, wlo, last=True):
                    pe.matmul(ps, xh, whi, start=True, stop=False)
                    pe.matmul(ps, xh, wlo, start=False, stop=False)
                    return pe.matmul(ps, xl, whi, start=False, stop=True)

                def project_qk(at):
                    pe.wait_ge(sq_done, ph.n(at, 2))
                    pe.wait_ge(rot_done, ph.n(at, 2))
                    three(QKB[at.pair][:, :], xTh[:, at.bpair, :], xTl[:, at.bpair, :],
                          wh[:, at.q, 0:2 * QW], wl[:, at.q, 0:2 * QW]).then_inc(qk_ps, 1)

                def project_v(at):
                    pe.wait_ge(v_done, ph.n(at, 1))
                    three(VB, xTh[:, at.bpair, :], xTl[:, at.bpair, :],
                          wh[:, at.q, 2 * QW:3 * QW], wl[:, at.q, 2 * QW:3 * QW]).then_inc(v_ps, 1)

                def transpose_qk(at):
                    pe.wait_ge(qks_done, ph.n(at))
                    pe.wait_ge(qT_done, ph.n(at, 1))
                    pe.wait_ge(kT_done, ph.n(at, 1))
                    for j in range(4):
                        mm = pe.transpose(TB_[:, j * P:(j + 1) * P], qks[:, at.pair, j * P:(j + 1) * P], ident[:, :])
                    mm.then_inc(t_ps, 1)

                def body(i, k, live):
                    if live(0) and k % QUARTERS == 1:
                        nxt = At(i, k + 3)
                        before_x(ph, i, k, live)
                        transpose_x(ph, nxt, nxt.batch + (ph.xb + 1))
                    if live(0):
                        at = At(i, k)
                        if at.q == 0:
                            pe.wait_ge(xT_done, at.batch + (ph.xb + 1))
                        project_qk(at)
                    if live(ph.at_sims):
                        sims(ph, At(i, k - ph.at_sims))
                    if live(ph.at_out):
                        transpose_p(ph, At(i, k - ph.at_out))
                    if live(0):
                        before_values(ph, i, k, live)
                        project_v(At(i, k))
                    if live(ph.at_wo):
                        project_o(ph, i, k, live)
                    if live(1):
                        transpose_qk(At(i, k - 1))
                    if live(ph.at_out):
                        at = At(i, k - ph.at_out)
                        weighted_v(ph, at, ph.n(At(i, k) if live(0) else at))

                def shifted(g):
                    pe.wait_ge(f_z, l * GROUPS + g + 1)
                    pe.matmul(bank[0][:, 0:G * 64].rearrange("p (j d) -> p j d", d=64), shift[:, :],
                              x[:, bass.ds(g * G, G), 64:128], start=True, stop=True).then_inc(f_shift, 1)

                def shifted_ahead(k):
                    if k == 0:
                        pe.wait_ge(y_done, ph.nb(At(1, QUARTERS)))
                        pe.wait_ge(rot_done, ph.n(At(OUTER, 0), 1))
                        shifted(0)

                def front_T(g):
                    pe.wait_ge(ln_out, l * GROUPS + g + (LN_FF + 1))
                    pe.wait_ge(f_xT, l * GROUPS + g + 1)
                    for j in range(G):
                        mm = pe.transpose(bank[1][:, j * P:(j + 1) * P], lnx[:, j, :], ident[:, :])
                    mm.then_inc(f_T, 1)

                def hidden(g, j):
                    if j == 0:
                        pe.wait_ge(f_split, l * GROUPS + g + 1)
                    if j == 2:
                        pe.wait_ge(f_h, (l * GROUPS + g) * FB + 1)
                    c0, cn = FBLK[j]
                    for a in range(2):
                        c = a * FF + c0
                        mm = three(bank[2 + 2 * (j % 2) + a][0:cn, :], w1h[:, c:c + cn], w1l[:, c:c + cn],
                                   xfTh[:, :, :].rearrange("p j t -> p (j t)"),
                                   xfTl[:, :, :].rearrange("p j t -> p (j t)"))
                    mm.then_inc(f_ab, 1)

                def down(g):
                    pe.wait_ge(f_h, (l * GROUPS + g) * FB + FB)
                    for b in range(G):
                        for j, (c0, cn) in enumerate(FBLK):
                            mm = pe.matmul(bank[6][:, b * P:(b + 1) * P], hT[0:cn, j, b * P:(b + 1) * P],
                                           w2[0:cn, j, :], start=(j == 0), stop=(j == FB - 1))
                    mm.then_inc(f_y, 1)

                transpose_x(ph, At(0, 0), ph.xb + 1)
                pe.wait_ge(f_x, l * GROUPS + GROUPS)
                pe.wait_ge(wq_split, l * QUARTERS + QUARTERS)
                pe.wait_ge(ld_wo, l * 16 + 16)
                quarter_steps(pe, body, ph.at_wo, shifted_ahead)

                pe.wait_ge(w1_split, l + 1)
                pe.wait_ge(ld_w2, l * 32 + 32)
                pe.wait_ge(y_done, l * B + (2 * B + CREDIT))
                front_T(0)
                shifted(1)

                def ffn_pass(g, last):
                    hidden(g - 1, 0)
                    hidden(g - 1, 1)
                    front_T(g)
                    hidden(g - 1, 2)
                    if not last:
                        shifted(g + 1)
                    pe.wait_ge(f_x, l * GROUPS + g + (GROUPS - 1))
                    down(g - 1)

                with pe.Fori(1, GROUPS - 1) as g:
                    ffn_pass(g, False)
                ffn_pass(GROUPS - 1, True)
                for j in range(FB):
                    hidden(GROUPS - 1, j)
                pe.wait_ge(f_x, l * GROUPS + (2 * GROUPS - 1))
                down(GROUPS - 1)


N_LD_FIRST = 6
N_LD_C = 7 + 1
N_LD_TAB = 4
NVEC = 2 + 2 * FB
LN_POST2 = 2 * GROUPS
LN_FF = 4 * GROUPS
LN_FINAL = LN_FF + LAYERS * GROUPS

INPUTS = ["x", "ctx_2048", "L0_attn_gamma", "L0_attn_beta", "L0_attn_Wqkv", "L0_attn_Wout", "L0_xattn_Wq",
          "L0_xattn_Wkv", "L0_xattn_null_kv", "L0_xattn_Wout", "L0_xattn_ln_scale", "L0_xattn_ln_bias",
          "L0_ffn_Wqkv", "L0_ffn_Wo", "L0_ffn_W1", "L0_ffn_W2", "L0_ffn_b2"]


def laid_out(inputs):
    scales = np.stack([inputs["L0_ffn_q_scale"], inputs["L0_ffn_k_scale"]], 1).reshape(LAYERS, 2 * DH)
    b1 = np.zeros((LAYERS, 2, FB * P), inputs["L0_ffn_b1"].dtype)
    b1[:, :, :FF] = np.asarray(inputs["L0_ffn_b1"]).reshape(LAYERS, 2, FF)
    rows = [np.asarray(inputs["L0_ffn_ln_g"])[:, None], np.asarray(inputs["L0_ffn_ln_b"])[:, None],
            b1.reshape(LAYERS, 2 * FB, P)]
    named = {"qk_scales": scales, "vectors": np.concatenate(rows, 1).transpose(2, 0, 1)}
    return {name: np.ascontiguousarray(a) for name, a in named.items()}


def shape_constants():
    f = np.float32
    rows = np.arange(P) // HD
    blockmask = (rows[:, None] == rows[None, :]).astype(f)
    headmask = (rows[:, None] == np.arange(H)[None, :]).astype(f)
    half = np.arange(0, DH, 2, dtype=f)
    inv_freq = (f(1.0) / f(10000.0) ** (half / f(DH))).astype(f)
    pos = np.arange(P, dtype=f)
    freqs = pos[:, None] * inv_freq[None, :]
    freqs = np.concatenate([freqs, freqs], -1)
    base = (half + f(0.4 * DH)) / f(1.4 * DH)
    scale = base[None, :] ** ((pos - P // 2) / (WINDOW // 2))[:, None]
    scale = np.concatenate([scale, scale], -1).astype(f)
    sign = np.where(np.arange(DH) < DH // 2, f(-1), f(1))[None, :]
    rot = np.empty((P, 2, 2, DH), f)
    qk_scale = f(8.0)
    rot[:, 0, 0] = np.cos(freqs) * scale * qk_scale
    rot[:, 0, 1] = np.cos(freqs) / scale
    rot[:, 1, 0] = sign * np.sin(freqs) * scale * qk_scale
    rot[:, 1, 1] = sign * np.sin(freqs) / scale
    return {"c_blockmask": blockmask, "c_headmask": headmask, "c_rot": rot}


def kernel(**inputs):
    import concourse.bacc as bacc
    from concourse.bass_utils import run_bass_kernel_spmd

    nc = bacc.Bacc("TRN2", target_bir_lowering=False, num_devices=1)
    arrays = {name: np.ascontiguousarray(inputs[name]) for name in INPUTS}
    arrays = arrays | laid_out(inputs) | shape_constants()
    feeds, t = {}, {}
    for name, a in arrays.items():
        feeds[f"in_{name}"] = a
        t[name] = nc.dram_tensor(f"in_{name}", a.shape, mybir.dt.from_np(a.dtype), kind="ExternalInput").ap()
    out = nc.dram_tensor("out_y", (B, P, D), F32, kind="ExternalOutput").ap()
    build(nc, t, out)
    r = run_bass_kernel_spmd(nc, [feeds], core_ids=[0])
    return r.results[0]["out_y"]
```
